# Optimizing a Trainium2 kernel written in Bass

```python
import numpy as np
import jax
import jax.numpy as jnp

def _softmax(x, axis=-1):
    return jax.nn.softmax(x, axis=axis)

def _gelu(x):
    return jax.nn.gelu(x, approximate=True)

def _silu(x):
    return jax.nn.silu(x)

def _sigmoid(x):
    return jax.nn.sigmoid(x)

def _layernorm(x, axis=-1, eps=1e-05):
    m = jnp.mean(x, axis=axis, keepdims=True)
    v = jnp.var(x, axis=axis, keepdims=True)
    return (x - m) / jnp.sqrt(v + eps)

def _scatter_add(tgt, idx, src, axis=0):
    return tgt.at[idx].add(src)

def _segment_sum(src, seg, n):
    return jax.ops.segment_sum(src, seg, n)
kernel_name = 'mk_xattn_ffn_d2_seqx_r8_ec6e37'

def setup_inputs(seed: int=0):
    np.random.seed(seed)
    _w = jnp.asarray

    def _rec_inputs():
        import jax
        import jax.numpy as jnp
        _rk = jax.random.key(seed)
        x = 0.0002417 + 0.9998 * jax.random.normal(jax.random.fold_in(_rk, 1), (4, 512, 128), jnp.float32)
        _lenS = 512 - jax.random.randint(jax.random.fold_in(_rk, 7), (4,), 0, max(1, 512 // 4) + 1, jnp.int32)
        _lenS2 = 154 - jax.random.randint(jax.random.fold_in(_rk, 8), (4,), 0, max(1, 154 // 4) + 1, jnp.int32)
        _ctx_1024P = jax.random.normal(jax.random.fold_in(_rk, 11), (4, 16, 128), jnp.float32)
        _ctx_1024c = jax.random.dirichlet(jax.random.fold_in(_rk, 511), 0.3 * jnp.ones((16,), jnp.float32), (4, 154))
        _ctx_1024t = jnp.einsum('bsk,bkd->bsd', _ctx_1024c, _ctx_1024P)
        _ctx_1024t = _ctx_1024t * jax.lax.rsqrt(jnp.mean(jnp.square(_ctx_1024t)) + 1e-12) * 0.953939
        ctx_1024 = 7.22013e-05 + 1.00017 * (_ctx_1024t + 0.3 * jax.random.normal(jax.random.fold_in(_rk, 611), (4, 154, 128), jnp.float32))
        _validS = jnp.arange(512)[None, :] < _lenS[:, None]
        _validS2 = jnp.arange(154)[None, :] < _lenS2[:, None]
        _causal = jnp.tril(jnp.ones((512, 512), dtype=bool))
        mask_BxS2_if0 = jnp.where(jnp.ones((4, 154), dtype=bool), 0, 1).astype(jnp.int32)
        return (x, ctx_1024, mask_BxS2_if0)
    x, ctx_1024, mask_BxS2_if0 = _rec_inputs()

    def _L0_xattn_setup():
        import jax, jax.numpy as jnp
        import numpy as np
        import math
        B, M, D, H, NK = (4, 256, 128, 16, 5)
        HD = D // H

        def _gather_pad0(x, idx):
            Bx, Hx, W, hd = x.shape
            valid = (idx >= 0) & (idx < W)
            idxc = jnp.clip(idx, 0, W - 1).reshape(Bx, Hx, -1)
            g = jnp.take_along_axis(x, idxc[..., None], axis=2)
            g = g.reshape(idx.shape + (hd,))
            return g * valid[..., None].astype(x.dtype)
        key = jax.random.key(seed)
        ks = jax.random.split(key, 9)
        w = lambda k, shape: jax.random.normal(k, shape, jnp.float32) * 0.02
        return {'k': jax.random.normal(ks[0], (B, M, D), jnp.float32), 'v': jax.random.normal(ks[1], (B, M, D), jnp.float32), 'q': jax.random.normal(ks[2], (B, M, D), jnp.float32), 'mask': jnp.zeros((B, M), jnp.int32), 'Wk': w(ks[3], (D, D)), 'bk': jnp.zeros((D,), jnp.float32), 'Wv': w(ks[4], (D, D)), 'bv': jnp.zeros((D,), jnp.float32), 'Wq': w(ks[5], (D, D)), 'bq': jnp.zeros((D,), jnp.float32), 'Woff': w(ks[6], (H * NK, D)), 'boff': jnp.zeros((H * NK,), jnp.float32), 'Wo': w(ks[7], (D, D)), 'bo': jnp.zeros((D,), jnp.float32)}
    _L0_xattn_all = _L0_xattn_setup()
    _L0_xattn_in = {k: v for k, v in _L0_xattn_all.items() if k in ('Wk', 'bk', 'Wv', 'bv', 'Wq', 'bq', 'Woff', 'boff', 'Wo', 'bo')}
    del _L0_xattn_all

    def _L0_ffn_setup():
        import jax, jax.numpy as jnp
        import numpy as np
        E = 32
        K = 4
        H = 128
        I = 96
        ROUTED_SCALING_FACTOR = 1.0
        key = jax.random.key(seed)
        k0, k1, k2, k3, k4, k5 = jax.random.split(key, 6)
        return {'hidden_states': jax.random.normal(k0, (1, 256, H), jnp.float32), 'gate_w': jax.random.normal(k1, (E, H), jnp.float32) * 0.02, 'w1': jax.random.normal(k2, (E, H, I), jnp.float32) * 0.02, 'w3': jax.random.normal(k3, (E, H, I), jnp.float32) * 0.02, 'w2': jax.random.normal(k4, (E, I, H), jnp.float32) * 0.02, 'e_bias': jax.random.normal(k5, (E,), jnp.float32) * 0.02}
    _L0_ffn_all = _L0_ffn_setup()
    _L0_ffn_in = {k: v for k, v in _L0_ffn_all.items() if k in ('gate_w', 'w1', 'w3', 'w2', 'e_bias')}
    del _L0_ffn_all

    def _L1_xattn_setup():
        import jax, jax.numpy as jnp
        import numpy as np
        DIM = 128
        NUM_HEADS = 16
        HEAD_DIM = DIM // NUM_HEADS
        LN_EPS = 1e-05
        key = jax.random.key(seed)
        ks = jax.random.split(key, 12)
        B, S = (2, 256)
        queries = jax.random.normal(ks[0], (B, S, DIM), dtype=jnp.float32)
        keys = jax.random.normal(ks[1], (B, S, DIM), dtype=jnp.float32)
        values = jax.random.normal(ks[2], (B, S, DIM), dtype=jnp.float32)
        scale = 1.0 / np.sqrt(DIM)
        Wq = jax.random.uniform(ks[3], (NUM_HEADS, DIM, HEAD_DIM), jnp.float32, -scale, scale)
        bq = jax.random.uniform(ks[4], (NUM_HEADS, HEAD_DIM), jnp.float32, -scale, scale)
        Wk = jax.random.uniform(ks[5], (NUM_HEADS, DIM, HEAD_DIM), jnp.float32, -scale, scale)
        bk = jax.random.uniform(ks[6], (NUM_HEADS, HEAD_DIM), jnp.float32, -scale, scale)
        Wv = jax.random.uniform(ks[7], (NUM_HEADS, DIM, HEAD_DIM), jnp.float32, -scale, scale)
        bv = jax.random.uniform(ks[8], (NUM_HEADS, HEAD_DIM), jnp.float32, -scale, scale)
        gamma = jnp.ones((DIM,), dtype=jnp.float32)
        beta = jnp.zeros((DIM,), dtype=jnp.float32)
        return {'queries': queries, 'keys': keys, 'values': values, 'Wq': Wq, 'bq': bq, 'Wk': Wk, 'bk': bk, 'Wv': Wv, 'bv': bv, 'gamma': gamma, 'beta': beta}
    _L1_xattn_all = _L1_xattn_setup()
    _L1_xattn_in = {k: v for k, v in _L1_xattn_all.items() if k in ('Wq', 'bq', 'Wk', 'bk', 'Wv', 'bv', 'gamma', 'beta')}
    del _L1_xattn_all

    def _L1_ffn_setup():
        import jax, jax.numpy as jnp
        import numpy as np
        EPS = 0.05
        N_ITERS = 20
        TOP_K = 2

        def _sinkhorn(cost, n_iters=N_ITERS, epsilon=EPS):
            la = cost / epsilon
            for _ in range(n_iters):
                la = la - jax.scipy.special.logsumexp(la, axis=-1, keepdims=True)
                la = la - jax.scipy.special.logsumexp(la, axis=-2, keepdims=True)
            return jnp.exp(la)
        key = jax.random.key(seed)
        k0, k1, k2, k3, k4 = jax.random.split(key, 5)
        B, T, D, F, E = (2, 256, 128, 512, 8)
        x = jax.random.normal(k0, (B, T, D), dtype=jnp.float32)
        gate_W = jax.random.normal(k1, (E, D), dtype=jnp.float32) * 0.02
        W_gate = jax.random.normal(k2, (E, F, D), dtype=jnp.float32) * 0.02
        W_up = jax.random.normal(k3, (E, F, D), dtype=jnp.float32) * 0.02
        W_down = jax.random.normal(k4, (E, D, F), dtype=jnp.float32) * 0.02
        return {'x': x, 'gate_W': gate_W, 'W_gate': W_gate, 'W_up': W_up, 'W_down': W_down}
    _L1_ffn_all = _L1_ffn_setup()
    _L1_ffn_in = {k: v for k, v in _L1_ffn_all.items() if k in ('gate_W', 'W_gate', 'W_up', 'W_down')}
    del _L1_ffn_all
    return {'x': x, 'ctx_1024': ctx_1024, 'mask_BxS2_if0': mask_BxS2_if0, 'L0_xattn_Wk': _L0_xattn_in['Wk'], 'L0_xattn_bk': _L0_xattn_in['bk'], 'L0_xattn_Wv': _L0_xattn_in['Wv'], 'L0_xattn_bv': _L0_xattn_in['bv'], 'L0_xattn_Wq': _L0_xattn_in['Wq'], 'L0_xattn_bq': _L0_xattn_in['bq'], 'L0_xattn_Woff': _L0_xattn_in['Woff'], 'L0_xattn_boff': _L0_xattn_in['boff'], 'L0_xattn_Wo': _L0_xattn_in['Wo'], 'L0_xattn_bo': _L0_xattn_in['bo'], 'L0_ffn_gate_w': _L0_ffn_in['gate_w'], 'L0_ffn_w1': _L0_ffn_in['w1'], 'L0_ffn_w3': _L0_ffn_in['w3'], 'L0_ffn_w2': _L0_ffn_in['w2'], 'L0_ffn_e_bias': _L0_ffn_in['e_bias'], 'L1_xattn_Wq': _L1_xattn_in['Wq'], 'L1_xattn_bq': _L1_xattn_in['bq'], 'L1_xattn_Wk': _L1_xattn_in['Wk'], 'L1_xattn_bk': _L1_xattn_in['bk'], 'L1_xattn_Wv': _L1_xattn_in['Wv'], 'L1_xattn_bv': _L1_xattn_in['bv'], 'L1_xattn_gamma': _L1_xattn_in['gamma'], 'L1_xattn_beta': _L1_xattn_in['beta'], 'L1_ffn_gate_W': _L1_ffn_in['gate_W'], 'L1_ffn_W_gate': _L1_ffn_in['W_gate'], 'L1_ffn_W_up': _L1_ffn_in['W_up'], 'L1_ffn_W_down': _L1_ffn_in['W_down']}

def reference(x, ctx_1024, mask_BxS2_if0, L0_xattn_Wk, L0_xattn_bk, L0_xattn_Wv, L0_xattn_bv, L0_xattn_Wq, L0_xattn_bq, L0_xattn_Woff, L0_xattn_boff, L0_xattn_Wo, L0_xattn_bo, L0_ffn_gate_w, L0_ffn_w1, L0_ffn_w3, L0_ffn_w2, L0_ffn_e_bias, L1_xattn_Wq, L1_xattn_bq, L1_xattn_Wk, L1_xattn_bk, L1_xattn_Wv, L1_xattn_bv, L1_xattn_gamma, L1_xattn_beta, L1_ffn_gate_W, L1_ffn_W_gate, L1_ffn_W_up, L1_ffn_W_down):
    import jax
    import jax.numpy as jnp

    def _L0_xattn_ref(k, v, q, mask, Wk, bk, Wv, bv, Wq, bq, Woff, boff, Wo, bo):
        import jax, jax.numpy as jnp
        import numpy as np
        import math
        B, M, D, H, NK = (4, 256, 128, 16, 5)
        HD = D // H

        def _gather_pad0(x, idx):
            Bx, Hx, W, hd = x.shape
            valid = (idx >= 0) & (idx < W)
            idxc = jnp.clip(idx, 0, W - 1).reshape(Bx, Hx, -1)
            g = jnp.take_along_axis(x, idxc[..., None], axis=2)
            g = g.reshape(idx.shape + (hd,))
            return g * valid[..., None].astype(x.dtype)
        Bq, Q, _ = q.shape
        key_len = k.shape[1]
        K = jnp.einsum('bmd,ed->bme', k, Wk) + bk
        V = jnp.einsum('bmd,ed->bme', v, Wv) + bv
        Qp = jnp.einsum('bqd,ed->bqe', q, Wq) + bq
        off = jnp.einsum('bqd,ed->bqe', Qp, Woff) + boff
        off = off.reshape(Bq, Q, H, NK).transpose(0, 2, 1, 3)
        Kh = K.reshape(Bq, key_len, H, HD).transpose(0, 2, 1, 3)
        Vh = V.reshape(Bq, key_len, H, HD).transpose(0, 2, 1, 3)
        Qh = Qp.reshape(Bq, Q, H, HD).transpose(0, 2, 1, 3)
        loc = jnp.arange(Q, dtype=jnp.float32)[:, None]
        left = -NK // 2
        ref = jnp.arange(left, NK + left, dtype=jnp.float32)
        sign_lens = (1 - mask).sum(-1).astype(jnp.float32) - 1.0
        loc_x = jnp.mod(ref + off + loc, sign_lens[:, None, None, None])
        xg = loc_x / (key_len - 1) * 2.0 - 1.0
        ix = ((xg + 1.0) * key_len - 1.0) / 2.0
        x0 = jnp.floor(ix)
        dx = ix - x0
        i0 = x0.astype(jnp.int32)
        i1 = i0 + 1
        w0 = (1.0 - dx)[..., None]
        w1 = dx[..., None]
        sk = 0.5 * (w0 * _gather_pad0(Kh, i0) + w1 * _gather_pad0(Kh, i1))
        sv = 0.5 * (w0 * _gather_pad0(Vh, i0) + w1 * _gather_pad0(Vh, i1))
        scores = jnp.einsum('bhqd,bhqkd->bhqk', Qh / math.sqrt(HD), sk)
        attn = jax.nn.softmax(scores, axis=-1)
        ctx = jnp.einsum('bhqk,bhqkd->bhqd', attn, sv)
        ctx = ctx.transpose(0, 2, 1, 3).reshape(Bq, Q, H * HD)
        return jnp.einsum('bqd,ed->bqe', ctx, Wo) + bo

    def _L0_ffn_ref(hidden_states, gate_w, w1, w3, w2, e_bias):
        import jax, jax.numpy as jnp
        import numpy as np
        E = 32
        K = 4
        H = 128
        I = 96
        ROUTED_SCALING_FACTOR = 1.0
        orig_shape = hidden_states.shape
        x = hidden_states.reshape(-1, orig_shape[-1])
        T = x.shape[0]
        router_logits = x @ gate_w.T
        scores = jax.nn.sigmoid(router_logits.astype(jnp.float32))
        _, topk_ids = jax.lax.top_k(scores + e_bias[None, :], K)
        topk_w = jnp.take_along_axis(scores, topk_ids, axis=1)
        topk_w = topk_w / jnp.sum(topk_w, axis=1, keepdims=True)
        combine = jnp.zeros((T, E), jnp.float32).at[jnp.arange(T)[:, None], topk_ids].add(topk_w)
        g = jnp.einsum('th,ehi->tei', x, w1)
        u = jnp.einsum('th,ehi->tei', x, w3)
        a = jax.nn.silu(g) * u * combine[:, :, None].astype(x.dtype)
        out = jnp.einsum('tei,eih->th', a, w2)
        out = out * ROUTED_SCALING_FACTOR
        return out.reshape(orig_shape)

    def _L1_xattn_ref(queries, keys, values, Wq, bq, Wk, bk, Wv, bv, gamma, beta):
        import jax, jax.numpy as jnp
        import numpy as np
        DIM = 128
        NUM_HEADS = 16
        HEAD_DIM = DIM // NUM_HEADS
        LN_EPS = 1e-05
        q = jnp.einsum('bsd,hdk->bhsk', queries, Wq) + bq[None, :, None, :]
        k = jnp.einsum('bsd,hdk->bhsk', keys, Wk) + bk[None, :, None, :]
        v = jnp.einsum('bsd,hdk->bhsk', values, Wv) + bv[None, :, None, :]
        scores = jnp.einsum('bhsk,bhtk->bhst', q, k) / jnp.sqrt(jnp.float32(HEAD_DIM))
        probs = jax.nn.softmax(scores, axis=-1)
        attended = jnp.einsum('bhst,bhtk->bhsk', probs, v)
        B, H, S, K = attended.shape
        attended = attended.transpose(0, 2, 1, 3).reshape(B, S, H * K)
        mean = jnp.mean(attended, axis=-1, keepdims=True)
        var = jnp.mean(jnp.square(attended - mean), axis=-1, keepdims=True)
        normed = (attended - mean) * jax.lax.rsqrt(var + LN_EPS)
        return normed * gamma + beta

    def _L1_ffn_ref(x, gate_W, W_gate, W_up, W_down):
        import jax, jax.numpy as jnp
        import numpy as np
        EPS = 0.05
        N_ITERS = 20
        TOP_K = 2

        def _sinkhorn(cost, n_iters=N_ITERS, epsilon=EPS):
            la = cost / epsilon
            for _ in range(n_iters):
                la = la - jax.scipy.special.logsumexp(la, axis=-1, keepdims=True)
                la = la - jax.scipy.special.logsumexp(la, axis=-2, keepdims=True)
            return jnp.exp(la)
        B, T, D = x.shape
        xf = x.reshape(B * T, D)
        logits = xf @ gate_W.T
        pi = _sinkhorn(-logits)
        _, top_idx = jax.lax.top_k(pi, TOP_K)
        g = jnp.einsum('nd,efd->enf', xf, W_gate)
        u = jnp.einsum('nd,efd->enf', xf, W_up)
        y = jnp.einsum('enf,edf->end', jax.nn.silu(g) * u, W_down)
        n_ar = jnp.arange(xf.shape[0])
        out = jnp.zeros_like(xf)
        for k in range(TOP_K):
            out = out + y[top_idx[:, k], n_ar] * pi[:, k:k + 1]
        return out.reshape(B, T, D)
    x = x + _L0_xattn_ref(ctx_1024, ctx_1024, _layernorm(x, axis=-1), mask_BxS2_if0, L0_xattn_Wk, L0_xattn_bk, L0_xattn_Wv, L0_xattn_bv, L0_xattn_Wq, L0_xattn_bq, L0_xattn_Woff, L0_xattn_boff, L0_xattn_Wo, L0_xattn_bo)
    x = x + _L0_ffn_ref(_layernorm(x, axis=-1), L0_ffn_gate_w, L0_ffn_w1, L0_ffn_w3, L0_ffn_w2, L0_ffn_e_bias)
    x = x + _L1_xattn_ref(_layernorm(x, axis=-1), ctx_1024, ctx_1024, L1_xattn_Wq, L1_xattn_bq, L1_xattn_Wk, L1_xattn_bk, L1_xattn_Wv, L1_xattn_bv, L1_xattn_gamma, L1_xattn_beta)
    x = x + _L1_ffn_ref(_layernorm(x, axis=-1), L1_ffn_gate_W, L1_ffn_W_gate, L1_ffn_W_up, L1_ffn_W_down)
    return x

_drawn_inputs = setup_inputs


def setup_inputs(seed=0):
    import zlib

    import numpy as np

    out = dict(_drawn_inputs(seed))
    spreads = {'L0_xattn_bk': (0.0, 0.8),
     'L0_xattn_bv': (0.0, 0.8),
     'L0_xattn_bq': (0.0, 0.8),
     'L0_xattn_boff': (0.0, 0.8),
     'L0_xattn_bo': (0.0, 0.1),
     'L1_xattn_gamma': (1.0, 0.2),
     'L1_xattn_beta': (0.0, 0.1)}
    factors = {'L0_xattn_Wk': 8.0,
     'L0_xattn_Wv': 4.98,
     'L0_xattn_Wq': 8.0,
     'L0_xattn_Woff': 8.0,
     'L0_xattn_Wo': 3.868,
     'L0_ffn_gate_w': 8.0,
     'L0_ffn_w1': 8.0,
     'L0_ffn_w3': 8.0,
     'L0_ffn_w2': 8.0,
     'L0_ffn_e_bias': 8.0,
     'L1_xattn_bq': 6.292,
     'L1_xattn_bk': 64.0,
     'L1_ffn_gate_W': 64.0,
     'L1_ffn_W_gate': 64.0,
     'L1_ffn_W_up': 64.0,
     'L1_ffn_W_down': 64.0}
    for name, (base, spread) in spreads.items():
        noise = np.random.default_rng([zlib.crc32(name.encode()), seed]).standard_normal(out[name].shape)
        drawn = base * np.exp(spread * noise) if base else spread * noise
        out[name] = jnp.asarray(drawn.astype(out[name].dtype))
    for name, factor in factors.items():
        out[name] = (out[name] * factor).astype(out[name].dtype)
    return out
```

```python
import math
from contextlib import ExitStack

import concourse.bass as bass
from concourse import mybir

F32 = mybir.dt.float32
F32R = mybir.dt.float32r
BF16 = mybir.dt.bfloat16
I32 = mybir.dt.int32
U32 = mybir.dt.uint32
ALU = mybir.AluOpType
ACT = mybir.ActivationFunctionType
AX_X = mybir.AxisListType.X

P = 128
B, S, D = 4, 512, 128
M = 154
H, HD = 16, 8
NK = 5
QT = S // P
GH = 4
NG = H // GH
HK = H * NK
CW = 162
E0, I0, K0 = 32, 96, 4
E1, F1D = 8, 512
C0 = E0 * I0 // P
C1 = E1 * F1D // P
SINK = 20
EPS = 1e-5
EXP_FLOOR = -87.33654
NT = B * QT


class Steps:

    def __init__(self, eng, sem):
        self.eng, self.sem, self.n = eng, sem, 0

    def tick(self, ins):
        self.n += 1
        return ins.then_inc(self.sem, 1)

    def settle(self):
        if self.n:
            self.eng.wait_ge(self.sem, self.n)

    def link(self, ins):
        self.tick(ins)
        self.settle()


def seq_kernel(nc, a, out):
    ctx = ExitStack()
    with ctx:
        def sb(name, shape, dt=F32, where=ctx):
            return where.enter_context(nc.sbuf_tensor(name, shape, dt))

        def sem(name):
            return ctx.enter_context(nc.semaphore(name))

        PS = ctx.enter_context(nc.psum_tensor("PS", [P, 8, 512], F32))

        ident = sb("ident", [P, P])
        identb = sb("identb", [P, P], BF16)
        ident3 = sb("ident3", [3 * 32, 32])
        ident3b = sb("ident3b", [3 * 32, 32], BF16)
        pcol = sb("pcol", [P, 8])
        locrow = sb("locrow", [HK, S])
        erow = sb("erow", [P, 32])
        lower = sb("lower", [P, E1 * E1])
        onerow = sb("onerow", [1, P])
        vrow = sb("vrow", [1, CW])
        vtail = sb("vtail", [1, 2, P])
        wkv = sb("wkv", [D, 2 * D])
        wq0 = sb("wq0", [D, D])
        woff = sb("woff", [D, HK])
        wo = sb("wo", [D, D])
        bkv = sb("bkv", [1, 2 * D])
        bq0 = sb("bq0", [1, D])
        bo = sb("bo", [1, D])
        bcol = sb("bcol", [P, 2])
        wq1 = sb("wq1", [D, NG * P])
        wk1 = sb("wk1", [D, NG * P])
        wv1 = sb("wv1", [D, NG * P])
        bqk1 = sb("bqk1", [P, 2, NG])
        bv1 = sb("bv1", [1, NG * P])
        gamma = sb("gamma", [P, D])
        beta = sb("beta", [P, D])
        gw0 = sb("gw0", [D, E0])
        eb0 = sb("eb0", [P, E0])
        gw1 = sb("gw1", [D, E1])

        XR = sb("XR", [P, NT, D])
        XT3 = sb("XT3", [D, B * S])
        CST = sb("CST", [P, NT, E1])

        X = sb("X", [P, QT, D])
        xn = sb("xn", [P, QT, D])
        xnT = sb("xnT", [D, S])
        xhi = sb("xhi", [D, S], F32R)
        xlo = sb("xlo", [D, S], F32R)
        cbT = sb("cbT", [3 * 32, S], BF16)
        sg = sb("sg", [P, 2, S])
        h1 = sb("h1", [P, 2, S])
        hh = sb("hh", [P, 2, S])
        yT = sb("yT", [D, S])
        st = sb("st", [P, QT, 6])
        mv = sb("mv", [P, QT, 2])
        var = sb("var", [P, QT])
        std = sb("std", [P, QT])
        rstd = sb("rstd", [P, QT])

        loop_ctx = ExitStack()
        lsb = lambda name, shape, dt=F32: sb(name, shape, dt, loop_ctx)
        wg0h = lsb("wg0h", [D, C0 * P], F32R)
        wu0h = lsb("wu0h", [D, C0 * P], F32R)
        with ExitStack() as raw_ctx:
            wg0r = sb("wg0r", [D, C0 * P], F32, raw_ctx)
            wu0r = sb("wu0r", [D, C0 * P], F32, raw_ctx)
        wg0l = lsb("wg0l", [D, C0 * P], F32R)
        wu0l = lsb("wu0l", [D, C0 * P], F32R)
        wd0 = lsb("wd0", [P, C0, D])
        cpad = lsb("cpad", [D, CW])
        ctail = lsb("ctail", [D, 2, P])
        mski = lsb("mski", [HK, M], I32)
        mskf = lsb("mskf", [HK, M])
        len3 = lsb("len3", [HK, 3])
        T1 = lsb("T1", [P, 3, 2, H * 32], BF16)
        T2 = lsb("T2", [P, 3, NG, P], BF16)
        Kbd = lsb("Kbd", [P, NG, GH, 160], F32R)
        Kb2 = lsb("Kb2", [P, NG, P], F32R)
        V2d = lsb("V2d", [P, NG, P])
        NMp = lsb("NMp", [P, 2, QT, P])
        V1 = lsb("V1", [P, NG * P])

        a_ctx = ExitStack()
        asb = lambda name, shape, dt=F32: sb(name, shape, dt, a_ctx)
        tabf = asb("tabf", [P, 2, H * 32])
        tabr = asb("tabr", [P, 2, H * 32])
        qT = asb("qT", [D, S])
        qhg = asb("qhg", [P, NG, QT, GH * HD])
        v0 = asb("v0", [HK, S])
        v1 = asb("v1", [HK, S])
        vi = asb("vi", [HK, S], I32)
        dxf = asb("dxf", [HK, S])
        ibf = asb("ibf", [HK, S], BF16)
        dxg = asb("dxg", [P, NG, NK, QT * GH])
        cbc = asb("cbc", [P, GH, S], BF16)
        oh1 = asb("oh1", [P, 2, GH, S], BF16)
        oh2 = asb("oh2", [P, 2, S], BF16)
        gs = asb("gs", [P, 2, S])
        pk = asb("pk", [P, NK, 2, QT * GH, HD])
        vv = asb("vv", [P, NK, 2, QT * GH, HD])
        pkr = asb("pkr", [P, NK, 2, QT * GH])
        sc = asb("sc", [P, NK, QT * GH])
        ee = asb("ee", [P, NK, QT * GH])
        coef = asb("coef", [P, NK, 2, QT * GH])
        sm = asb("sm", [P, 3, QT * GH])
        ctok = asb("ctok", [P, QT, D])
        ctxT = yT
        a_ctx.close()

        c_ctx = ExitStack()
        csb = lambda name, shape, dt=F32: sb(name, shape, dt, c_ctx)
        rsc = csb("rsc", [P, QT, E0])
        rbi = csb("rbi", [P, QT, E0])
        rmx = csb("rmx", [P, QT, 8])
        rix = csb("rix", [P, QT, 8], U32)
        rif = csb("rif", [P, QT, 8])
        roh = csb("roh", [P, QT, K0, E0])
        rms = csb("rms", [P, QT, E0])
        rcm = csb("rcm", [P, QT, E0])
        rsum = csb("rsum", [P, QT, 2])
        cb3 = csb("cb3", [P, QT, 3, 32], BF16)
        ktmp = csb("ktmp", [P, NG, M])
        khi = csb("khi", [P, NG, M], F32R)
        qtmp = csb("qtmp", [P, NG, S])
        qhi = csb("qhi", [P, S], F32R)
        qf = csb("qf", [P, NG, S], F32R)
        nmx = csb("nmx", [P, QT, GH])
        nmh = csb("nmh", [P, QT, GH], F32R)
        Ex = csb("Ex", [P, GH, S])
        Ex2 = csb("Ex2", [P, S])
        ots = csb("ots", [P, S])
        rden = csb("rden", [P, QT, GH])
        att = csb("att", [P, QT, D])
        c_ctx.close()
        loop_ctx.close()

        f_ctx = ExitStack()
        fsb = lambda name, shape, dt=F32: sb(name, shape, dt, f_ctx)
        wg1h = fsb("wg1h", [D, C1 * P], F32R)
        wu1h = fsb("wu1h", [D, C1 * P], F32R)
        with ExitStack() as raw_ctx:
            wg1r = sb("wg1r", [D, C1 * P], F32, raw_ctx)
            wu1r = sb("wu1r", [D, C1 * P], F32, raw_ctx)
        wg1l = fsb("wg1l", [D, C1 * P], F32R)
        wu1l = fsb("wu1l", [D, C1 * P], F32R)
        wd1 = fsb("wd1", [P, C1, D])
        wTall = fsb("wTall", [3 * 32, B * S], BF16)
        w3 = fsb("w3", [P, NT, 3, 32], BF16)
        sR = fsb("sR", [P, NT, E1])
        sE = fsb("sE", [P, NT, E1])
        srow = fsb("srow", [P, 4, NT])
        scol = fsb("scol", [P, 4, E1])
        smx = fsb("smx", [E1, 1])
        sdg = fsb("sdg", [E1, E1])
        onesm = fsb("onesm", [P, P])
        rk1 = fsb("rk1", [P, NT, E1, E1])
        rk2 = fsb("rk2", [P, NT, E1, E1])
        rank = fsb("rank", [P, NT, E1])
        f_ctx.close()

        consts_in = sem("consts_in")
        experts0_in = sem("experts0_in")
        setup_act = sem("setup_act")
        setup_pool = sem("setup_pool")
        consts_made = sem("consts_made")
        experts0_split = sem("experts0_split")
        names = """x_in ctx_in tails tab_ps tab_f tab_ready ln_var ln_std xn_ready xnT_ps xnT_ready
            q_ps qT_ready qhg_ready off_ps off_ready dxT_ps dxg_ready
            bc_a bc_b bc_c ev_a ev_b oh_a oh_b oh_c g_ps g_ev pt_ps pt_used sc_in sc_exp coef_ready vp_ready ctok_ready
            ctxT_ps ctxT_ready y_ps xhi_ready xlo_ready lg_ps score_in cb3_ready cbT_ps cbT_ready
            gu_ps sg_ready h_used h_ready acc_ps yT_ready yt_ps x_sum
            q1_ps q1_ev k1_ps k1_ev v1_ps v1_ready kbd_ready qf_ready mx_ps mx_used nm_ready nm_ps qn_ready
            s_a s_b s_c e_a e_b e_c ot_ps ot_ev ott_ps att_step kept out_in
            act_step dve_step pool_step arrived""".split()
        s = {n: sem(n) for n in names}
        go = {e: sem("go_" + e) for e in ("pe", "act", "dve", "pool")}
        experts1_in = sem("experts1_in")
        experts1_split = sem("experts1_split")
        sk_act = sem("sk_act")
        sk_dve = sem("sk_dve")
        sk_colT = sem("sk_colT")
        sk_diag = sem("sk_diag")
        sk_colmax = sem("sk_colmax")
        sk_sum_in = sem("sk_sum_in")
        sk_colsum = sem("sk_colsum")
        sk_exp_in = sem("sk_exp_in")
        sk_exp = sem("sk_exp")
        sk_ln = sem("sk_ln")
        sk_ln_in = sem("sk_ln_in")
        w3_ready = sem("w3_ready")
        w3_ps = sem("w3_ps")
        w3_used = sem("w3_used")

        block = ctx.enter_context(nc.Block())
        INV_SQRT = 1.0 / math.sqrt(HD)

        def finish_turn(eng, name):
            eng.drain().then_inc(s["arrived"], 1)
            eng.wait_ge(go[name], 1)
            eng.sem_clear(go[name])

        @block.sync
        def _(sp):
            consts = [(ident[:], a["ident"]), (ident3[:], a["ident3"]), (pcol[:], a["pcol"]),
                      (locrow[:], a["locrow"]), (erow[:], a["erow"]), (lower[:], a["lower"]),
                      (onerow[:], a["onerow"]), (vrow[:], a["vrow"]),
                      (vtail[:], a["vtail"]), (wkv[:], a["wkv"]), (wq0[:], a["wq0"]),
                      (woff[:], a["woff"]), (wo[:], a["wo"]), (bkv[:], a["bkv"]), (bq0[:], a["bq0"]),
                      (bo[:], a["bo"]), (bcol[:], a["bcol"]), (wq1[:], a["wq1"]), (wk1[:], a["wk1"]),
                      (wv1[:], a["wv1"]), (bqk1[:], a["bqk1"]), (bv1[:], a["bv1"]), (gamma[:], a["gamma"]),
                      (beta[:], a["beta"]), (gw0[:], a["gw0"]), (eb0[:], a["eb0"]), (gw1[:], a["gw1"])]
            assert len(consts) == N_CONSTS
            for dst, src in consts:
                sp.dma_start(dst, src).then_inc(consts_in, 16)
            sp.dma_start(wg0r[:], a["wg0"]).then_inc(experts0_in, 16)
            sp.dma_start(wu0r[:], a["wu0"]).then_inc(experts0_in, 16)
            sp.dma_start(wd0[:], a["wd0"]).then_inc(experts0_in, 16)
            with sp.Fori(0, B) as b:
                sp.dma_start(cpad[:], a["ctxp"][bass.ds(b, 1)].rearrange("a p m -> (a p) m")).then_inc(s["ctx_in"], 16)
                sp.dma_start(mski[:], a["mask"][bass.ds(b, 1)].rearrange("a p m -> (a p) m")).then_inc(s["ctx_in"], 16)
                sp.dma_start(X[:], a["x"][bass.ds(b, 1)].rearrange("a (t p) d -> p (a t) d", p=P)).then_inc(s["x_in"], 16)
                sp.wait_ge(s["arrived"], 4)
                for n in names:
                    sp.sem_clear(s[n])
                for e in go:
                    sp.sem_inc(go[e], 1)
            sp.dma_start(wg1r[:], a["wg1"]).then_inc(experts1_in, 16)
            sp.dma_start(wu1r[:], a["wu1"]).then_inc(experts1_in, 16)
            sp.dma_start(wd1[:], a["wd1"]).then_inc(experts1_in, 16)
            with sp.Fori(0, B) as b:
                sp.wait_ge(s["x_sum"], 1)
                sp.dma_start(out[bass.ds(b, 1)].rearrange("a (t p) d -> p (a t) d", p=P), X[:]).then_inc(s["out_in"], 16)
                sp.wait_ge(s["out_in"], 16)
                sp.wait_ge(s["arrived"], 4)
                for n in names:
                    sp.sem_clear(s[n])
                for e in go:
                    sp.sem_inc(go[e], 1)

        @block.gpsimd
        def _(pool):
            zeros = [T2, V2d, NMp]
            for z in zeros:
                pool.memset(z[:], 0.0).then_inc(setup_pool, 1)
            pool.memset(Kbd[:].bitcast(F32), 0.0).then_inc(setup_pool, 1)
            pool.memset(Kb2[:].bitcast(F32), 0.0).then_inc(setup_pool, 1)
            pool.wait_ge(consts_in, 16 * N_CONSTS)
            pool.tensor_copy(identb[:], ident[:]).then_inc(consts_made, 1)
            pool.tensor_copy(ident3b[:], ident3[:]).then_inc(consts_made, 1)
            pool.wait_ge(setup_pool, 5)
            with pool.Fori(0, B) as b:
                c = Steps(pool, s["pool_step"])
                pool.wait_ge(s["ctx_in"], 32)
                for n in range(2):
                    src = cpad[:, P + n:P + n + 32].unsqueeze(1).to_broadcast([D, GH, 32])
                    pool.tensor_copy(ctail[:, n, :].rearrange("p (j r) -> p j r", j=GH), src).then_inc(s["tails"], 1)
                pool.wait_ge(s["tab_f"], 2)
                c.link(pool.tensor_copy(T1[:, 0], tabf[:]))
                c.link(pool.tensor_tensor(tabr[:], tabf[:], T1[:, 0], ALU.subtract))
                c.link(pool.tensor_copy(T1[:, 1], tabr[:]))
                pool.tensor_tensor(T1[:, 2], tabr[:], T1[:, 1], ALU.subtract).then_inc(s["tab_ready"], 1)
                pool.wait_ge(s["xnT_ready"], 4)
                pool.tensor_copy(XT3[:, bass.ds(b * S, S)], xnT[:]).then_inc(s["kept"], 1)
                pool.tensor_copy(XR[:, bass.ds(b * QT, QT), :], X[:]).then_inc(s["kept"], 1)
                pool.wait_ge(s["kept"], 2)
                finish_turn(pool, "pool")
            with pool.Fori(0, B) as b:
                finish_turn(pool, "pool")

        def act_ffn(act, chunks):
            for j in range(chunks):
                act.wait_ge(s["gu_ps"], j + 1)
                if j >= 2:
                    act.wait_ge(s["h_used"], j - 1)
                act.activation(sg[:, j % 2, :], PS[:, j % 2, :], ACT.Silu).then_inc(s["sg_ready"], 1)
            act.wait_ge(s["acc_ps"], 1)
            act.copy(yT[:], PS[:, 7, :]).then_inc(s["yT_ready"], 1)

        @block.scalar
        def _(act):
            act.wait_ge(experts0_in, 48)
            act.copy(wg0h[:], wg0r[:]).then_inc(setup_act, 1)
            act.copy(wu0h[:], wu0r[:]).then_inc(setup_act, 1)
            with act.Fori(0, B) as b:
                c = Steps(act, s["act_step"])

                def deviation(n):
                    act.wait_ge(s["ln_var"], n + 1)
                    act.activation(std[:], var[:], ACT.Sqrt).then_inc(s["ln_std"], 1)

                def turned(n):
                    act.wait_ge(s["xnT_ps"], n + 1)
                    act.copy(xnT[:], PS[:, 0, :]).then_inc(s["xnT_ready"], 1)

                deviation(0)
                turned(0)
                act.wait_ge(s["q_ps"], 1)
                act.activation(qT[:], PS[:, 1, :], ACT.Identity, bias=bcol[:, 0:1]).then_inc(s["qT_ready"], 1)
                for n in range(NG * NK + 1):
                    if n < NG * NK:
                        act.wait_ge(s["bc_a"], n + 1)
                        if n >= 1:
                            act.wait_ge(s["oh_a"], n)
                        act.copy(cbc[:, 0:2, :], PS[:, 0:2, :]).then_inc(s["ev_a"], 1)
                        act.wait_ge(s["bc_b"], n + 1)
                        if n >= 1:
                            act.wait_ge(s["oh_b"], n)
                        act.copy(cbc[:, 2:4, :], PS[:, 2:4, :]).then_inc(s["ev_b"], 1)
                    if n >= 1:
                        act.wait_ge(s["g_ps"], n)
                        if n >= 3:
                            act.wait_ge(s["pt_ps"], n - 2)
                        act.copy(gs[:, (n - 1) % 2, :], PS[:, 5 + (n - 1) % 2, :]).then_inc(s["g_ev"], 1)
                    if n > NK and n % NK == 2:
                        g = n // NK - 1
                        act.wait_ge(s["sc_in"], g + 1)
                        act.activation(ee[:], sc[:], ACT.Exp, scale=0.5 * INV_SQRT).then_inc(s["sc_exp"], 1)
                act.wait_ge(s["sc_in"], NG)
                act.activation(ee[:], sc[:], ACT.Exp, scale=0.5 * INV_SQRT).then_inc(s["sc_exp"], 1)
                act.wait_ge(s["ctxT_ps"], 1)
                act.mul(ctxT[:], PS[:, 0, :], 0.5).then_inc(s["ctxT_ready"], 1)

                deviation(1)
                turned(1)
                act.copy(xhi[:], PS[:, 0, :]).then_inc(s["xhi_ready"], 1)
                act.wait_ge(s["lg_ps"], 1)
                act.activation(rsc[:], PS[:, 1, 0:QT * E0].rearrange("p (t e) -> p t e", t=QT), ACT.Sigmoid)\
                   .then_inc(s["score_in"], 1)
                act.wait_ge(s["cbT_ps"], 1)
                act.copy(cbT[:], PS[0:96, 2, :].bitcast(BF16)[:, 0:S]).then_inc(s["cbT_ready"], 1)
                act_ffn(act, C0)

                deviation(2)
                turned(2)
                for g in range(NG):
                    act.wait_ge(s["q1_ps"], g + 1)
                    act.activation(qtmp[:, g, :], PS[:, g, :], ACT.Identity, bias=bqk1[:, 0, g:g + 1])\
                       .then_inc(s["q1_ev"], 1)
                for g in range(NG):
                    act.wait_ge(s["k1_ps"], g + 1)
                    act.activation(ktmp[:, g, :], PS[:, 4 + g, 0:M], ACT.Identity, bias=bqk1[:, 1, g:g + 1])\
                       .then_inc(s["k1_ev"], 1)
                for g in range(NG):
                    act.wait_ge(s["s_a"], g + 1)
                    if g >= 1:
                        act.wait_ge(s["ot_ps"], g)
                    act.activation(Ex[:, 0:2, :], PS[:, 0:2, :], ACT.Exp, scale=INV_SQRT).then_inc(s["e_a"], 1)
                    act.wait_ge(s["s_b"], g + 1)
                    act.activation(Ex[:, 2:4, :], PS[:, 2:4, :], ACT.Exp, scale=INV_SQRT).then_inc(s["e_b"], 1)
                    act.wait_ge(s["s_c"], g + 1)
                    act.activation(Ex2[:], PS[:, 4, :], ACT.Exp, scale=INV_SQRT).then_inc(s["e_c"], 1)
                deviation(3)
                deviation(4)
                turned(3)
                finish_turn(act, "act")

            act.preload_act_table_set("natural_log_exp_and_others")
            for it in range(SINK):
                for half in range(2):
                    n = 2 * it + half
                    act.wait_ge(sk_exp_in, n + 1)
                    act.activation(sE[:], sR[:], ACT.Exp).then_inc(sk_exp, 1)
                    act.wait_ge(sk_ln_in, n + 1)
                    if half == 0:
                        act.activation(srow[:, 2, :], srow[:, 1, :], ACT.Ln).then_inc(sk_ln, 1)
                    else:
                        act.activation(scol[:, 2, :], PS[:, 2, 0:E1], ACT.Ln).then_inc(sk_ln, 1)
            act.wait_ge(sk_exp_in, 2 * SINK + 1)
            act.activation(sE[:], sR[:], ACT.Exp).then_inc(sk_exp, 1)
            for b in range(B):
                act.wait_ge(w3_ps, b + 1)
                act.copy(wTall[:, b * S:(b + 1) * S], PS[0:96, 3 + b, :].bitcast(BF16)[:, 0:S]).then_inc(w3_used, 1)
            act.wait_ge(w3_used, B)
            with act.Fori(0, B) as b:
                act.copy(cbT[:], wTall[:, bass.ds(b * S, S)]).then_inc(s["cbT_ready"], 1)
                act_ffn(act, C1)
                finish_turn(act, "act")

        def dve_ffn(dve, chunks, per_expert):
            for j in range(chunks):
                dve.wait_ge(s["sg_ready"], j + 1)
                dve.tensor_tensor(h1[:, j % 2, :], sg[:, j % 2, :], PS[:, 2 + j % 2, :], ALU.mult).then_inc(s["h_used"], 1)
                dve.wait_ge(s["h_used"], j + 1)
                if j >= 2:
                    dve.wait_ge(s["y_ps"], y_base[0] + j - 1)
                cbank = 4 + (j // per_expert) % 2
                dve.tensor_tensor(hh[:, j % 2, :], h1[:, j % 2, :], PS[:, cbank, :], ALU.mult).then_inc(s["h_ready"], 1)

        y_base = [0]

        @block.vector
        def _(dve):
            dve.wait_ge(setup_act, 2)
            dve.tensor_tensor(wg0l[:], wg0r[:], wg0h[:].bitcast(F32), ALU.subtract).then_inc(experts0_split, 1)
            dve.tensor_tensor(wu0l[:], wu0r[:], wu0h[:].bitcast(F32), ALU.subtract).then_inc(experts0_split, 1)
            dve.wait_ge(consts_in, 16 * N_CONSTS)
            dve.wait_ge(setup_pool, 5)
            with dve.Fori(0, B) as b:
                c = Steps(dve, s["dve_step"])

                def layernorm(src, dst, n, signal):
                    for t in range(QT):
                        last = dve.bn_stats(st[:, t, :], src[:, t, :])
                    c.link(last)
                    for t in range(QT):
                        last = dve.bn_aggr(mv[:, t, :], st[:, t, :])
                    c.link(last)
                    dve.tensor_scalar(var[:], mv[:, :, 1], EPS, None, ALU.add).then_inc(s["ln_var"], 1)
                    dve.wait_ge(s["ln_std"], n + 1)
                    c.link(dve.reciprocal(rstd[:], std[:]))
                    for t in range(QT):
                        last = dve.tensor_scalar(dst[:, t, :], src[:, t, :], mv[:, t, 0:1], rstd[:, t:t + 1],
                                                 ALU.subtract, ALU.mult)
                    if signal is None:
                        c.link(last)
                    else:
                        last.then_inc(s[signal], 1)

                dve.wait_ge(s["x_in"], 16)
                layernorm(X, xn, 0, "xn_ready")

                dve.wait_ge(s["tab_ps"], 1)
                for ch in range(2):
                    t4 = tabf[:, ch, :].rearrange("p (h v s c) -> p v h s c", h=H, v=2, s=2)
                    ps = PS[:, 4 + ch, :].rearrange("p (n v h c) -> p n v h c", n=2, v=2, h=H)
                    c.link(dve.tensor_copy(t4[:, :, :, 0, :], ps[:, 0]))
                    dve.tensor_tensor(t4[:, :, :, 1, :], ps[:, 1], t4[:, :, :, 0, :], ALU.subtract).then_inc(s["tab_f"], 1)

                dve.wait_ge(s["ctx_in"], 32)
                c.link(dve.tensor_copy(mskf[:], mski[:]))
                c.link(dve.reduce_sum(len3[:, 0:1], mskf[:], AX_X))
                c.link(dve.tensor_scalar(len3[:, 1:2], len3[:, 0:1], -1.0, float(M - 1), ALU.mult, ALU.add))
                c.link(dve.reciprocal(len3[:, 2:3], len3[:, 1:2]))
                length, rlength = len3[:, 1:2], len3[:, 2:3]

                dve.wait_ge(s["q_ps"], 2)
                dve.tensor_copy(qhg[:].rearrange("p g t e -> p t g e"),
                                PS[:, 2, :].rearrange("p (t g e) -> p t g e", t=QT, g=NG)).then_inc(s["qhg_ready"], 1)

                dve.wait_ge(s["off_ps"], 1)
                c.link(dve.tensor_scalar(v0[:], PS[0:HK, 3, :], bcol[0:HK, 1:2], pcol[0:HK, 2:3], ALU.add, ALU.add))
                c.link(dve.tensor_tensor(v0[:], v0[:], locrow[:], ALU.add))
                c.link(dve.tensor_scalar(vi[:], v0[:], rlength, None, ALU.mult))
                c.link(dve.tensor_copy(v1[:], vi[:]))
                c.link(dve.tensor_scalar(v1[:], v1[:], length, -1.0, ALU.mult, ALU.mult))
                c.link(dve.tensor_tensor(v0[:], v0[:], v1[:], ALU.add))
                c.link(dve.tensor_scalar(v1[:], v0[:], rlength, 0.0, ALU.mult, ALU.is_lt))
                c.link(dve.scalar_tensor_tensor(out=v0[:], in0=v1[:], scalar=length, in1=v0[:], op0=ALU.mult, op1=ALU.add))
                c.link(dve.tensor_scalar(v0[:], v0[:], float(M) / (M - 1), -0.5, ALU.mult, ALU.add))
                c.link(dve.tensor_copy(vi[:], v0[:]))
                c.link(dve.tensor_copy(v1[:], vi[:]))
                c.link(dve.tensor_tensor(dxf[:], v1[:], v0[:], ALU.is_gt))
                c.link(dve.tensor_tensor(v1[:], v1[:], dxf[:], ALU.subtract))
                c.tick(dve.tensor_scalar(ibf[:], v1[:], 1.0, None, ALU.add))
                dve.tensor_tensor(dxf[:], v0[:], v1[:], ALU.subtract).then_inc(s["off_ready"], 1)
                dve.wait_ge(s["tab_ready"], 1)
                for j in range(GH):
                    r = slice(32 * j, 32 * j + 32)
                    for p in range(3):
                        last = dve.tensor_copy(T2[r, p, :, r], T1[r, p, 1, :].rearrange("p (g j c) -> p g j c", g=NG, j=GH)[:, :, j, :])
                c.link(last)
                dve.wait_ge(s["dxT_ps"], 1)
                for g in range(NG):
                    src = PS[:, 0, 0:QT * HK].rearrange("p (t h k) -> p k t h", t=QT, k=NK)[:, :, :, g * GH:(g + 1) * GH]
                    last = dve.tensor_copy(dxg[:, g].rearrange("p k (t h) -> p k t h", t=QT), src)
                last.then_inc(s["dxg_ready"], 1)

                def weigh(g):
                    c.link(dve.reduce_sum(pkr[:].rearrange("p k s q -> p (k s q)"),
                                          pk[:].rearrange("p k s q c -> p (k s q) c"), AX_X))
                    c.link(dve.tensor_tensor(sc[:], pkr[:, :, 1, :], dxg[:, g], ALU.mult))
                    c.link(dve.tensor_tensor(sc[:], sc[:], pkr[:, :, 0, :], ALU.add))
                    c.link(dve.reduce_max(sm[:, 0, :], sc[:].rearrange("p k q -> p q k"), AX_X))
                    dve.tensor_tensor(sc[:], sc[:], sm[:, 0, :].unsqueeze(1).to_broadcast([P, NK, QT * GH]),
                                      ALU.subtract).then_inc(s["sc_in"], 1)

                def combine(g):
                    dve.wait_ge(s["sc_exp"], g + 1)
                    c.link(dve.reduce_sum(sm[:, 1, :], ee[:].rearrange("p k q -> p q k"), AX_X))
                    c.link(dve.reciprocal(sm[:, 2, :], sm[:, 1, :]))
                    c.link(dve.tensor_tensor(coef[:, :, 0, :], ee[:],
                                             sm[:, 2, :].unsqueeze(1).to_broadcast([P, NK, QT * GH]), ALU.mult))
                    c.link(dve.tensor_tensor(coef[:, :, 1, :], coef[:, :, 0, :], dxg[:, g], ALU.mult))
                    w = coef[:].rearrange("p k s q -> p (k s q)").unsqueeze(2).to_broadcast([P, NK * 2 * QT * GH, HD])
                    v = vv[:].rearrange("p k s q c -> p (k s q) c")
                    c.link(dve.tensor_tensor(v, v, w, ALU.mult))
                    dve.reduce_sum(ctok[:, :, g * GH * HD:(g + 1) * GH * HD],
                                   vv[:].rearrange("p k s (t j) c -> p t (j c) (k s)", t=QT), AX_X)\
                       .then_inc(s["ctok_ready"], 1)
                    dve.wait_ge(s["ctok_ready"], g + 1)

                for n in range(NG * NK + 2):
                    if n < NG * NK:
                        dve.wait_ge(s["ev_a"], n + 1)
                        if n >= 2:
                            dve.wait_ge(s["g_ps"], n - 1)
                        dve.tensor_scalar(oh1[:, n % 2, 0:2, :], cbc[:, 0:2, :], pcol[:, 0:1], None, ALU.is_equal)\
                           .then_inc(s["oh_a"], 1)
                        dve.wait_ge(s["bc_c"], n + 1)
                        dve.tensor_scalar(oh2[:, n % 2, :], PS[:, 4, :], pcol[:, 1:2], None, ALU.is_equal)\
                           .then_inc(s["oh_c"], 1)
                        dve.wait_ge(s["ev_b"], n + 1)
                        dve.tensor_scalar(oh1[:, n % 2, 2:4, :], cbc[:, 2:4, :], pcol[:, 0:1], None, ALU.is_equal)\
                           .then_inc(s["oh_b"], 1)
                    if n >= 2:
                        m = n - 2
                        g, k = m // NK, m % NK
                        if k == 0 and g >= 1:
                            combine(g - 1)
                        dve.wait_ge(s["pt_ps"], m + 1)
                        pt = PS[:, 7, :].rearrange("p (q v s c) -> p v s q c", q=QT * GH, v=2, s=2)
                        q = qhg[:, g].rearrange("p t (j c) -> p (t j) c", j=GH)
                        dve.tensor_tensor(pk[:, k], pt[:, 0], q.unsqueeze(1).to_broadcast([P, 2, QT * GH, HD]), ALU.mult)
                        c.tick(dve.tensor_copy(vv[:, k], pt[:, 1]))
                        c.settle()
                        dve.sem_inc(s["pt_used"], 1)
                        if k == NK - 1:
                            weigh(g)
                combine(NG - 1)

                dve.wait_ge(s["y_ps"], 1)
                c.link(dve.tensor_tensor(X[:], X[:], PS[:, 1, :].rearrange("p (t d) -> p t d", t=QT), ALU.add))

                layernorm(X, xn, 1, "xn_ready")
                dve.wait_ge(s["xhi_ready"], 1)
                dve.tensor_tensor(xlo[:], PS[:, 0, :], xhi[:].bitcast(F32), ALU.subtract).then_inc(s["xlo_ready"], 1)
                dve.wait_ge(s["score_in"], 1)
                c.link(dve.tensor_tensor(rbi[:], rsc[:], eb0[:].unsqueeze(1).to_broadcast([P, QT, E0]), ALU.add))
                for t in range(QT):
                    last = dve.max(rmx[:, t, :], rbi[:, t, :])
                c.link(last)
                for t in range(QT):
                    last = dve.max_index(rix[:, t, :], rmx[:, t, :], rbi[:, t, :])
                c.link(last)
                c.link(dve.tensor_copy(rif[:], rix[:]))
                for t in range(QT):
                    last = dve.tensor_tensor(roh[:, t], erow[:].unsqueeze(1).to_broadcast([P, K0, E0]),
                                             rif[:, t, 0:K0].unsqueeze(2).to_broadcast([P, K0, E0]), ALU.is_equal)
                c.link(last)
                c.link(dve.reduce_sum(rms[:], roh[:].rearrange("p t k e -> p t e k"), AX_X))
                c.link(dve.tensor_tensor(rms[:], rms[:], rsc[:], ALU.mult))
                c.link(dve.reduce_sum(rsum[:, :, 0], rms[:], AX_X))
                c.link(dve.reciprocal(rsum[:, :, 1], rsum[:, :, 0]))
                c.link(dve.tensor_tensor(rcm[:], rms[:], rsum[:, :, 1:2].to_broadcast([P, QT, E0]), ALU.mult))
                c.link(dve.tensor_copy(cb3[:, :, 0, :], rcm[:]))
                c.link(dve.tensor_tensor(rbi[:], rcm[:], cb3[:, :, 0, :], ALU.subtract))
                c.link(dve.tensor_copy(cb3[:, :, 1, :], rbi[:]))
                dve.tensor_tensor(cb3[:, :, 2, :], rbi[:], cb3[:, :, 1, :], ALU.subtract).then_inc(s["cb3_ready"], 1)
                y_base[0] = 1
                dve_ffn(dve, C0, 1)
                dve.wait_ge(s["yt_ps"], 1)
                c.link(dve.tensor_tensor(X[:], X[:], PS[:, 6, :].rearrange("p (t d) -> p t d", t=QT), ALU.add))

                layernorm(X, xn, 2, "xn_ready")
                for g in range(NG):
                    dve.wait_ge(s["q1_ev"], g + 1)
                    c.link(dve.tensor_copy(qhi[:], qtmp[:, g, :]))
                    c.link(dve.scalar_tensor_tensor(out=qf[:, g, :], in0=qhi[:].bitcast(F32), scalar=pcol[:, 3:4],
                                                    in1=qtmp[:, g, :], op0=ALU.mult, op1=ALU.add))
                dve.sem_inc(s["qf_ready"], 1)
                dve.wait_ge(s["k1_ev"], NG)
                c.link(dve.tensor_copy(khi[:], ktmp[:]))
                for j in range(GH):
                    r = slice(32 * j, 32 * j + 32)
                    dve.scalar_tensor_tensor(out=Kbd[r, :, j, 0:M], in0=khi[r].bitcast(F32), scalar=pcol[r, 4:5],
                                             in1=ktmp[r], op0=ALU.mult, op1=ALU.add)
                    last = dve.scalar_tensor_tensor(out=Kb2[r, :, 32 * j:32 * j + M - P], in0=khi[r, :, P:M].bitcast(F32),
                                                    scalar=pcol[r, 4:5], in1=ktmp[r, :, P:M], op0=ALU.mult, op1=ALU.add)
                last.then_inc(s["kbd_ready"], 1)
                dve.wait_ge(s["v1_ps"], 1)
                dve.tensor_copy(V1[:], PS[:, 0, :])
                for j in range(GH):
                    r = slice(32 * j, 32 * j + 32)
                    last = dve.tensor_copy(V2d[r, :, r], PS[r, 1, :].rearrange("p (g j c) -> p g j c", g=NG, j=GH)[:, :, j, :])
                last.then_inc(s["v1_ready"], 1)
                for g in range(NG):
                    for t in range(QT):
                        u = g * QT + t
                        dve.wait_ge(s["mx_ps"], u + 1)
                        bank = 2 * (u % 3)
                        src = PS[:, bank:bank + 2, :].rearrange("p a (j m) -> p (a j) m", j=2)[:, :, 0:M]
                        dve.reduce_max(nmx[:, t, :], src, AX_X).then_inc(s["mx_used"], 1)
                    dve.wait_ge(s["mx_used"], QT * (g + 1))
                    if g >= 2:
                        dve.wait_ge(s["nm_ps"], g - 1)
                    nm = NMp[:, g % 2].rearrange("p t (j c) -> p t j c", j=GH)
                    c.link(dve.tensor_scalar(nmh[:], nmx[:], -1.0, None, ALU.mult))
                    dve.tensor_copy(nm[:, :, :, 24], nmh[:].bitcast(F32))
                    dve.scalar_tensor_tensor(out=nm[:, :, :, 25], in0=nmx[:], scalar=-1.0, in1=nmh[:].bitcast(F32),
                                             op0=ALU.mult, op1=ALU.subtract).then_inc(s["nm_ready"], 1)
                    dve.wait_ge(s["nm_ps"], g + 1)
                    dve.tensor_tensor(qf[:, g, :], qf[:, g, :].bitcast(F32), PS[:, 6, :], ALU.add).then_inc(s["qn_ready"], 1)
                for g in range(NG):
                    dve.wait_ge(s["ot_ps"], g + 1)
                    if g >= 1:
                        dve.wait_ge(s["ott_ps"], g)
                    dve.tensor_copy(ots[:], PS[:, 5, :]).then_inc(s["ot_ev"], 1)
                    dve.wait_ge(s["ott_ps"], g + 1)
                    pt = PS[:, 7, :].rearrange("p (t j c) -> p t j c", t=QT, j=GH)
                    c.link(dve.reciprocal(rden[:], pt[:, :, :, HD]))
                    av = att[:, :, g * GH * HD:(g + 1) * GH * HD].rearrange("p t (j c) -> p t j c", j=GH)
                    for t in range(QT):
                        last = dve.tensor_tensor(av[:, t], pt[:, t, :, 0:HD],
                                                 rden[:, t, :].unsqueeze(2).to_broadcast([P, GH, HD]), ALU.mult)
                    last.then_inc(s["att_step"], 1)
                dve.wait_ge(s["att_step"], NG)
                layernorm(att, att, 3, None)
                c.link(dve.tensor_tensor(att[:], att[:], gamma[:].unsqueeze(1).to_broadcast([P, QT, D]), ALU.mult))
                c.link(dve.tensor_tensor(att[:], att[:], beta[:].unsqueeze(1).to_broadcast([P, QT, D]), ALU.add))
                c.link(dve.tensor_tensor(X[:], X[:], att[:], ALU.add))
                layernorm(X, xn, 4, "xn_ready")
                dve.wait_ge(s["lg_ps"], 2)
                c.link(dve.tensor_scalar(CST[:, bass.ds(b * QT, QT), :],
                                         PS[:, 1, 0:QT * E1].rearrange("p (t e) -> p t e", t=QT), -20.0, None, ALU.mult))
                finish_turn(dve, "dve")

            c = Steps(dve, sk_dve)
            c.tick(dve.memset(onesm[:], 1.0))
            c.link(dve.memset(scol[:, 3, :], 0.0))
            u, v = srow[:, 3, :], scol[:, 3, :]
            ub = u.unsqueeze(2).to_broadcast([P, NT, E1])
            vb = v.unsqueeze(1).to_broadcast([P, NT, E1])
            for it in range(SINK):
                c.link(dve.tensor_tensor(sR[:], CST[:], vb, ALU.subtract))
                c.link(dve.reduce_max(srow[:, 0, :], sR[:], AX_X))
                dve.tensor_tensor(sR[:], sR[:], srow[:, 0, :].unsqueeze(2).to_broadcast([P, NT, E1]), ALU.subtract)\
                   .then_inc(sk_exp_in, 1)
                dve.wait_ge(sk_exp, 2 * it + 1)
                dve.reduce_sum(srow[:, 1, :], sE[:], AX_X).then_inc(sk_ln_in, 1)
                dve.wait_ge(sk_ln, 2 * it + 1)
                c.link(dve.tensor_tensor(u, srow[:, 0, :], srow[:, 2, :], ALU.add))
                c.link(dve.tensor_tensor(sR[:], CST[:], ub, ALU.subtract))
                dve.reduce_max(scol[:, 0, :], sR[:].rearrange("p t e -> p e t"), AX_X).then_inc(sk_colT, 1)
                dve.wait_ge(sk_diag, 2 * it + 1)
                c.link(dve.reduce_max(smx[:], PS[0:E1, 0, 0:P], AX_X))
                c.link(dve.tensor_scalar(sdg[:], ident[0:E1, 0:E1], smx[:, 0:1], None, ALU.mult))
                dve.sem_inc(sk_colT, 1)
                dve.wait_ge(sk_diag, 2 * it + 2)
                c.link(dve.tensor_copy(scol[:, 0, :], PS[:, 1, 0:E1]))
                dve.tensor_tensor(sR[:], sR[:], scol[:, 0, :].unsqueeze(1).to_broadcast([P, NT, E1]), ALU.subtract)\
                   .then_inc(sk_exp_in, 1)
                dve.wait_ge(sk_exp, 2 * it + 2)
                dve.reduce_sum(scol[:, 1, :], sE[:].rearrange("p t e -> p e t"), AX_X).then_inc(sk_sum_in, 1)
                dve.wait_ge(sk_ln, 2 * it + 2)
                c.link(dve.tensor_tensor(v, scol[:, 0, :], scol[:, 2, :], ALU.add))
            c.link(dve.tensor_tensor(sR[:], CST[:], ub, ALU.subtract))
            c.link(dve.tensor_tensor(sR[:], sR[:], vb, ALU.subtract))
            dve.sem_inc(sk_exp_in, 1)
            c.link(dve.tensor_scalar(rank[:], sR[:], EXP_FLOOR, None, ALU.is_ge))
            dve.wait_ge(sk_exp, 2 * SINK + 1)
            c.link(dve.tensor_tensor(sE[:], sE[:], rank[:], ALU.mult))
            for t in range(NT):
                mine = sE[:, t, :].unsqueeze(2).to_broadcast([P, E1, E1])
                other = sE[:, t, :].unsqueeze(1).to_broadcast([P, E1, E1])
                dve.tensor_tensor(rk1[:, t], other, mine, ALU.is_gt)
                last = dve.tensor_tensor(rk2[:, t], other, mine, ALU.is_ge)
            c.link(last)
            r1 = rk1[:].rearrange("p t a b -> p t (a b)")
            r2 = rk2[:].rearrange("p t a b -> p t (a b)")
            c.link(dve.tensor_tensor(r2, r2, r1, ALU.subtract))
            c.link(dve.tensor_tensor(r2, r2, lower[:].unsqueeze(1).to_broadcast([P, NT, E1 * E1]), ALU.mult))
            c.link(dve.tensor_tensor(r2, r2, r1, ALU.add))
            c.link(dve.reduce_sum(rank[:], rk2[:], AX_X))
            c.tick(dve.tensor_scalar(sR[:], rank[:], 0.0, None, ALU.is_equal))
            c.tick(dve.memset(w3[:], 0.0))
            c.link(dve.tensor_scalar(rank[:], rank[:], 1.0, None, ALU.is_equal))
            c.link(dve.tensor_tensor(sR[:], sR[:], sE[:, :, 0:1].to_broadcast([P, NT, E1]), ALU.mult))
            c.link(dve.tensor_tensor(rank[:], rank[:], sE[:, :, 1:2].to_broadcast([P, NT, E1]), ALU.mult))
            c.link(dve.tensor_tensor(sR[:], sR[:], rank[:], ALU.add))
            c.link(dve.tensor_copy(w3[:, :, 0, 0:E1], sR[:]))
            c.link(dve.tensor_tensor(sR[:], sR[:], w3[:, :, 0, 0:E1], ALU.subtract))
            c.link(dve.tensor_copy(w3[:, :, 1, 0:E1], sR[:]))
            dve.tensor_tensor(w3[:, :, 2, 0:E1], sR[:], w3[:, :, 1, 0:E1], ALU.subtract).then_inc(w3_ready, 1)
            dve.wait_ge(experts1_in, 48)
            for h, l, r in ((wg1h, wg1l, wg1r), (wu1h, wu1l, wu1r)):
                c.link(dve.tensor_copy(h[:], r[:]))
                dve.tensor_tensor(l[:], r[:], h[:].bitcast(F32), ALU.subtract).then_inc(experts1_split, 1)
            with dve.Fori(0, B) as b:
                dve.tensor_copy(xhi[:], XT3[:, bass.ds(b * S, S)]).then_inc(s["xhi_ready"], 1)
                dve.wait_ge(s["xhi_ready"], 1)
                dve.tensor_tensor(xlo[:], XT3[:, bass.ds(b * S, S)], xhi[:].bitcast(F32), ALU.subtract)\
                   .then_inc(s["xlo_ready"], 1)
                y_base[0] = 0
                dve_ffn(dve, C1, C1 // E1)
                dve.wait_ge(s["yt_ps"], 1)
                dve.tensor_tensor(X[:], XR[:, bass.ds(b * QT, QT), :], PS[:, 6, :].rearrange("p (t d) -> p t d", t=QT),
                                  ALU.add).then_inc(s["x_sum"], 1)
                finish_turn(dve, "dve")

        def pe_ffn(pe, chunks, per_expert, wgh, wgl, wuh, wul, wd):
            def down(j):
                pe.wait_ge(s["h_ready"], j + 1)
                pe.matmul(PS[:, 7, :], wd[:, j, :], hh[:, j % 2, :], start=(j == 0), stop=(j == chunks - 1),
                          skip_group_check=True).then_inc(s["y_ps"], 1)

            for j in range(chunks):
                cs = slice(j * P, (j + 1) * P)
                if j >= 2:
                    pe.wait_ge(s["sg_ready"], j - 1)
                for n, (w, x) in enumerate(((wgh, xhi), (wgh, xlo), (wgl, xhi))):
                    pe.matmul(PS[:, j % 2, :], w[:, cs], x[:], start=(n == 0), stop=(n == 2))
                if j >= 2:
                    pe.wait_ge(s["h_ready"], j - 1)
                for n, (w, x) in enumerate(((wuh, xhi), (wuh, xlo), (wul, xhi))):
                    last = pe.matmul(PS[:, 2 + j % 2, :], w[:, cs], x[:], start=(n == 0), stop=(n == 2))
                if per_expert == 1:
                    for i in range(GH):
                        e = (GH * j + i) // (I0 // 32)
                        last = pe.matmul(PS[32 * i:32 * i + 32, 4 + j % 2, :], ident3b[:, e:e + 1].to_broadcast([96, 32]),
                                         cbT[:], start=True, stop=True)
                elif j % per_expert == 0:
                    e = j // per_expert
                    last = pe.matmul(PS[:, 4 + e % 2, :], ident3b[:, e:e + 1].to_broadcast([96, P]),
                                     cbT[:], start=True, stop=True)
                last.then_inc(s["gu_ps"], 1)
                if j >= 1:
                    down(j - 1)
            down(chunks - 1)
            pe.wait_ge(s["y_ps"], y_base[0] + chunks)
            pe.sem_inc(s["acc_ps"], 1)
            pe.wait_ge(s["yT_ready"], 1)
            for t in range(QT):
                last = pe.transpose(PS[:, 6, t * P:(t + 1) * P], yT[:, t * P:(t + 1) * P], ident[:])
            last.then_inc(s["yt_ps"], 1)

        @block.tensor
        def _(pe):
            pe.wait_ge(consts_in, 16 * N_CONSTS)
            pe.wait_ge(consts_made, 2)
            with pe.Fori(0, B) as b:
                def turn(n):
                    pe.wait_ge(s["xn_ready"], n + 1)
                    for t in range(QT):
                        last = pe.transpose(PS[:, 0, t * P:(t + 1) * P], xn[:, t, :], ident[:])
                    last.then_inc(s["xnT_ps"], 1)
                    pe.wait_ge(s["xnT_ready"], n + 1)

                pe.wait_ge(s["ctx_in"], 32)
                pe.wait_ge(s["tails"], 2)
                for ch in range(2):
                    for n in range(2):
                        rows = cpad[:, n:n + P] if ch == 0 else ctail[:, n, :]
                        there = vrow[:, n:n + P] if ch == 0 else vtail[:, n, :]
                        o = PS[:, 4 + ch, n * 2 * D:(n + 1) * 2 * D]
                        pe.matmul(o, rows, wkv[:], start=True, stop=False)
                        last = pe.matmul(o, there, bkv[:], start=False, stop=True)
                last.then_inc(s["tab_ps"], 1)

                turn(0)
                pe.matmul(PS[:, 1, :], wq0[:], xnT[:], start=True, stop=True).then_inc(s["q_ps"], 1)
                for t in range(QT):
                    o = PS[:, 2, t * P:(t + 1) * P]
                    pe.matmul(o, xnT[:, t * P:(t + 1) * P], wq0[:], start=True, stop=False)
                    last = pe.matmul(o, onerow[:], bq0[:], start=False, stop=True)
                last.then_inc(s["q_ps"], 1)
                pe.wait_ge(s["qT_ready"], 1)
                pe.matmul(PS[0:HK, 3, :], woff[:], qT[:], start=True, stop=True).then_inc(s["off_ps"], 1)
                pe.wait_ge(s["off_ready"], 1)
                for t in range(QT):
                    last = pe.transpose(PS[:, 0, t * HK:(t + 1) * HK], dxf[:, t * P:(t + 1) * P], ident[0:HK, 0:HK])
                last.then_inc(s["dxT_ps"], 1)
                pe.wait_ge(s["dxg_ready"], 1)

                for n in range(NG * NK + 2):
                    if n < NG * NK:
                        g, k = n // NK, n % NK
                        row = lambda j: (GH * g + j) * NK + k
                        if n >= 1:
                            pe.wait_ge(s["ev_a"], n)
                        for j in range(2):
                            last = pe.matmul(PS[:, j, :], identb[0:HK, row(j):row(j) + 1].to_broadcast([HK, P]), ibf[:],
                                             start=True, stop=True)
                        last.then_inc(s["bc_a"], 1)
                        if n >= 1:
                            pe.wait_ge(s["ev_b"], n)
                        for j in range(2, 4):
                            last = pe.matmul(PS[:, j, :], identb[0:HK, row(j):row(j) + 1].to_broadcast([HK, P]), ibf[:],
                                             start=True, stop=True)
                        last.then_inc(s["bc_b"], 1)
                        if n >= 1:
                            pe.wait_ge(s["oh_c"], n)
                        for j in range(4):
                            last = pe.matmul(PS[32 * j:32 * j + 32, 4, :],
                                             identb[0:HK, row(j):row(j) + 1].to_broadcast([HK, 32]), ibf[:],
                                             start=True, stop=True)
                        last.then_inc(s["bc_c"], 1)
                    if 1 <= n <= NG * NK:
                        m = n - 1
                        g = m // NK
                        o = PS[:, 5 + m % 2, :]
                        if m >= 2:
                            pe.wait_ge(s["g_ev"], m - 1)
                        pe.wait_ge(s["oh_c"], m + 1)
                        for p in range(3):
                            pe.matmul(o, T2[:, p, g, :], oh2[:, m % 2, :], start=(p == 0), stop=False, skip_group_check=True)
                        pe.wait_ge(s["oh_a"], m + 1)
                        pe.wait_ge(s["oh_b"], m + 1)
                        for p in range(3):
                            for j in range(GH):
                                h = GH * g + j
                                last = pe.matmul(o[32 * j:32 * j + 32, :], T1[:, p, 0, 32 * h:32 * h + 32], oh1[:, m % 2, j, :],
                                                 start=False, stop=(p == 2), skip_group_check=True)
                        last.then_inc(s["g_ps"], 1)
                    if n >= 2:
                        m = n - 2
                        pe.wait_ge(s["g_ev"], m + 1)
                        if m >= 1:
                            pe.wait_ge(s["pt_used"], m)
                        for t in range(QT):
                            last = pe.transpose(PS[:, 7, t * P:(t + 1) * P], gs[:, m % 2, t * P:(t + 1) * P], ident[:])
                        last.then_inc(s["pt_ps"], 1)

                pe.wait_ge(s["ctok_ready"], NG)
                for t in range(QT):
                    last = pe.transpose(PS[:, 0, t * P:(t + 1) * P], ctok[:, t, :], ident[:])
                last.then_inc(s["ctxT_ps"], 1)
                pe.wait_ge(s["ctxT_ready"], 1)
                for t in range(QT):
                    o = PS[:, 1, t * P:(t + 1) * P]
                    pe.matmul(o, ctxT[:, t * P:(t + 1) * P], wo[:], start=True, stop=False)
                    last = pe.matmul(o, onerow[:], bo[:], start=False, stop=True)
                last.then_inc(s["y_ps"], 1)

                turn(1)
                for t in range(QT):
                    last = pe.matmul(PS[:, 1, t * E0:(t + 1) * E0], xnT[:, t * P:(t + 1) * P], gw0[:], start=True, stop=True)
                last.then_inc(s["lg_ps"], 1)
                pe.wait_ge(s["cb3_ready"], 1)
                turned = PS[0:96, 2, :].bitcast(BF16)
                for t in range(QT):
                    last = pe.transpose(turned[:, t * P:(t + 1) * P], cb3[:, t].rearrange("p a e -> p (a e)"), identb[:])
                last.then_inc(s["cbT_ps"], 1)
                pe.wait_ge(s["cbT_ready"], 1)
                pe.wait_ge(s["xlo_ready"], 1)
                pe.wait_ge(experts0_split, 2)
                pe.wait_ge(experts0_in, 48)
                y_base[0] = 1
                pe_ffn(pe, C0, 1, wg0h, wg0l, wu0h, wu0l, wd0)

                turn(2)
                for g in range(NG):
                    pe.matmul(PS[:, g, :], wq1[:, g * P:(g + 1) * P], xnT[:], start=True, stop=True).then_inc(s["q1_ps"], 1)
                for g in range(NG):
                    pe.matmul(PS[:, 4 + g, 0:M], wk1[:, g * P:(g + 1) * P], cpad[:, 1:1 + M], start=True, stop=True)\
                      .then_inc(s["k1_ps"], 1)
                pe.wait_ge(s["q1_ev"], 2)
                pe.matmul(PS[:, 0, :], cpad[:, 1:1 + P], wv1[:], start=True, stop=False)
                pe.matmul(PS[:, 0, :], vrow[:, 1:1 + P], bv1[:], start=False, stop=True)
                pe.matmul(PS[:, 1, :], ctail[:, 1, :], wv1[:], start=True, stop=False)
                pe.matmul(PS[:, 1, :], vtail[:, 1, :], bv1[:], start=False, stop=True).then_inc(s["v1_ps"], 1)
                pe.wait_ge(s["kbd_ready"], 1)
                pe.wait_ge(s["v1_ready"], 1)
                pe.wait_ge(s["qf_ready"], 1)
                for g in range(NG):
                    for t in range(QT):
                        u = g * QT + t
                        if u >= 3:
                            pe.wait_ge(s["mx_used"], u - 2)
                        for i in range(2):
                            o = PS[:, 2 * (u % 3) + i, :].rearrange("p (j m) -> p j m", j=2)[:, :, 0:M]
                            last = pe.matmul(o, qf[:, g, t * P:(t + 1) * P], Kbd[:, g, 2 * i:2 * i + 2, 0:M],
                                             start=True, stop=True)
                        last.then_inc(s["mx_ps"], 1)
                    pe.wait_ge(s["nm_ready"], g + 1)
                    if g >= 1:
                        pe.wait_ge(s["qn_ready"], g)
                    for t in range(QT):
                        last = pe.transpose(PS[:, 6, t * P:(t + 1) * P], NMp[:, g % 2, t, :], ident[:])
                    last.then_inc(s["nm_ps"], 1)
                for g in range(NG + 1):
                    if g < NG:
                        pe.wait_ge(s["qn_ready"], NG if g == 0 else g + 1)
                        if g >= 1:
                            pe.wait_ge(s["e_a"], g)
                        for j in range(2):
                            last = pe.matmul(PS[:, j, :], Kbd[:, g, j, 0:P], qf[:, g, :], start=True, stop=True)
                        last.then_inc(s["s_a"], 1)
                        if g >= 1:
                            pe.wait_ge(s["e_b"], g)
                        for j in range(2, 4):
                            last = pe.matmul(PS[:, j, :], Kbd[:, g, j, 0:P], qf[:, g, :], start=True, stop=True)
                        last.then_inc(s["s_b"], 1)
                        if g >= 1:
                            pe.wait_ge(s["e_c"], g)
                        pe.matmul(PS[:, 4, :], Kb2[:, g, :], qf[:, g, :], start=True, stop=True).then_inc(s["s_c"], 1)
                    if g >= 1:
                        m = g - 1
                        pe.wait_ge(s["e_a"], m + 1)
                        pe.wait_ge(s["e_b"], m + 1)
                        pe.wait_ge(s["e_c"], m + 1)
                        if m >= 1:
                            pe.wait_ge(s["ot_ev"], m)
                        pe.matmul(PS[:, 5, :], V2d[:, m, :], Ex2[:], start=True, stop=False, skip_group_check=True)
                        for j in range(GH):
                            last = pe.matmul(PS[32 * j:32 * j + 32, 5, :], V1[:, m * P + 32 * j:m * P + 32 * j + 32],
                                             Ex[:, j, :], start=False, stop=True, skip_group_check=True)
                        last.then_inc(s["ot_ps"], 1)
                        pe.wait_ge(s["ot_ev"], m + 1)
                        if m >= 1:
                            pe.wait_ge(s["att_step"], m)
                        for t in range(QT):
                            last = pe.transpose(PS[:, 7, t * P:(t + 1) * P], ots[:, t * P:(t + 1) * P], ident[:])
                        last.then_inc(s["ott_ps"], 1)

                turn(3)
                for t in range(QT):
                    last = pe.matmul(PS[:, 1, t * E1:(t + 1) * E1], xnT[:, t * P:(t + 1) * P], gw1[:], start=True, stop=True)
                last.then_inc(s["lg_ps"], 1)
                finish_turn(pe, "pe")

            for it in range(SINK):
                pe.wait_ge(sk_colT, 2 * it + 1)
                pe.transpose(PS[0:E1, 0, 0:P], scol[:, 0, :], ident[:]).then_inc(sk_diag, 1)
                pe.wait_ge(sk_colT, 2 * it + 2)
                pe.matmul(PS[:, 1, 0:E1], onesm[0:E1, :], sdg[:], start=True, stop=True).then_inc(sk_diag, 1)
                pe.wait_ge(sk_sum_in, it + 1)
                pe.matmul(PS[:, 2, 0:E1], onesm[:], scol[:, 1, :], start=True, stop=True).then_inc(sk_ln_in, 1)
            pe.wait_ge(w3_ready, 1)
            for b in range(B):
                turned = PS[0:96, 3 + b, :].bitcast(BF16)
                for t in range(QT):
                    last = pe.transpose(turned[:, t * P:(t + 1) * P], w3[:, b * QT + t].rearrange("p a e -> p (a e)"), identb[:])
                last.then_inc(w3_ps, 1)
            pe.wait_ge(w3_used, B)
            pe.wait_ge(experts1_in, 48)
            pe.wait_ge(experts1_split, 2)
            with pe.Fori(0, B) as b:
                pe.wait_ge(s["cbT_ready"], 1)
                pe.wait_ge(s["xlo_ready"], 1)
                y_base[0] = 0
                pe_ffn(pe, C1, C1 // E1, wg1h, wg1l, wu1h, wu1l, wd1)
                finish_turn(pe, "pe")


N_CONSTS = 27
_OUTS = [((B, S, D), "float32")]


def _layout(x, ctx_1024, mask_BxS2_if0, **w):
    import numpy as np
    f = np.float32

    def padded(m, slots, tail=()):
        fill = np.zeros(m.shape[:-1] + (32 - slots * HD,), f)
        fill[..., :len(tail)] = tail
        return np.concatenate([m] * slots + [fill], -1).reshape(m.shape[:-2] + (H * 32,))

    a = {}
    p = np.arange(P)
    a["ident"] = np.eye(P, dtype=f)
    a["ident3"] = np.tile(np.eye(32, dtype=f), (3, 1))
    slot = (p % 32) // HD
    pc = np.zeros((P, 8), f)
    pc[:, 0] = p
    pc[:, 1] = P + p % 32
    pc[:, 2] = p % NK - (NK + 1) // 2
    pc[:, 3] = -(slot == 1).astype(f)
    pc[:, 4] = -(slot == 2).astype(f)
    a["pcol"] = pc
    a["locrow"] = np.tile(np.arange(S, dtype=f), (HK, 1))
    a["erow"] = np.tile(np.arange(32, dtype=f), (P, 1))
    a["lower"] = np.tile(np.tril(np.ones((E1, E1), f), -1).reshape(1, -1), (P, 1))
    a["onerow"] = np.ones((1, P), f)
    v = np.zeros((1, CW), f)
    v[:, 1:1 + M] = 1
    a["vrow"] = v
    a["vtail"] = np.stack([np.tile(v[:, P + n:P + n + 32], (1, GH)) for n in range(2)], 1)
    a["wkv"] = np.concatenate([w["L0_xattn_Wk"].T, w["L0_xattn_Wv"].T], 1)
    a["wq0"] = w["L0_xattn_Wq"].T
    a["woff"] = w["L0_xattn_Woff"].T
    a["wo"] = w["L0_xattn_Wo"].T
    a["bkv"] = np.concatenate([w["L0_xattn_bk"], w["L0_xattn_bv"]])[None]
    a["bq0"] = w["L0_xattn_bq"][None]
    a["bo"] = w["L0_xattn_bo"][None]
    bc = np.zeros((P, 2), f)
    bc[:, 0] = w["L0_xattn_bq"]
    bc[:HK, 1] = w["L0_xattn_boff"]
    a["bcol"] = bc
    t = lambda m: m.transpose(1, 0, 2)
    a["wq1"] = padded(t(w["L1_xattn_Wq"]), 3)
    a["wk1"] = padded(t(w["L1_xattn_Wk"]), 3)
    a["wv1"] = padded(t(w["L1_xattn_Wv"]), 1)
    bq = padded(w["L1_xattn_bq"], 3).reshape(NG, P).T
    bk = padded(w["L1_xattn_bk"], 3, (1, 1)).reshape(NG, P).T
    a["bqk1"] = np.stack([bq, bk], 1)
    a["bv1"] = padded(w["L1_xattn_bv"], 1, (1,))[None]
    a["gamma"] = np.tile(w["L1_xattn_gamma"][None], (P, 1))
    a["beta"] = np.tile(w["L1_xattn_beta"][None], (P, 1))
    a["gw0"] = w["L0_ffn_gate_w"].T
    a["eb0"] = np.tile(w["L0_ffn_e_bias"][None], (P, 1))
    a["gw1"] = w["L1_ffn_gate_W"].T
    a["wg0"] = w["L0_ffn_w1"].transpose(1, 0, 2).reshape(D, -1)
    a["wu0"] = w["L0_ffn_w3"].transpose(1, 0, 2).reshape(D, -1)
    a["wd0"] = w["L0_ffn_w2"].reshape(C0, P, D).transpose(1, 0, 2)
    a["wg1"] = w["L1_ffn_W_gate"].reshape(-1, D).T
    a["wu1"] = w["L1_ffn_W_up"].reshape(-1, D).T
    a["wd1"] = w["L1_ffn_W_down"].transpose(0, 2, 1).reshape(C1, P, D).transpose(1, 0, 2)
    cp = np.zeros((B, D, CW), f)
    cp[:, :, 1:1 + M] = ctx_1024.transpose(0, 2, 1)
    a["ctxp"] = cp
    a["mask"] = np.repeat(mask_BxS2_if0[:, None, :], HK, 1)
    a["x"] = x
    return {k: np.ascontiguousarray(m) for k, m in a.items()}


def kernel(**inputs):
    import numpy as _np
    import concourse.bacc as _bacc
    from concourse.bass_utils import run_bass_kernel_spmd as _run

    nc = _bacc.Bacc("TRN2", target_bir_lowering=False, num_devices=1)
    arrays = _layout(**{k: _np.asarray(v) for k, v in inputs.items()})
    aps = {k: nc.dram_tensor("in_" + k, m.shape, mybir.dt.from_np(m.dtype), kind="ExternalInput").ap()
           for k, m in arrays.items()}
    out = nc.dram_tensor("out_0", _OUTS[0][0], F32, kind="ExternalOutput").ap()
    seq_kernel(nc, aps, out)
    r = _run(nc, [{"in_" + k: m for k, m in arrays.items()}], core_ids=[0])
    return r.results[0]["out_0"]
```

```python
import math
from contextlib import ExitStack

import concourse.bass as bass
from concourse import mybir

F32 = mybir.dt.float32
F32R = mybir.dt.float32r
BF16 = mybir.dt.bfloat16
I32 = mybir.dt.int32
U32 = mybir.dt.uint32
ALU = mybir.AluOpType
ACT = mybir.ActivationFunctionType
AX_X = mybir.AxisListType.X

P = 128
B, S, D = 4, 512, 128
M = 154
H, HD = 16, 8
NK = 5
QT = S // P
GH = 4
NG = H // GH
HK = H * NK
CW = 162
E0, I0, K0 = 32, 96, 4
E1, F1D = 8, 512
C0 = E0 * I0 // P
C1 = E1 * F1D // P
SINK = 20
EPS = 1e-5
EXP_FLOOR = -87.33654
NT = B * QT


class Steps:

    def __init__(self, eng, sem):
        self.eng, self.sem, self.n = eng, sem, 0

    def tick(self, ins):
        self.n += 1
        return ins.then_inc(self.sem, 1)

    def settle(self):
        if self.n:
            self.eng.wait_ge(self.sem, self.n)

    def link(self, ins):
        self.tick(ins)
        self.settle()


def seq_kernel(nc, a, out):
    ctx = ExitStack()
    with ctx:
        def sb(name, shape, dt=F32, where=ctx):
            return where.enter_context(nc.sbuf_tensor(name, shape, dt))

        def sem(name):
            return ctx.enter_context(nc.semaphore(name))

        PS = ctx.enter_context(nc.psum_tensor("PS", [P, 8, 512], F32))

        ident = sb("ident", [P, P])
        identb = sb("identb", [P, P], BF16)
        ident3 = sb("ident3", [3 * 32, 32])
        ident3b = sb("ident3b", [3 * 32, 32], BF16)
        pcol = sb("pcol", [P, 8])
        locrow = sb("locrow", [HK, S])
        erow = sb("erow", [P, 32])
        lower = sb("lower", [P, E1 * E1])
        onerow = sb("onerow", [1, P])
        vrow = sb("vrow", [1, CW])
        vtail = sb("vtail", [1, 2, P])
        wkv = sb("wkv", [D, 2 * D])
        wq0 = sb("wq0", [D, D])
        woff = sb("woff", [D, HK])
        wo = sb("wo", [D, D])
        bkv = sb("bkv", [1, 2 * D])
        bq0 = sb("bq0", [1, D])
        bo = sb("bo", [1, D])
        bcol = sb("bcol", [P, 2])
        wq1 = sb("wq1", [D, NG * P])
        wk1 = sb("wk1", [D, NG * P])
        wv1 = sb("wv1", [D, NG * P])
        bqk1 = sb("bqk1", [P, 2, NG])
        bv1 = sb("bv1", [1, NG * P])
        gamma = sb("gamma", [P, D])
        beta = sb("beta", [P, D])
        gw0 = sb("gw0", [D, E0])
        eb0 = sb("eb0", [P, E0])
        gw1 = sb("gw1", [D, E1])

        XR = sb("XR", [P, NT, D])
        with ExitStack() as raw_ctx:
            XT3 = sb("XT3", [D, B * S], F32, raw_ctx)
        xlall = sb("xlall", [D, B * S], F32R)
        CST = sb("CST", [P, NT, E1])

        XI = sb("XI", [P, QT, D])
        XX = sb("XX", [P, 2 * QT, D])
        xn = sb("xn", [P, 2 * QT, D])
        xnT = sb("xnT", [D, S])
        pnT = sb("pnT", [D, S])
        xhi = sb("xhi", [D, S], F32R)
        xlo = sb("xlo", [D, S], F32R)
        cbT = sb("cbT", [3 * 32, S], BF16)
        with ExitStack() as vv_ctx:
            vv1 = sb("vv1", [P, NK, 2, QT * GH, HD], F32, vv_ctx)
        sg = sb("sg", [P, 2, S])
        hh = sb("hh", [P, 2, S])
        yT = sb("yT", [D, S])
        st = sb("st", [P, 2 * QT, 6])
        mv = sb("mv", [P, 2 * QT, 2])
        var = sb("var", [P, 2 * QT])
        std = sb("std", [P, 2 * QT])
        rstd = sb("rstd", [P, 2 * QT])

        loop_ctx = ExitStack()
        lsb = lambda name, shape, dt=F32: sb(name, shape, dt, loop_ctx)
        wg0h = lsb("wg0h", [D, C0 * P], F32R)
        wu0h = lsb("wu0h", [D, C0 * P], F32R)
        with ExitStack() as raw_ctx:
            wg0r = sb("wg0r", [D, C0 * P], F32, raw_ctx)
            wu0r = sb("wu0r", [D, C0 * P], F32, raw_ctx)
        wg0l = lsb("wg0l", [D, C0 * P], F32R)
        wu0l = lsb("wu0l", [D, C0 * P], F32R)
        wd0 = lsb("wd0", [P, C0, D])
        cpad = lsb("cpad", [D, CW])
        cprev = lsb("cprev", [D, CW])
        ctailp = lsb("ctailp", [D, P])
        ctail = lsb("ctail", [D, 2, P])
        mski = lsb("mski", [HK, M], I32)
        mskf = lsb("mskf", [HK, M])
        len3 = lsb("len3", [HK, 4])
        T1 = lsb("T1", [P, 3, 2, H * 32], BF16)
        T2 = lsb("T2", [P, 3, NG, P], BF16)
        Kbd = lsb("Kbd", [P, NG, GH, 160], F32R)
        Kb2 = lsb("Kb2", [P, NG, P], F32R)
        V2d = lsb("V2d", [P, NG, P])
        NMp = lsb("NMp", [P, 2, QT, P])
        V1 = lsb("V1", [P, NG * P])

        att = lsb("att", [P, QT, D])

        a_ctx = ExitStack()
        asb = lambda name, shape, dt=F32: sb(name, shape, dt, a_ctx)
        qT = asb("qT", [D, S])
        v0 = asb("v0", [HK, S])
        v1 = asb("v1", [HK, S])
        vi = asb("vi", [HK, S], I32)
        dxf = asb("dxf", [HK, S])
        ibf = asb("ibf", [HK, S], BF16)
        cbc = asb("cbc", [P, GH, S], BF16)
        oh1 = asb("oh1", [P, 2, GH, S], BF16)
        oh2 = asb("oh2", [P, 2, S], BF16)
        gs = asb("gs", [P, 2, S])
        qhg = asb("qhg", [P, NG, QT, GH * HD])
        dxg = asb("dxg", [P, NG, NK, QT * GH])
        tabf, tabr = xnT, qT
        pk = asb("pk", [P, NK, 2, QT * GH, HD])
        vv0 = asb("vv0", [P, NK, 2, QT * GH, HD])
        pkr = asb("pkr", [P, NK, 2, QT * GH])
        sc = asb("sc", [P, NK, QT * GH])
        ee = asb("ee", [P, NK, QT * GH])
        coef = asb("coef", [P, 2, NK, 2, QT * GH])
        sm = asb("sm", [P, 3, QT * GH])
        ctok = asb("ctok", [P, QT, D])
        ctxT = yT
        vv = (vv0, vv1)
        a_ctx.close()

        c_ctx = ExitStack()
        csb = lambda name, shape, dt=F32: sb(name, shape, dt, c_ctx)
        ktmp = csb("ktmp", [P, NG, M])
        khi = csb("khi", [P, NG, M], F32R)
        qhi = csb("qhi", [P, 2, S], F32R)
        qtmp = csb("qtmp", [P, NG, S])
        qf = csb("qf", [P, NG, S], F32R)
        Ex2 = csb("Ex2", [P, S])
        ots = csb("ots", [P, S])
        rsc = csb("rsc", [P, QT, E0])
        rbi = csb("rbi", [P, QT, E0])
        rmx = csb("rmx", [P, QT, 8])
        rix = csb("rix", [P, QT, 8], U32)
        rif = csb("rif", [P, QT, 8])
        roh = csb("roh", [P, QT, K0, E0])
        rms = csb("rms", [P, QT, E0])
        rcm = csb("rcm", [P, QT, E0])
        rsum = csb("rsum", [P, QT, 2])
        cb3 = csb("cb3", [P, QT, 3, 32], BF16)
        nmx = csb("nmx", [P, QT, GH])
        nmh = csb("nmh", [P, QT, GH], F32R)
        Ex = csb("Ex", [P, GH, S])
        rden = csb("rden", [P, QT, GH])
        c_ctx.close()
        loop_ctx.close()

        f_ctx = ExitStack()
        fsb = lambda name, shape, dt=F32: sb(name, shape, dt, f_ctx)
        wg1h = fsb("wg1h", [D, C1 * P], F32R)
        wu1h = fsb("wu1h", [D, C1 * P], F32R)
        with ExitStack() as raw_ctx:
            wg1r = sb("wg1r", [D, C1 * P], F32, raw_ctx)
            wu1r = sb("wu1r", [D, C1 * P], F32, raw_ctx)
        wg1l = fsb("wg1l", [D, C1 * P], F32R)
        wu1l = fsb("wu1l", [D, C1 * P], F32R)
        wd1h = fsb("wd1h", [P, C1, D], F32R)
        with ExitStack() as raw_ctx:
            wd1r = sb("wd1r", [P, C1, D], F32, raw_ctx)
        wd1l = fsb("wd1l", [P, C1, D], F32R)
        xhall = fsb("xhall", [D, B * S], F32R)
        hhi = fsb("hhi", [P, 3, S], F32R)
        hlo = fsb("hlo", [P, 3, S], F32R)
        wTall = fsb("wTall", [3 * 32, B * S], BF16)
        w3 = fsb("w3", [P, NT, 3, 32], BF16)
        sR = fsb("sR", [P, NT, E1])
        sE = fsb("sE", [P, NT, E1])
        sG = fsb("sG", [P, NT, E1])
        sQ = fsb("sQ", [P, NT, E1])
        sT = fsb("sT", [P, NT, E1])
        srow = fsb("srow", [P, 4, NT])
        scol = fsb("scol", [P, 4, E1])
        smx = fsb("smx", [E1, 1])
        onesm = fsb("onesm", [P, P])
        rk1 = fsb("rk1", [P, NT, E1, E1])
        rk2 = fsb("rk2", [P, NT, E1, E1])
        rank = fsb("rank", [P, NT, E1])
        f_ctx.close()

        consts_in = sem("consts_in")
        late_consts_in = sem("late_consts_in")
        experts0_in = sem("experts0_in")
        setup_pool = sem("setup_pool")
        consts_made = sem("consts_made")
        experts0_split = sem("experts0_split")
        experts0_low = sem("experts0_low")
        names = """next_in prev_in residual_made prev_used tails tailp tab_ps tab_f tab_split tab_ready ln_var ln_std xn_ready xnT_ps xnT_ready
            q_ps qT_ready qhg_ready off_ps off_read off_ready dxT_ps dxg_ready
            bc_a bc_b bc_c ev_a ev_b oh_a oh_b oh_c g_ps g_ev pt_ps pt_used sc_in sc_exp coef_ready vw_ready ctok_pool ctok_ready
            ctxT_ps ctxT_ready y_ps xhi_ready xlo_ready lg_ps score_in cb3_ready cbT_ps cbT_ready
            gu_ps g_in sg_ready h_used h_ready d_ps hhi_ready hlo_ready acc_ps yT_ready yt_ps x_sum
            q1_ps q1_ev k1_ps k1_ev v1_ps v1_ready kbd_ready qf_ready mx_ps mx_used nm_ready qn_ready cost_out x3_ready
            s_a s_b s_c e_a e_b e_c ot_ps ot_ev ott_ps att_step att_normed gamma_step cost_read kept out_in
            dve_step pool_step comb_step split_step arrived""".split()
        s = {n: sem(n) for n in names}
        last_names = """g_in sg_ready gu_ps h_used h_ready hhi_ready hlo_ready d_ps yT_ready yt_ps x_sum out_in
            dve_step arrived""".split()
        go = {e: sem("go_" + e) for e in ("pe", "act", "dve", "pool")}
        experts1_in = sem("experts1_in")
        experts1_split = sem("experts1_split")
        x_split = sem("x_split")
        sk_dve = sem("sk_dve")
        sk_row_in = sem("sk_row_in")
        sk_row_exp = sem("sk_row_exp")
        sk_row_sum = sem("sk_row_sum")
        sk_row_ln = sem("sk_row_ln")
        sk_part_max = sem("sk_part_max")
        sk_turned = sem("sk_turned")
        sk_col_max = sem("sk_col_max")
        sk_col_spread = sem("sk_col_spread")
        sk_col_in = sem("sk_col_in")
        sk_col_exp = sem("sk_col_exp")
        sk_part_sum = sem("sk_part_sum")
        sk_col_sum = sem("sk_col_sum")
        sk_col_ln = sem("sk_col_ln")
        w3_ready = sem("w3_ready")
        w3_ps = sem("w3_ps")
        w3_used = sem("w3_used")

        block = ctx.enter_context(nc.Block())
        INV_SQRT = 1.0 / math.sqrt(HD)

        def finish_turn(eng, name):
            eng.drain().then_inc(s["arrived"], 1)
            eng.wait_ge(go[name], 1)
            eng.sem_clear(go[name])

        @block.sync
        def _(sp):
            def load_batch(b):
                sp.dma_start(XI[:], a["x"][bass.ds(b, 1)].rearrange("a (t p) d -> p (a t) d", p=P)).then_inc(s["next_in"], 16)
                sp.dma_start(cpad[:], a["ctxp"][bass.ds(b, 1)].rearrange("a p m -> (a p) m")).then_inc(s["next_in"], 16)
                sp.dma_start(mski[:], a["mask"][bass.ds(b, 1)].rearrange("a p m -> (a p) m")).then_inc(s["next_in"], 16)

            def load_previous(b):
                sp.dma_start(cprev[:], a["ctxp"][bass.ds(b, 1)].rearrange("a p m -> (a p) m")).then_inc(s["prev_in"], 16)

            load_batch(0)
            consts = [(ident[:], a["ident"]), (wq0[:], a["wq0"]), (bq0[:], a["bq0"]), (bcol[:], a["bcol"]),
                      (onerow[:], a["onerow"]), (woff[:], a["woff"]), (pcol[:], a["pcol"]), (locrow[:], a["locrow"]),
                      (wkv[:], a["wkv"]), (bkv[:], a["bkv"]), (vrow[:], a["vrow"]), (vtail[:], a["vtail"])]
            assert len(consts) == N_CONSTS
            for dst, src in consts:
                sp.dma_start(dst, src).then_inc(consts_in, 16)
            late = [(ident3[:], a["ident3"]), (erow[:], a["erow"]), (lower[:], a["lower"]), (wo[:], a["wo"]),
                    (bo[:], a["bo"]), (wq1[:], a["wq1"]), (wk1[:], a["wk1"]), (wv1[:], a["wv1"]),
                    (bqk1[:], a["bqk1"]), (bv1[:], a["bv1"]), (gamma[:], a["gamma"]), (beta[:], a["beta"]),
                    (gw0[:], a["gw0"]), (eb0[:], a["eb0"]), (gw1[:], a["gw1"])]
            assert len(late) == N_LATE
            for dst, src in late:
                sp.dma_start(dst, src).then_inc(late_consts_in, 16)
            sp.dma_start(wg0r[:], a["wg0"]).then_inc(experts0_in, 16)
            sp.dma_start(wu0r[:], a["wu0"]).then_inc(experts0_in, 16)
            sp.dma_start(wd0[:], a["wd0"]).then_inc(experts0_in, 16)

            def next_turn(used=names):
                sp.wait_ge(s["arrived"], 4)
                for n in used:
                    sp.sem_clear(s[n])
                for e in go:
                    sp.sem_inc(go[e], 1)

            next_turn()
            for b in (0,):
                sp.wait_ge(s["residual_made"], 1)
                load_batch(b + 1)
                load_previous(b)
                sp.wait_ge(s["prev_in"], 16)
                next_turn()
            with sp.Fori(1, B - 1) as b:
                sp.wait_ge(s["residual_made"], 1)
                load_batch(b + 1)
                sp.wait_ge(s["prev_used"], 1)
                load_previous(b)
                sp.wait_ge(s["prev_in"], 16)
                next_turn()
            sp.wait_ge(s["prev_used"], 1)
            load_previous(B - 1)
            sp.wait_ge(s["prev_in"], 16)
            next_turn()
            next_turn()
            sp.dma_start(wg1r[:], a["wg1"]).then_inc(experts1_in, 16)
            sp.dma_start(wu1r[:], a["wu1"]).then_inc(experts1_in, 16)
            sp.dma_start(wd1r[:], a["wd1"]).then_inc(experts1_in, 16)
            with sp.Fori(0, B // 2) as b:
                for i in range(2):
                    sp.wait_ge(s["x_sum"], i + 1)
                    sp.dma_start(out[bass.ds(b + 2 * i, 1)].rearrange("a (t p) d -> p (a t) d", p=P), XX[:, i * QT:(i + 1) * QT])\
                      .then_inc(s["out_in"], 16)
                sp.wait_ge(s["out_in"], 32)
                next_turn(last_names)

        @block.gpsimd
        def _(pool):
            zeros = [T2, V2d, NMp, att]
            for z in zeros:
                pool.memset(z[:], 0.0).then_inc(setup_pool, 1)
            pool.memset(Kbd[:].bitcast(F32), 0.0).then_inc(setup_pool, 1)
            pool.memset(Kb2[:].bitcast(F32), 0.0).then_inc(setup_pool, 1)
            pool.memset(XR[:, 0:QT, :], 0.0).then_inc(setup_pool, 1)
            pool.wait_ge(consts_in, 16 * N_CONSTS)
            pool.tensor_copy(identb[:], ident[:]).then_inc(consts_made, 1)
            pool.wait_ge(setup_pool, 7)

            def prepare():
                c = Steps(pool, s["pool_step"])
                pool.wait_ge(s["next_in"], 48)
                for n in range(2):
                    src = cpad[:, P + n:P + n + 32].unsqueeze(1).to_broadcast([D, GH, 32])
                    pool.tensor_copy(ctail[:, n, :].rearrange("p (j r) -> p j r", j=GH), src).then_inc(s["tails"], 1)
                for i, ch in enumerate((1, 0)):
                    pool.wait_ge(s["tab_f"], 2 * i + 2)
                    c.link(pool.tensor_copy(T1[:, 0, ch], tabf[:]))
                    pool.tensor_tensor(tabr[:], tabf[:], T1[:, 0, ch], ALU.subtract).then_inc(s["tab_split"], 1)
                    pool.wait_ge(s["tab_split"], i + 1)
                    c.link(pool.tensor_copy(T1[:, 1, ch], tabr[:]))
                    pool.tensor_tensor(T1[:, 2, ch], tabr[:], T1[:, 1, ch], ALU.subtract).then_inc(s["tab_ready"], 1)
                    pool.wait_ge(s["tab_ready"], i + 1)

            def tail_of_previous():
                pool.tensor_copy(ctailp[:].rearrange("p (j r) -> p j r", j=GH),
                                 cprev[:, P + 1:P + 33].unsqueeze(1).to_broadcast([D, GH, 32])).then_inc(s["tailp"], 1)

            def combine():
                c = Steps(pool, s["comb_step"])
                for g in range(NG - 1):
                    pool.wait_ge(s["coef_ready"], g + 1)
                    w = coef[:, g % 2].rearrange("p k s q -> p (k s q)").unsqueeze(2).to_broadcast([P, NK * 2 * QT * GH, HD])
                    v = vv[g % 2][:].rearrange("p k s q c -> p (k s q) c")
                    pool.tensor_tensor(v, v, w, ALU.mult).then_inc(s["vw_ready"], 1)
                    pool.wait_ge(s["vw_ready"], g + 1)
                    part = vv[g % 2][:].rearrange("p k s q c -> p (k s) (q c)")
                    for n in (5, 2, 1):
                        c.link(pool.tensor_tensor(part[:, 0:n], part[:, 0:n], part[:, n:2 * n], ALU.add))
                        if n == 5:
                            c.link(pool.tensor_tensor(part[:, 0:1], part[:, 0:1], part[:, 4:5], ALU.add))
                    pool.tensor_copy(ctok[:, :, g * GH * HD:(g + 1) * GH * HD],
                                     part[:, 0].rearrange("p (t c) -> p t c", t=QT)).then_inc(s["ctok_pool"], 1)
                    pool.wait_ge(s["ctok_pool"], g + 1)

            def split_queries():
                c = Steps(pool, s["split_step"])
                for g in range(NG):
                    pool.wait_ge(s["q1_ev"], g + 1)
                    c.link(pool.tensor_scalar(qhi[:, g % 2, :], qhi[:, g % 2, :].bitcast(F32), pcol[:, 3:4], None, ALU.mult))
                    pool.tensor_tensor(qf[:, g, :], qtmp[:, g, :], qhi[:, g % 2, :].bitcast(F32), ALU.add)\
                        .then_inc(s["qf_ready"], 1)

            def keep(slot):
                pool.tensor_tensor(XR[:, bass.ds(slot * QT, QT), :], XX[:, QT:],
                                   beta[:].unsqueeze(1).to_broadcast([P, QT, D]), ALU.add).then_inc(s["kept"], 1)

            def add_attention(slot, n):
                pool.wait_ge(s["att_normed"], n)
                pool.tensor_tensor(att[:], att[:], gamma[:].unsqueeze(1).to_broadcast([P, QT, D]), ALU.mult)\
                    .then_inc(s["gamma_step"], 1)
                pool.wait_ge(s["gamma_step"], n)
                rows = bass.ds(slot * QT, QT)
                pool.tensor_tensor(XR[:, rows, :], XR[:, rows, :], att[:], ALU.add).then_inc(s["x3_ready"], 1)

            def split_weights(loaded, split, weights):
                pool.wait_ge(loaded, 48)
                for n, (high, low, raw) in enumerate(weights):
                    pool.tensor_copy(high[:], raw[:]).then_inc(split, 1)
                    pool.wait_ge(split, 2 * n + 1)
                    pool.tensor_tensor(low[:], raw[:], high[:].bitcast(F32), ALU.subtract).then_inc(split, 1)

            prepare()
            finish_turn(pool, "pool")
            pool.wait_ge(late_consts_in, 16 * N_LATE)
            pool.tensor_copy(ident3b[:], ident3[:]).then_inc(consts_made, 1)
            combine()
            prepare()
            finish_turn(pool, "pool")

            def turn_of_loop(b, more):
                tail_of_previous()
                keep(b)
                add_attention(b - 1, 1)
                combine()
                split_queries()
                if more:
                    prepare()
                finish_turn(pool, "pool")

            with pool.Fori(1, B - 1) as b:
                turn_of_loop(b, True)
            turn_of_loop(B - 1, False)
            tail_of_previous()
            keep(0)
            add_attention(B - 1, 1)
            split_queries()
            pool.wait_ge(s["kept"], 1)
            add_attention(0, 2)
            finish_turn(pool, "pool")
            pool.tensor_copy(xhall[:], XT3[:]).then_inc(x_split, 1)
            pool.wait_ge(x_split, 1)
            pool.tensor_tensor(xlall[:], XT3[:], xhall[:].bitcast(F32), ALU.subtract).then_inc(x_split, 1)
            split_weights(experts1_in, experts1_split, ((wg1h, wg1l, wg1r), (wu1h, wu1l, wu1r), (wd1h, wd1l, wd1r)))
            with pool.Fori(0, B // 2) as b:
                for n in range(2 * C1):
                    pool.wait_ge(s["hhi_ready"], n + 1)
                    if n >= 3:
                        pool.wait_ge(s["d_ps"], n - 2)
                    pool.tensor_tensor(hlo[:, n % 3, :], hh[:, n % 2, :], hhi[:, n % 3, :].bitcast(F32), ALU.subtract)\
                        .then_inc(s["hlo_ready"], 1)
                finish_turn(pool, "pool")

        def act_ffn(act, chunks, between):
            for j in range(chunks):
                act.wait_ge(s["g_in"], j + 1)
                if j >= 2:
                    act.wait_ge(s["h_ready"], j - 1)
                act.activation(sg[:, j % 2, :], PS[:, 0, :], ACT.Silu).then_inc(s["sg_ready"], 1)
                between(j)
            act.wait_ge(s["acc_ps"], 1)
            act.copy(yT[:], PS[:, 3, :]).then_inc(s["yT_ready"], 1)

        @block.scalar
        def _(act):
            def deviation(n, tiles=slice(0, 2 * QT)):
                act.wait_ge(s["ln_var"], n)
                act.activation(std[:, tiles], var[:, tiles], ACT.Sqrt).then_inc(s["ln_std"], 1)

            def turned(n, dst, bank):
                act.wait_ge(s["xnT_ps"], n)
                act.copy(dst[:], PS[:, bank, :]).then_inc(s["xnT_ready"], 1)

            def sampling(prev, slot):
                for n in range(NG * NK + 1):
                    if prev and n in DEVIATIONS:
                        i = DEVIATIONS.index(n)
                        deviation(i + 1, slice(QT, 2 * QT) if i == 0 else slice(0, QT))
                    if n < NG * NK:
                        act.wait_ge(s["bc_a"], n + 1)
                        if n >= 1:
                            act.wait_ge(s["oh_a"], n)
                        act.copy(cbc[:, 0:2, :], PS[:, 0:2, :]).then_inc(s["ev_a"], 1)
                        act.wait_ge(s["bc_b"], n + 1)
                        if n >= 1:
                            act.wait_ge(s["oh_b"], n)
                        act.copy(cbc[:, 2:4, :], PS[:, 2:4, :]).then_inc(s["ev_b"], 1)
                    if n >= 1:
                        act.wait_ge(s["g_ps"], n)
                        if n >= 3:
                            act.wait_ge(s["pt_ps"], n - 2)
                        act.copy(gs[:, (n - 1) % 2, :], PS[:, 5 + (n - 1) % 2, :]).then_inc(s["g_ev"], 1)
                    if n > NK and n % NK == 2:
                        g = n // NK - 1
                        act.wait_ge(s["sc_in"], g + 1)
                        act.activation(ee[:], sc[:], ACT.Exp, scale=0.5 * INV_SQRT).then_inc(s["sc_exp"], 1)
                if prev:
                    keys()
                    turned(1, pnT, 4)
                    finished(slot, 2)
                    values()
                act.wait_ge(s["sc_in"], NG)
                act.activation(ee[:], sc[:], ACT.Exp, scale=0.5 * INV_SQRT).then_inc(s["sc_exp"], 1)
                if prev:
                    queries(range(2))
                    act.wait_ge(s["cost_read"], 1)
                act.wait_ge(s["ctxT_ps"], 1)
                act.mul(ctxT[:], PS[:, 0, :], 0.5).then_inc(s["ctxT_ready"], 1)
                if prev:
                    queries(range(2, NG))

            def finished(slot, n):
                act.wait_ge(s["xnT_ps"], n)
                act.copy(XT3[:, bass.ds(slot * S, S)], PS[:, 0, :])
                act.copy(yT[:], PS[:, 0, :]).then_inc(s["xnT_ready"], 1)

            def keys():
                for g in range(NG):
                    act.wait_ge(s["k1_ps"], 2 * (g // 2) + 2)
                    src = PS[:, K_BANK[g], (g % 2) * 256:(g % 2) * 256 + M]
                    act.activation(ktmp[:, g, :], src, ACT.Identity, bias=bqk1[:, 1, g:g + 1])
                    act.activation(khi[:, g, :], src, ACT.Identity, bias=bqk1[:, 1, g:g + 1]).then_inc(s["k1_ev"], 1)

            def values():
                act.wait_ge(s["v1_ps"], 1)
                act.copy(V1[:], PS[:, 5, :])
                for j in range(GH):
                    r = slice(32 * j, 32 * j + 32)
                    last = act.copy(V2d[r, :, r], PS[r, 6, :].rearrange("p (g j c) -> p g j c", g=NG, j=GH)[:, :, j, :])
                last.then_inc(s["v1_ready"], 1)

            def queries(groups):
                for g in groups:
                    act.wait_ge(s["q1_ps"], g + 1)
                    if g >= 2:
                        act.wait_ge(s["qf_ready"], g - 1)
                    act.activation(qtmp[:, g, :], PS[:, 4 + g, :], ACT.Identity, bias=bqk1[:, 0, g:g + 1])
                    act.activation(qhi[:, g % 2, :], PS[:, 4 + g, :], ACT.Identity, bias=bqk1[:, 0, g:g + 1])\
                       .then_inc(s["q1_ev"], 1)

            def attend(j):
                g, part = (j - S_SLOT) // 3, (j - S_SLOT) % 3
                if j >= S_SLOT and g < NG and part == 0:
                    if g >= 1:
                        act.wait_ge(s["ot_ps"], g)
                    act.wait_ge(s["s_b"], g + 1)
                    act.activation(Ex[:, 2:4, :], PS[:, 6:8, :], ACT.Exp, scale=INV_SQRT).then_inc(s["e_b"], 1)
                    act.wait_ge(s["s_c"], g + 1)
                    act.activation(Ex2[:], PS[:, 5, :], ACT.Exp, scale=INV_SQRT).then_inc(s["e_c"], 1)
                if j >= S_SLOT and g < NG and part == 1:
                    act.wait_ge(s["s_a"], g + 1)
                    act.activation(Ex[:, 0:2, :], PS[:, 6:8, :], ACT.Exp, scale=INV_SQRT).then_inc(s["e_a"], 1)

            def prepare(j, ln, turns):
                if j == NORM_SLOT:
                    deviation(ln + 1, slice(0, QT))
                if j == TURN_SLOT:
                    turned(turns + 1, xnT, 4)
                if j == Q_SLOT:
                    act.wait_ge(s["q_ps"], 1)
                    act.activation(qT[:], PS[:, 4, :], ACT.Identity, bias=bcol[:, 0:1]).then_inc(s["qT_ready"], 1)

            def batch(prev, more=True, slot=None):
                norms, turns = (4, 3) if prev else (1, 1)

                def between(j):
                    if j == 0:
                        act.wait_ge(s["cbT_ps"], 1)
                        act.copy(cbT[:], PS[0:96, 3, :].bitcast(BF16)[:, 0:S]).then_inc(s["cbT_ready"], 1)
                    if prev:
                        attend(j)
                    if more:
                        prepare(j, norms, turns)

                sampling(prev, slot)
                deviation(norms, slice(0, QT))
                turned(turns, xnT, 0)
                act.copy(xhi[:], PS[:, 0, :]).then_inc(s["xhi_ready"], 1)
                act.wait_ge(s["lg_ps"], 1)
                act.activation(rsc[:], PS[:, 1, 0:QT * E0].rearrange("p (t e) -> p t e", t=QT), ACT.Sigmoid)\
                   .then_inc(s["score_in"], 1)
                act_ffn(act, C0, between)
                finish_turn(act, "act")

            act.wait_ge(consts_in, 16 * N_CONSTS)
            for j in range(C0):
                prepare(j, 0, 0)
            act.wait_ge(experts0_in, 48)
            act.copy(wg0h[:], wg0r[:]).then_inc(experts0_split, 1)
            act.copy(wu0h[:], wu0r[:]).then_inc(experts0_split, 1)
            finish_turn(act, "act")
            act.wait_ge(late_consts_in, 16 * N_LATE)
            batch(False)
            with act.Fori(1, B - 1) as b:
                batch(True, slot=b - 1)
            batch(True, False, B - 2)
            deviation(1, slice(QT, 2 * QT))
            keys()
            turned(1, pnT, 4)
            values()
            deviation(2, slice(0, QT))
            deviation(3, slice(0, QT))
            queries(range(NG))
            finished(B - 1, 2)
            for j in range(-1, S_SLOT + 3 * NG + 1):
                attend(j)
            deviation(4, slice(0, QT))
            deviation(5, slice(0, QT))
            finished(0, 3)
            finish_turn(act, "act")

            act.preload_act_table_set("natural_log_exp_and_others")
            for it in range(SINK):
                act.wait_ge(sk_row_in, it + 1)
                act.activation(sE[:], sR[:], ACT.Exp).then_inc(sk_row_exp, 1)
                act.wait_ge(sk_col_in, it + 1)
                act.activation(sG[:], sQ[:], ACT.Exp).then_inc(sk_col_exp, 1)
                if it == SINK - 1:
                    act.wait_ge(sk_row_sum, 1)
                    act.activation(srow[:, 2, :], srow[:, 1, :], ACT.Ln).then_inc(sk_row_ln, 1)
                act.wait_ge(sk_col_sum, it + 1)
                act.activation(scol[:, 2, :], PS[:, 2, 0:E1], ACT.Ln).then_inc(sk_col_ln, 1)
            act.wait_ge(sk_row_in, SINK + 1)
            act.activation(sE[:], sR[:], ACT.Exp).then_inc(sk_row_exp, 1)
            for b in range(B):
                act.wait_ge(w3_ps, b + 1)
                act.copy(wTall[:, b * S:(b + 1) * S], PS[0:96, 3 + b, :].bitcast(BF16)[:, 0:S]).then_inc(w3_used, 1)
            act.wait_ge(w3_used, B)

            def high_part(n):
                act.wait_ge(s["h_ready"], n + 1)
                if n >= 3:
                    act.wait_ge(s["d_ps"], n - 2)
                act.copy(hhi[:, n % 3, :], hh[:, n % 2, :]).then_inc(s["hhi_ready"], 1)

            def result(i):
                act.wait_ge(s["d_ps"], (i + 1) * C1)
                if i:
                    act.wait_ge(s["yt_ps"], i)
                act.copy(yT[:], PS[:, 3 + i, :]).then_inc(s["yT_ready"], 1)

            with act.Fori(0, B // 2) as b:
                for n in range(2 * C1):
                    act.wait_ge(s["g_in"], n + 1)
                    if n >= 2:
                        act.wait_ge(s["h_used"], n - 1)
                        act.wait_ge(s["h_ready"], n - 1)
                    act.activation(sg[:, n % 2, :], PS[:, 0, :], ACT.Silu).then_inc(s["sg_ready"], 1)
                    if n >= 1:
                        high_part(n - 1)
                    if n == C1 + 3:
                        result(0)
                high_part(2 * C1 - 1)
                result(1)
                finish_turn(act, "act")

        def dve_ffn(dve, chunks, between):
            for j in range(chunks):
                dve.wait_ge(s["sg_ready"], j + 1)
                dve.wait_ge(s["gu_ps"], j + 1)
                dve.tensor_tensor(sg[:, j % 2, :], sg[:, j % 2, :], PS[:, 1, :], ALU.mult).then_inc(s["h_used"], 1)
                dve.wait_ge(s["h_used"], j + 1)
                if j >= 2:
                    dve.wait_ge(s["d_ps"], j - 1)
                dve.tensor_tensor(hh[:, j % 2, :], sg[:, j % 2, :], PS[:, 2, :], ALU.mult).then_inc(s["h_ready"], 1)
                between(j)

        @block.vector
        def _(dve):
            dve.wait_ge(consts_in, 16 * N_CONSTS)
            dve.wait_ge(setup_pool, 7)

            def norm_stats(c, src, tiles):
                for t in tiles:
                    last = dve.bn_stats(st[:, t, :], src[:, t, :])
                c.link(last)
                for t in tiles:
                    last = dve.bn_aggr(mv[:, t, :], st[:, t, :])
                c.link(last)
                r = slice(tiles[0], tiles[-1] + 1)
                dve.tensor_scalar(var[:, r], mv[:, r, 1], EPS, None, ALU.add).then_inc(s["ln_var"], 1)

            def norm_apply(c, src, dst, tiles, n):
                r = slice(tiles[0], tiles[-1] + 1)
                dve.wait_ge(s["ln_std"], n)
                c.link(dve.reciprocal(rstd[:, r], std[:, r]))
                for t in tiles:
                    last = dve.tensor_scalar(dst[:, t, :], src[:, t, :], mv[:, t, 0:1], rstd[:, t:t + 1],
                                             ALU.subtract, ALU.mult)
                return last

            def prepare(c, j, ln):
                length, minus_length, rlength = len3[:, 1:2], len3[:, 2:3], len3[:, 3:4]
                if j == NORM_SLOT:
                    dve.wait_ge(s["next_in"], 48)
                    norm_stats(c, XI, range(QT))
                if j == NORM_SLOT + 1:
                    norm_apply(c, XI, xn, range(QT), ln + 1).then_inc(s["xn_ready"], 1)
                if j == TURN_SLOT:
                    c.link(dve.tensor_copy(mskf[:], mski[:]))
                    c.link(dve.reduce_sum(len3[:, 0:1], mskf[:], AX_X))
                    c.tick(dve.tensor_scalar(len3[:, 1:2], len3[:, 0:1], -1.0, float(M - 1), ALU.mult, ALU.add))
                    c.link(dve.tensor_scalar(len3[:, 2:3], len3[:, 0:1], float(M - 1), None, ALU.subtract))
                    c.link(dve.reciprocal(len3[:, 3:4], len3[:, 1:2]))
                if j == QT_SLOT:
                    dve.wait_ge(s["q_ps"], 2)
                    dve.tensor_copy(qhg[:].rearrange("p g t e -> p t g e"),
                                    PS[:, 4, :].rearrange("p (t g e) -> p t g e", t=QT, g=NG)).then_inc(s["qhg_ready"], 1)
                if j == OFF_SLOT:
                    dve.wait_ge(s["off_ps"], 1)
                    dve.tensor_scalar(v0[:], PS[0:HK, 4, :], bcol[0:HK, 1:2], pcol[0:HK, 2:3], ALU.add, ALU.add)\
                       .then_inc(s["off_read"], 1)
                    dve.wait_ge(s["off_read"], 1)
                    c.link(dve.tensor_tensor(v0[:], v0[:], locrow[:], ALU.add))
                if j == OFF_SLOT + 1:
                    c.link(dve.tensor_scalar(vi[:], v0[:], rlength, None, ALU.mult))
                    c.link(dve.scalar_tensor_tensor(out=v0[:], in0=vi[:], scalar=minus_length, in1=v0[:], op0=ALU.mult, op1=ALU.add))
                if j == OFF_SLOT + 2:
                    c.link(dve.tensor_scalar(v1[:], v0[:], rlength, 0.0, ALU.mult, ALU.is_lt))
                    c.link(dve.scalar_tensor_tensor(out=v0[:], in0=v1[:], scalar=length, in1=v0[:], op0=ALU.mult, op1=ALU.add))
                if j == OFF_SLOT + 3:
                    c.link(dve.tensor_scalar(v0[:], v0[:], float(M) / (M - 1), -0.5, ALU.mult, ALU.add))
                    c.link(dve.tensor_copy(vi[:], v0[:]))
                if j == OFF_SLOT + 4:
                    c.link(dve.tensor_tensor(dxf[:], vi[:], v0[:], ALU.is_gt))
                    c.link(dve.tensor_tensor(v1[:], vi[:], dxf[:], ALU.subtract))
                if j == OFF_SLOT + 5:
                    c.tick(dve.tensor_scalar(ibf[:], v1[:], 1.0, None, ALU.add))
                    dve.tensor_tensor(dxf[:], v0[:], v1[:], ALU.subtract).then_inc(s["off_ready"], 1)
                for i in range(2):
                    if j == TABLE_SLOTS[i]:
                        dve.wait_ge(s["tab_ps"], i + 1)
                        if i:
                            dve.wait_ge(s["tab_split"], 1)
                        t4 = tabf[:].rearrange("p (h v s c) -> p v h s c", h=H, v=2, s=2)
                        ps = PS[:, 4, :].rearrange("p (n v h c) -> p n v h c", n=2, v=2, h=H)
                        dve.tensor_copy(t4[:, :, :, 0, :], ps[:, 0]).then_inc(s["tab_f"], 1)
                        dve.wait_ge(s["tab_f"], 2 * i + 1)
                        dve.tensor_tensor(t4[:, :, :, 1, :], ps[:, 1], t4[:, :, :, 0, :], ALU.subtract).then_inc(s["tab_f"], 1)
                if j == DX_SLOT:
                    dve.wait_ge(s["tab_ready"], 1)
                    for h in range(GH):
                        r = slice(32 * h, 32 * h + 32)
                        for p in range(3):
                            c.tick(dve.tensor_copy(T2[r, p, :, r], T1[r, p, 1, :].rearrange("p (g h c) -> p g h c", g=NG, h=GH)[:, :, h, :]))
                    dve.wait_ge(s["dxT_ps"], 1)
                    for g in range(NG):
                        src = PS[:, 4, 0:QT * HK].rearrange("p (t h k) -> p k t h", t=QT, k=NK)[:, :, :, g * GH:(g + 1) * GH]
                        last = dve.tensor_copy(dxg[:, g].rearrange("p k (t h) -> p k t h", t=QT), src)
                    last.then_inc(s["dxg_ready"], 1)

            def attention_normed(c, n):
                norm_apply(c, att, att, range(QT), n).then_inc(s["att_normed"], 1)

            def residual_stats(c, slot, n):
                dve.wait_ge(s["x3_ready"], n)
                norm_stats(c, XR[:, bass.ds(slot * QT, QT), :], range(QT))

            def residual_normed(c, slot, n):
                norm_apply(c, XR[:, bass.ds(slot * QT, QT), :], xn, range(QT), n).then_inc(s["xn_ready"], 1)

            def costs(c, slot, n):
                dve.wait_ge(s["cost_out"], n)
                dve.tensor_scalar(CST[:, bass.ds(slot * QT, QT), :], PS[:, 1, 0:QT * E1].rearrange("p (t e) -> p t e", t=QT),
                                  -20.0, None, ALU.mult).then_inc(s["cost_read"], 1)

            def sampling(c, prev, slot):
                if prev:
                    norm_stats(c, XX, range(QT, 2 * QT))
                def weigh(g):
                    c.link(dve.reduce_sum(pkr[:].rearrange("p k s q -> p (k s q)"),
                                          pk[:].rearrange("p k s q c -> p (k s q) c"), AX_X))
                    c.link(dve.tensor_tensor(sc[:], pkr[:, :, 1, :], dxg[:, g], ALU.mult))
                    c.link(dve.tensor_tensor(sc[:], sc[:], pkr[:, :, 0, :], ALU.add))
                    c.link(dve.reduce_max(sm[:, 0, :], sc[:].rearrange("p k q -> p q k"), AX_X))
                    dve.tensor_tensor(sc[:], sc[:], sm[:, 0, :].unsqueeze(1).to_broadcast([P, NK, QT * GH]),
                                      ALU.subtract).then_inc(s["sc_in"], 1)

                def weights(g):
                    dve.wait_ge(s["sc_exp"], g + 1)
                    w = coef[:, g % 2]
                    c.link(dve.reduce_sum(sm[:, 1, :], ee[:].rearrange("p k q -> p q k"), AX_X))
                    c.link(dve.reciprocal(sm[:, 2, :], sm[:, 1, :]))
                    if g >= 2:
                        dve.wait_ge(s["vw_ready"], g - 1)
                    c.link(dve.tensor_tensor(w[:, :, 0, :], ee[:],
                                             sm[:, 2, :].unsqueeze(1).to_broadcast([P, NK, QT * GH]), ALU.mult))
                    dve.tensor_tensor(w[:, :, 1, :], w[:, :, 0, :], dxg[:, g], ALU.mult).then_inc(s["coef_ready"], 1)

                def combine_last():
                    g = NG - 1
                    dve.wait_ge(s["coef_ready"], NG)
                    w = coef[:, g % 2].rearrange("p k s q -> p (k s q)").unsqueeze(2).to_broadcast([P, NK * 2 * QT * GH, HD])
                    v = vv[g % 2][:].rearrange("p k s q c -> p (k s q) c")
                    c.link(dve.tensor_tensor(v, v, w, ALU.mult))
                    dve.reduce_sum(ctok[:, :, g * GH * HD:(g + 1) * GH * HD],
                                   vv[g % 2][:].rearrange("p k s (t j) c -> p t (j c) (k s)", t=QT), AX_X)\
                       .then_inc(s["ctok_ready"], 1)

                for n in range(NG * NK + 2):
                    if n < NG * NK:
                        dve.wait_ge(s["ev_a"], n + 1)
                        if n >= 2:
                            dve.wait_ge(s["g_ps"], n - 1)
                        dve.tensor_scalar(oh1[:, n % 2, 0:2, :], cbc[:, 0:2, :], pcol[:, 0:1], None, ALU.is_equal)\
                           .then_inc(s["oh_a"], 1)
                        dve.wait_ge(s["bc_c"], n + 1)
                        dve.tensor_scalar(oh2[:, n % 2, :], PS[:, 4, :], pcol[:, 1:2], None, ALU.is_equal)\
                           .then_inc(s["oh_c"], 1)
                        dve.wait_ge(s["ev_b"], n + 1)
                        dve.tensor_scalar(oh1[:, n % 2, 2:4, :], cbc[:, 2:4, :], pcol[:, 0:1], None, ALU.is_equal)\
                           .then_inc(s["oh_b"], 1)
                    if n == 1 and prev:
                        norm_apply(c, XX, xn, range(QT, 2 * QT), 1).then_inc(s["xn_ready"], 1)
                    if n == 2 and prev:
                        norm_stats(c, att, range(QT))
                    if n == 5 and prev:
                        attention_normed(c, 2)
                    if n == 9 and prev:
                        residual_stats(c, slot, 1)
                    if n == 12 and prev:
                        residual_normed(c, slot, 3)
                    if n >= 2:
                        m = n - 2
                        g, k = m // NK, m % NK
                        if k == 0 and g >= 1:
                            weights(g - 1)
                            if g >= 2:
                                dve.wait_ge(s["ctok_pool"], g - 1)
                        dve.wait_ge(s["pt_ps"], m + 1)
                        pt = PS[:, 7, :].rearrange("p (q v s c) -> p v s q c", q=QT * GH, v=2, s=2)
                        q = qhg[:, g].rearrange("p t (j c) -> p (t j) c", j=GH)
                        dve.tensor_tensor(pk[:, k], pt[:, 0], q.unsqueeze(1).to_broadcast([P, 2, QT * GH, HD]), ALU.mult)
                        dve.tensor_copy(vv[g % 2][:, k], pt[:, 1]).then_inc(s["pt_used"], 1)
                        if k == NK - 1:
                            dve.wait_ge(s["pt_used"], m + 1)
                            weigh(g)
                weights(NG - 1)
                combine_last()
                if prev:
                    costs(c, slot, 1)
                    split_keys(c)
                else:
                    for n, (high, low, raw) in enumerate(((wg0h, wg0l, wg0r), (wu0h, wu0l, wu0r))):
                        dve.wait_ge(experts0_split, n + 1)
                        dve.tensor_tensor(low[:], raw[:], high[:].bitcast(F32), ALU.subtract).then_inc(experts0_low, 1)
                dve.wait_ge(s["y_ps"], 1)
                c.tick(dve.tensor_tensor(XX[:, 0:QT], XI[:], PS[:, 1, :].rearrange("p (t d) -> p t d", t=QT), ALU.add))
                c.settle()
                dve.sem_inc(s["residual_made"], 1)

            def route(c):
                dve.wait_ge(s["score_in"], 1)
                c.link(dve.tensor_tensor(rbi[:], rsc[:], eb0[:].unsqueeze(1).to_broadcast([P, QT, E0]), ALU.add))
                for t in range(QT):
                    last = dve.max(rmx[:, t, :], rbi[:, t, :])
                c.link(last)
                for t in range(QT):
                    last = dve.max_index(rix[:, t, :], rmx[:, t, :], rbi[:, t, :])
                c.link(last)
                c.link(dve.tensor_copy(rif[:], rix[:]))
                for t in range(QT):
                    last = dve.tensor_tensor(roh[:, t], erow[:].unsqueeze(1).to_broadcast([P, K0, E0]),
                                             rif[:, t, 0:K0].unsqueeze(2).to_broadcast([P, K0, E0]), ALU.is_equal)
                c.link(last)
                c.link(dve.reduce_sum(rms[:], roh[:].rearrange("p t k e -> p t e k"), AX_X))
                c.link(dve.tensor_tensor(rms[:], rms[:], rsc[:], ALU.mult))
                c.link(dve.reduce_sum(rsum[:, :, 0], rms[:], AX_X))
                c.link(dve.reciprocal(rsum[:, :, 1], rsum[:, :, 0]))
                c.link(dve.tensor_tensor(rcm[:], rms[:], rsum[:, :, 1:2].to_broadcast([P, QT, E0]), ALU.mult))
                c.link(dve.tensor_copy(cb3[:, :, 0, :], rcm[:]))
                c.link(dve.tensor_tensor(rbi[:], rcm[:], cb3[:, :, 0, :], ALU.subtract))
                c.link(dve.tensor_copy(cb3[:, :, 1, :], rbi[:]))
                dve.tensor_tensor(cb3[:, :, 2, :], rbi[:], cb3[:, :, 1, :], ALU.subtract).then_inc(s["cb3_ready"], 1)

            def split_keys(c):
                dve.wait_ge(s["k1_ev"], NG)
                for j in range(GH):
                    r = slice(32 * j, 32 * j + 32)
                    dve.scalar_tensor_tensor(out=Kbd[r, :, j, 0:M], in0=khi[r].bitcast(F32), scalar=pcol[r, 4:5],
                                             in1=ktmp[r], op0=ALU.mult, op1=ALU.add)
                    last = dve.scalar_tensor_tensor(out=Kb2[r, :, 32 * j:32 * j + M - P], in0=khi[r, :, P:M].bitcast(F32),
                                                    scalar=pcol[r, 4:5], in1=ktmp[r, :, P:M], op0=ALU.mult, op1=ALU.add)
                last.then_inc(s["kbd_ready"], 1)

            def attend(c, j):
                for n, (kind, g, t) in enumerate(MAX_UNITS):
                    if MX_SLOT + n // MX_PER != j:
                        continue
                    bank = 4 + 2 * (n % 2)
                    dve.wait_ge(s["mx_ps"], n + 1)
                    if kind == "turn":
                        dve.tensor_tensor(qf[:, g, :], qf[:, g, :].bitcast(F32), PS[:, bank, :], ALU.add).then_inc(s["mx_used"], 1)
                        continue
                    src = PS[:, bank:bank + 2, :].rearrange("p a (j m) -> p (a j) m", j=2)[:, :, 0:M]
                    dve.reduce_max(nmx[:, t, :], src, AX_X).then_inc(s["mx_used"], 1)
                    if t == QT - 1:
                        dve.wait_ge(s["mx_used"], n + 1)
                        nm = NMp[:, g % 2].rearrange("p t (j c) -> p t j c", j=GH)
                        c.link(dve.tensor_scalar(nmh[:], nmx[:], -1.0, None, ALU.mult))
                        dve.tensor_copy(nm[:, :, :, 24], nmh[:].bitcast(F32))
                        dve.scalar_tensor_tensor(out=nm[:, :, :, 25], in0=nmx[:], scalar=-1.0, in1=nmh[:].bitcast(F32),
                                                 op0=ALU.mult, op1=ALU.subtract).then_inc(s["nm_ready"], 1)
                        dve.wait_ge(s["nm_ready"], g + 1)
                g, part = (j - S_SLOT) // 3, (j - S_SLOT) % 3
                if j > S_SLOT and part == 0 and g <= NG:
                    m = g - 1
                    dve.wait_ge(s["ott_ps"], m + 1)
                    pt = PS[:, 4, :].rearrange("p (t j c) -> p t j c", t=QT, j=GH)
                    c.link(dve.reciprocal(rden[:], pt[:, :, :, HD]))
                    av = att[:, :, m * GH * HD:(m + 1) * GH * HD].rearrange("p t (j c) -> p t j c", j=GH)
                    for t in range(QT):
                        last = dve.tensor_tensor(av[:, t], pt[:, t, :, 0:HD],
                                                 rden[:, t, :].unsqueeze(2).to_broadcast([P, GH, HD]), ALU.mult)
                    last.then_inc(s["att_step"], 1)
                if j >= S_SLOT and part == 2 and g < NG:
                    dve.wait_ge(s["ot_ps"], g + 1)
                    if g >= 1:
                        dve.wait_ge(s["ott_ps"], g)
                    dve.tensor_copy(ots[:], PS[:, 5, :]).then_inc(s["ot_ev"], 1)

            def batch(b, prev, more=True):
                c = Steps(dve, s["dve_step"])

                norms = 4 if prev else 1

                def between(j):
                    if prev:
                        attend(c, j)
                    if more:
                        prepare(c, j, norms)

                sampling(c, prev, b - 1)
                norm_stats(c, XX, range(QT))
                norm_apply(c, XX, xn, range(QT), norms).then_inc(s["xn_ready"], 1)
                dve.wait_ge(s["xhi_ready"], 1)
                dve.tensor_tensor(xlo[:], PS[:, 0, :], xhi[:].bitcast(F32), ALU.subtract).then_inc(s["xlo_ready"], 1)
                route(c)
                if prev:
                    attend(c, -1)
                dve_ffn(dve, C0, between)
                dve.wait_ge(s["yt_ps"], 1)
                if prev:
                    dve.wait_ge(s["kept"], 1)
                c.link(dve.tensor_tensor(XX[:, QT:], XX[:, 0:QT], PS[:, 0, :].rearrange("p (t d) -> p t d", t=QT), ALU.add))
                finish_turn(dve, "dve")

            c = Steps(dve, s["dve_step"])
            for j in range(C0):
                prepare(c, j, 0)
            finish_turn(dve, "dve")
            dve.wait_ge(late_consts_in, 16 * N_LATE)
            batch(0, False)
            with dve.Fori(1, B - 1) as b:
                batch(b, True)
            batch(B - 1, True, False)
            c = Steps(dve, s["dve_step"])
            norm_stats(c, XX, range(QT, 2 * QT))
            norm_apply(c, XX, xn, range(QT, 2 * QT), 1).then_inc(s["xn_ready"], 1)
            norm_stats(c, att, range(QT))
            attention_normed(c, 2)
            split_keys(c)
            residual_stats(c, B - 1, 1)
            residual_normed(c, B - 1, 3)
            costs(c, B - 1, 1)
            for j in range(-1, S_SLOT + 3 * NG + 1):
                attend(c, j)
            c.settle()
            dve.wait_ge(s["att_step"], NG)
            norm_stats(c, att, range(QT))
            attention_normed(c, 4)
            residual_stats(c, 0, 2)
            residual_normed(c, 0, 5)
            costs(c, 0, 2)
            finish_turn(dve, "dve")

            c = Steps(dve, sk_dve)
            c.tick(dve.memset(onesm[:], 1.0))
            c.tick(dve.memset(scol[:, 2:4, :], 0.0))
            c.link(dve.tensor_copy(sT[:], CST[:]))
            m, rowsum, v, logsum = srow[:, 0, :], srow[:, 1, :], scol[:, 3, :], scol[:, 2, :]
            over_experts = lambda x: x.unsqueeze(2).to_broadcast([P, NT, E1])
            over_tokens = lambda x: x.unsqueeze(1).to_broadcast([P, NT, E1])
            for it in range(SINK):
                if it >= 1:
                    dve.wait_ge(sk_col_ln, it)
                c.link(dve.tensor_tensor(sR[:], sT[:], over_tokens(logsum), ALU.subtract))
                if it >= 1:
                    c.tick(dve.tensor_tensor(v, v, logsum, ALU.add))
                c.link(dve.reduce_max(m, sR[:], AX_X))
                dve.tensor_tensor(sR[:], sR[:], over_experts(m), ALU.subtract).then_inc(sk_row_in, 1)
                dve.wait_ge(sk_row_in, it + 1)
                dve.reduce_max(scol[:, 0, :], sR[:].rearrange("p t e -> p e t"), AX_X).then_inc(sk_part_max, 1)
                dve.wait_ge(sk_turned, it + 1)
                dve.reduce_max(smx[:], PS[0:E1, 0, 0:P], AX_X).then_inc(sk_col_max, 1)
                dve.wait_ge(sk_row_exp, it + 1)
                c.link(dve.reduce_sum(rowsum, sE[:], AX_X))
                if it == SINK - 1:
                    dve.sem_inc(sk_row_sum, 1)
                c.tick(dve.reciprocal(srow[:, 3, :], rowsum))
                dve.wait_ge(sk_col_spread, it + 1)
                dve.tensor_tensor(sQ[:], sR[:], over_tokens(PS[:, 1, 0:E1]), ALU.subtract).then_inc(sk_col_in, 1)
                c.link(dve.tensor_tensor(v, v, PS[:, 1, 0:E1], ALU.add))
                c.tick(dve.tensor_tensor(sT[:], CST[:], over_tokens(v), ALU.subtract))
                dve.wait_ge(sk_col_exp, it + 1)
                c.link(dve.tensor_tensor(sG[:], sG[:], over_experts(srow[:, 3, :]), ALU.mult))
                dve.reduce_sum(scol[:, 1, :], sG[:].rearrange("p t e -> p e t"), AX_X).then_inc(sk_part_sum, 1)
            dve.wait_ge(sk_row_ln, 1)
            c.link(dve.tensor_tensor(sQ[:], sQ[:], over_experts(srow[:, 2, :]), ALU.subtract))
            dve.wait_ge(sk_col_ln, SINK)
            c.link(dve.tensor_tensor(sR[:], sQ[:], over_tokens(logsum), ALU.subtract))
            dve.sem_inc(sk_row_in, 1)
            c.link(dve.tensor_scalar(rank[:], sR[:], EXP_FLOOR, None, ALU.is_ge))
            dve.wait_ge(sk_row_exp, SINK + 1)
            c.link(dve.tensor_tensor(sE[:], sE[:], rank[:], ALU.mult))
            for t in range(NT):
                mine = sE[:, t, :].unsqueeze(2).to_broadcast([P, E1, E1])
                other = sE[:, t, :].unsqueeze(1).to_broadcast([P, E1, E1])
                dve.tensor_tensor(rk1[:, t], other, mine, ALU.is_gt)
                last = dve.tensor_tensor(rk2[:, t], other, mine, ALU.is_ge)
            c.link(last)
            r1 = rk1[:].rearrange("p t a b -> p t (a b)")
            r2 = rk2[:].rearrange("p t a b -> p t (a b)")
            c.link(dve.tensor_tensor(r2, r2, r1, ALU.subtract))
            c.link(dve.tensor_tensor(r2, r2, lower[:].unsqueeze(1).to_broadcast([P, NT, E1 * E1]), ALU.mult))
            c.link(dve.tensor_tensor(r2, r2, r1, ALU.add))
            c.link(dve.reduce_sum(rank[:], rk2[:], AX_X))
            c.tick(dve.tensor_scalar(sR[:], rank[:], 0.0, None, ALU.is_equal))
            c.tick(dve.memset(w3[:], 0.0))
            c.link(dve.tensor_scalar(rank[:], rank[:], 1.0, None, ALU.is_equal))
            c.link(dve.tensor_tensor(sR[:], sR[:], sE[:, :, 0:1].to_broadcast([P, NT, E1]), ALU.mult))
            c.link(dve.tensor_tensor(rank[:], rank[:], sE[:, :, 1:2].to_broadcast([P, NT, E1]), ALU.mult))
            c.link(dve.tensor_tensor(sR[:], sR[:], rank[:], ALU.add))
            c.link(dve.tensor_copy(w3[:, :, 0, 0:E1], sR[:]))
            c.link(dve.tensor_tensor(sR[:], sR[:], w3[:, :, 0, 0:E1], ALU.subtract))
            c.link(dve.tensor_copy(w3[:, :, 1, 0:E1], sR[:]))
            dve.tensor_tensor(w3[:, :, 2, 0:E1], sR[:], w3[:, :, 1, 0:E1], ALU.subtract).then_inc(w3_ready, 1)

            def add_residual(b, i):
                dve.wait_ge(s["yt_ps"], i + 1)
                dve.tensor_tensor(XX[:, i * QT:(i + 1) * QT], XR[:, bass.ds(SLOT(b, i) * QT, QT), :],
                                  PS[:, 5, :].rearrange("p (t d) -> p t d", t=QT), ALU.add).then_inc(s["x_sum"], 1)

            with dve.Fori(0, B // 2) as b:
                for n in range(2 * C1):
                    dve.wait_ge(s["sg_ready"], n + 1)
                    dve.wait_ge(s["gu_ps"], n + 1)
                    dve.tensor_tensor(sg[:, n % 2, :], sg[:, n % 2, :], PS[:, 1, :], ALU.mult).then_inc(s["h_used"], 1)
                    dve.wait_ge(s["h_used"], n + 1)
                    if n >= 2:
                        dve.wait_ge(s["hlo_ready"], n - 1)
                    dve.tensor_tensor(hh[:, n % 2, :], sg[:, n % 2, :], PS[:, 2, :], ALU.mult).then_inc(s["h_ready"], 1)
                    if n == C1 + 5:
                        add_residual(b, 0)
                add_residual(b, 1)
                finish_turn(dve, "dve")

        def pe_ffn(pe, chunks, wgh, wgl, wuh, wul, wd, turn_weights, between):
            def down(j):
                pe.wait_ge(s["h_ready"], j + 1)
                pe.matmul(PS[:, 3, :], wd[:, j, :], hh[:, j % 2, :], start=(j == 0), stop=(j == chunks - 1),
                          skip_group_check=True).then_inc(s["d_ps"], 1)

            for j in range(chunks):
                cs = slice(j * P, (j + 1) * P)
                if j >= 1:
                    pe.wait_ge(s["sg_ready"], j)
                for n, (w, x) in enumerate(((wgh, xhi), (wgh, xlo), (wgl, xhi))):
                    last = pe.matmul(PS[:, 0, :], w[:, cs], x[:], start=(n == 0), stop=(n == 2))
                last.then_inc(s["g_in"], 1)
                if j >= 1:
                    pe.wait_ge(s["h_used"], j)
                for n, (w, x) in enumerate(((wuh, xhi), (wuh, xlo), (wul, xhi))):
                    last = pe.matmul(PS[:, 1, :], w[:, cs], x[:], start=(n == 0), stop=(n == 2))
                if j == 0:
                    turn_weights()
                if j >= 1:
                    pe.wait_ge(s["h_ready"], j)
                for i in range(GH):
                    e = (GH * j + i) // (I0 // 32)
                    last = pe.matmul(PS[32 * i:32 * i + 32, 2, :], ident3b[:, e:e + 1].to_broadcast([96, 32]),
                                     cbT[:], start=True, stop=True)
                last.then_inc(s["gu_ps"], 1)
                if j >= 1:
                    down(j - 1)
                between(j)
            down(chunks - 1)
            pe.wait_ge(s["d_ps"], chunks)
            pe.sem_inc(s["acc_ps"], 1)
            pe.wait_ge(s["yT_ready"], 1)
            for t in range(QT):
                last = pe.transpose(PS[:, 0, t * P:(t + 1) * P], yT[:, t * P:(t + 1) * P], ident[:])
            last.then_inc(s["yt_ps"], 1)

        @block.tensor
        def _(pe):
            pe.wait_ge(consts_in, 16 * N_CONSTS)
            pe.wait_ge(consts_made, 1)

            def turn(norms, t0, bank):
                pe.wait_ge(s["xn_ready"], norms)
                for t in range(QT):
                    last = pe.transpose(PS[:, bank, t * P:(t + 1) * P], xn[:, t0 + t, :], ident[:])
                last.then_inc(s["xnT_ps"], 1)

            def prepare_waits(j, turns):
                if j == TURN_SLOT + 1:
                    pe.wait_ge(s["xnT_ready"], turns + 1)
                if j == QT_SLOT + 1:
                    pe.wait_ge(s["qhg_ready"], 1)
                for i in range(2):
                    if j == TABLE_SLOTS[i] + 1:
                        pe.wait_ge(s["tab_f"], 2 * i + 2)
                if j == DX_SLOT + 1:
                    pe.wait_ge(s["dxg_ready"], 1)

            def prepare(j, norms, turns, prev):
                if j == TURN_SLOT:
                    if prev:
                        pe.wait_ge(s["mx_used"], len(MAX_UNITS))
                    turn(norms + 1, 0, 4)
                if j == Q_SLOT:
                    if prev:
                        pe.wait_ge(s["att_step"], 1)
                    pe.matmul(PS[:, 4, :], wq0[:], xnT[:], start=True, stop=True).then_inc(s["q_ps"], 1)
                if j == QT_SLOT:
                    pe.wait_ge(s["qT_ready"], 1)
                    for t in range(QT):
                        o = PS[:, 4, t * P:(t + 1) * P]
                        pe.matmul(o, xnT[:, t * P:(t + 1) * P], wq0[:], start=True, stop=False)
                        last = pe.matmul(o, onerow[:], bq0[:], start=False, stop=True)
                    last.then_inc(s["q_ps"], 1)
                if j == OFF_SLOT:
                    if prev:
                        pe.wait_ge(s["att_step"], 2)
                    pe.matmul(PS[0:HK, 4, :], woff[:], qT[:], start=True, stop=True).then_inc(s["off_ps"], 1)
                for i, ch in enumerate((1, 0)):
                    if j == TABLE_SLOTS[i]:
                        if i == 0:
                            pe.wait_ge(s["off_read"], 1)
                            pe.wait_ge(s["tails"], 2)
                        elif prev:
                            pe.wait_ge(s["att_step"], 3)
                        else:
                            pe.wait_ge(s["tab_f"], 2)
                        for n in range(2):
                            rows = cpad[:, n:n + P] if ch == 0 else ctail[:, n, :]
                            there = vrow[:, n:n + P] if ch == 0 else vtail[:, n, :]
                            o = PS[:, 4, n * 2 * D:(n + 1) * 2 * D]
                            pe.matmul(o, rows, wkv[:], start=True, stop=False)
                            last = pe.matmul(o, there, bkv[:], start=False, stop=True)
                        last.then_inc(s["tab_ps"], 1)
                if j == DX_SLOT:
                    if prev:
                        pe.wait_ge(s["att_step"], 4)
                    pe.wait_ge(s["off_ready"], 1)
                    for t in range(QT):
                        last = pe.transpose(PS[:, 4, t * HK:(t + 1) * HK], dxf[:, t * P:(t + 1) * P], ident[0:HK, 0:HK])
                    last.then_inc(s["dxT_ps"], 1)

            def sampling(prev):
                for n in range(NG * NK + 2):
                    if n == NG * NK + 1 and prev:
                        pe.wait_ge(s["ev_b"], NG * NK)
                        keys()
                        pe.wait_ge(s["oh_c"], NG * NK)
                        turn(1, QT, 4)
                        turn(2, 0, 0)
                    if n < NG * NK:
                        g, k = n // NK, n % NK
                        row = lambda j: (GH * g + j) * NK + k
                        if n >= 1:
                            pe.wait_ge(s["ev_a"], n)
                        for j in range(2):
                            last = pe.matmul(PS[:, j, :], identb[0:HK, row(j):row(j) + 1].to_broadcast([HK, P]), ibf[:],
                                             start=True, stop=True)
                        last.then_inc(s["bc_a"], 1)
                        if n >= 1:
                            pe.wait_ge(s["ev_b"], n)
                        for j in range(2, 4):
                            last = pe.matmul(PS[:, j, :], identb[0:HK, row(j):row(j) + 1].to_broadcast([HK, P]), ibf[:],
                                             start=True, stop=True)
                        last.then_inc(s["bc_b"], 1)
                        if n >= 1:
                            pe.wait_ge(s["oh_c"], n)
                        for j in range(4):
                            last = pe.matmul(PS[32 * j:32 * j + 32, 4, :],
                                             identb[0:HK, row(j):row(j) + 1].to_broadcast([HK, 32]), ibf[:],
                                             start=True, stop=True)
                        last.then_inc(s["bc_c"], 1)
                    if 1 <= n <= NG * NK:
                        m = n - 1
                        g = m // NK
                        o = PS[:, 5 + m % 2, :]
                        if m >= 2:
                            pe.wait_ge(s["g_ev"], m - 1)
                        pe.wait_ge(s["oh_c"], m + 1)
                        for p in range(3):
                            pe.matmul(o, T2[:, p, g, :], oh2[:, m % 2, :], start=(p == 0), stop=False, skip_group_check=True)
                        pe.wait_ge(s["oh_a"], m + 1)
                        pe.wait_ge(s["oh_b"], m + 1)
                        for p in range(3):
                            for j in range(GH):
                                h = GH * g + j
                                last = pe.matmul(o[32 * j:32 * j + 32, :], T1[:, p, 0, 32 * h:32 * h + 32], oh1[:, m % 2, j, :],
                                                 start=False, stop=(p == 2), skip_group_check=True)
                        last.then_inc(s["g_ps"], 1)
                    if n >= 2:
                        m = n - 2
                        pe.wait_ge(s["g_ev"], m + 1)
                        if m >= 1:
                            pe.wait_ge(s["pt_used"], m)
                        for t in range(QT):
                            last = pe.transpose(PS[:, 7, t * P:(t + 1) * P], gs[:, m % 2, t * P:(t + 1) * P], ident[:])
                        last.then_inc(s["pt_ps"], 1)

                if prev:
                    values()
                    pe.wait_ge(s["pt_used"], NG * NK)
                    queries()
                    logits(2)
                    pe.wait_ge(s["cost_read"], 1)
                pe.wait_ge(s["ctok_pool"], NG - 1)
                pe.wait_ge(s["ctok_ready"], 1)
                for t in range(QT):
                    last = pe.transpose(PS[:, 0, t * P:(t + 1) * P], ctok[:, t, :], ident[:])
                last.then_inc(s["ctxT_ps"], 1)
                pe.wait_ge(s["ctxT_ready"], 1)
                for t in range(QT):
                    o = PS[:, 1, t * P:(t + 1) * P]
                    pe.matmul(o, ctxT[:, t * P:(t + 1) * P], wo[:], start=True, stop=False)
                    last = pe.matmul(o, onerow[:], bo[:], start=False, stop=True)
                last.then_inc(s["y_ps"], 1)

            def logits(turns):
                pe.wait_ge(s["xnT_ready"], turns)
                for t in range(QT):
                    last = pe.matmul(PS[:, 1, t * E1:(t + 1) * E1], yT[:, t * P:(t + 1) * P], gw1[:], start=True, stop=True)
                last.then_inc(s["cost_out"], 1)

            def keys():
                for g in range(NG):
                    pe.matmul(PS[:, K_BANK[g], (g % 2) * 256:(g % 2) * 256 + M], wk1[:, g * P:(g + 1) * P],
                              cprev[:, 1:1 + M], start=True, stop=True).then_inc(s["k1_ps"], 1)

            def values():
                pe.wait_ge(s["tailp"], 1)
                pe.matmul(PS[:, 5, :], cprev[:, 1:1 + P], wv1[:], start=True, stop=False)
                pe.matmul(PS[:, 5, :], vrow[:, 1:1 + P], bv1[:], start=False, stop=True)
                pe.matmul(PS[:, 6, :], ctailp[:], wv1[:], start=True, stop=False)
                pe.matmul(PS[:, 6, :], vtail[:, 1, :], bv1[:], start=False, stop=True).then_inc(s["v1_ps"], 1)

            def queries():
                pe.wait_ge(s["xnT_ready"], 1)
                for g in range(NG):
                    if g == 1:
                        pe.wait_ge(s["v1_ready"], 1)
                    pe.matmul(PS[:, 4 + g, :], wq1[:, g * P:(g + 1) * P], pnT[:], start=True, stop=True).then_inc(s["q1_ps"], 1)

            def attend(j):
                for n, (kind, g, t) in enumerate(MAX_UNITS):
                    if MX_SLOT + n // MX_PER != j:
                        continue
                    bank = 4 + 2 * (n % 2)
                    if n == 0:
                        pe.wait_ge(s["kbd_ready"], 1)
                        pe.wait_ge(s["q1_ev"], NG)
                    if n >= 2:
                        pe.wait_ge(s["mx_used"], n - 1)
                    if kind == "turn":
                        pe.wait_ge(s["nm_ready"], g + 1)
                        for t in range(QT):
                            last = pe.transpose(PS[:, bank, t * P:(t + 1) * P], NMp[:, g % 2, t, :], ident[:])
                    else:
                        pe.wait_ge(s["qf_ready"], g + 1)
                        for i in range(2):
                            o = PS[:, bank + i, :].rearrange("p (j m) -> p j m", j=2)[:, :, 0:M]
                            last = pe.matmul(o, qf[:, g, t * P:(t + 1) * P], Kbd[:, g, 2 * i:2 * i + 2, 0:M],
                                             start=True, stop=True)
                    last.then_inc(s["mx_ps"], 1)
                g, part = (j - S_SLOT) // 3, (j - S_SLOT) % 3
                if j > S_SLOT and part == 0 and g <= NG:
                    m = g - 1
                    pe.wait_ge(s["ot_ev"], m + 1)
                    for t in range(QT):
                        last = pe.transpose(PS[:, 4, t * P:(t + 1) * P], ots[:, t * P:(t + 1) * P], ident[:])
                    last.then_inc(s["ott_ps"], 1)
                if j >= S_SLOT and g < NG and part == 0:
                    if g == 0:
                        pe.wait_ge(s["mx_used"], len(MAX_UNITS))
                    for h in range(2, 4):
                        last = pe.matmul(PS[:, 4 + h, :], Kbd[:, g, h, 0:P], qf[:, g, :], start=True, stop=True)
                    last.then_inc(s["s_b"], 1)
                    pe.matmul(PS[:, 5, :], Kb2[:, g, :], qf[:, g, :], start=True, stop=True).then_inc(s["s_c"], 1)
                if j >= S_SLOT and g < NG and part == 1:
                    pe.wait_ge(s["e_b"], g + 1)
                    for h in range(2):
                        last = pe.matmul(PS[:, 6 + h, :], Kbd[:, g, h, 0:P], qf[:, g, :], start=True, stop=True)
                    last.then_inc(s["s_a"], 1)
                if j >= S_SLOT and g < NG and part == 2:
                    pe.wait_ge(s["e_a"], g + 1)
                    pe.wait_ge(s["e_c"], g + 1)
                    if g == 0:
                        pe.wait_ge(s["v1_ready"], 1)
                    pe.matmul(PS[:, 5, :], V2d[:, g, :], Ex2[:], start=True, stop=False, skip_group_check=True)
                    for h in range(GH):
                        last = pe.matmul(PS[32 * h:32 * h + 32, 5, :], V1[:, g * P + 32 * h:g * P + 32 * h + 32],
                                         Ex[:, h, :], start=False, stop=True, skip_group_check=True)
                    last.then_inc(s["ot_ps"], 1)

            def batch(prev, more=True):
                norms = 3 if prev else 1

                def between(j):
                    if more:
                        prepare_waits(j, norms)
                    if prev:
                        attend(j)
                    if more:
                        prepare(j, norms, norms, prev)

                def turn_weights():
                    pe.wait_ge(s["cb3_ready"], 1)
                    turned = PS[0:96, 3, :].bitcast(BF16)
                    for t in range(QT):
                        last = pe.transpose(turned[:, t * P:(t + 1) * P], cb3[:, t].rearrange("p a e -> p (a e)"), identb[:])
                    last.then_inc(s["cbT_ps"], 1)
                    pe.wait_ge(s["cbT_ready"], 1)

                sampling(prev)
                turn(norms, 0, 0)
                pe.wait_ge(s["xnT_ready"], norms)
                for t in range(QT):
                    last = pe.matmul(PS[:, 1, t * E0:(t + 1) * E0], xnT[:, t * P:(t + 1) * P], gw0[:], start=True, stop=True)
                last.then_inc(s["lg_ps"], 1)
                if prev:
                    attend(-1)
                    pe.wait_ge(s["k1_ev"], NG)
                pe.wait_ge(s["score_in"], 1)
                pe.wait_ge(s["xlo_ready"], 1)
                if prev:
                    pe.sem_inc(s["prev_used"], 1)
                else:
                    pe.wait_ge(consts_made, 2)
                    pe.wait_ge(experts0_low, 2)
                    pe.wait_ge(experts0_in, 48)
                pe_ffn(pe, C0, wg0h, wg0l, wu0h, wu0l, wd0, turn_weights, between)
                finish_turn(pe, "pe")

            for j in range(C0):
                prepare_waits(j, 0)
                prepare(j, 0, 0, False)
            finish_turn(pe, "pe")
            pe.wait_ge(late_consts_in, 16 * N_LATE)
            batch(False)
            with pe.Fori(1, B - 1) as b:
                batch(True)
            batch(True, False)
            keys()
            turn(1, QT, 4)
            values()
            queries()
            turn(2, 0, 0)
            logits(2)
            for j in range(-1, S_SLOT + 3 * NG + 1):
                attend(j)
            pe.wait_ge(s["cost_read"], 1)
            turn(3, 0, 0)
            logits(3)
            finish_turn(pe, "pe")

            for it in range(SINK):
                pe.wait_ge(sk_part_max, it + 1)
                pe.transpose(PS[0:E1, 0, 0:P], scol[:, 0, :], ident[:]).then_inc(sk_turned, 1)
                pe.wait_ge(sk_col_max, it + 1)
                pe.matmul(PS[:, 1, 0:E1], smx[:].to_broadcast([E1, P]), ident[0:E1, 0:E1], start=True, stop=True)\
                  .then_inc(sk_col_spread, 1)
                pe.wait_ge(sk_part_sum, it + 1)
                pe.matmul(PS[:, 2, 0:E1], onesm[:], scol[:, 1, :], start=True, stop=True).then_inc(sk_col_sum, 1)
            pe.wait_ge(w3_ready, 1)
            for b in range(B):
                turned = PS[0:96, 3 + b, :].bitcast(BF16)
                for t in range(QT):
                    last = pe.transpose(turned[:, t * P:(t + 1) * P], w3[:, b * QT + t].rearrange("p a e -> p (a e)"), identb[:])
                last.then_inc(w3_ps, 1)
            pe.wait_ge(w3_used, B)
            pe.wait_ge(experts1_in, 48)
            pe.wait_ge(experts1_split, 4)
            pe.wait_ge(x_split, 2)

            def down(n):
                i, j = n // C1, n % C1
                pe.wait_ge(s["hlo_ready"], n + 1)
                if n == 2 * C1 - 1:
                    pe.wait_ge(s["yT_ready"], 1)
                for m, (w, h) in enumerate(((wd1h, hhi), (wd1h, hlo), (wd1l, hhi))):
                    last = pe.matmul(PS[:, 3 + i, :], w[:, j, :], h[:, n % 3, :], start=(j == 0 and m == 0),
                                     stop=(j == C1 - 1 and m == 2), skip_group_check=True)
                last.then_inc(s["d_ps"], 1)

            def turn_result(i):
                pe.wait_ge(s["yT_ready"], i + 1)
                if i:
                    pe.wait_ge(s["x_sum"], i)
                for t in range(QT):
                    last = pe.transpose(PS[:, 5, t * P:(t + 1) * P], yT[:, t * P:(t + 1) * P], ident[:])
                last.then_inc(s["yt_ps"], 1)

            with pe.Fori(0, B // 2) as b:
                for n in range(2 * C1):
                    i, j = n // C1, n % C1
                    cs = slice(j * P, (j + 1) * P)
                    rows = bass.ds(SLOT(b, i) * S, S)
                    if n >= 1:
                        pe.wait_ge(s["sg_ready"], n)
                    for m, (w, x) in enumerate(((wg1h, xhall), (wg1h, xlall), (wg1l, xhall))):
                        last = pe.matmul(PS[:, 0, :], w[:, cs], x[:, rows], start=(m == 0), stop=(m == 2))
                    last.then_inc(s["g_in"], 1)
                    if n >= 1:
                        pe.wait_ge(s["h_used"], n)
                    for m, (w, x) in enumerate(((wu1h, xhall), (wu1h, xlall), (wu1l, xhall))):
                        last = pe.matmul(PS[:, 1, :], w[:, cs], x[:, rows], start=(m == 0), stop=(m == 2))
                    if j % (C1 // E1) == 0:
                        if n >= 1:
                            pe.wait_ge(s["h_ready"], n)
                        e = j // (C1 // E1)
                        last = pe.matmul(PS[:, 2, :], ident3b[:, e:e + 1].to_broadcast([96, P]),
                                         wTall[:, rows], start=True, stop=True)
                    last.then_inc(s["gu_ps"], 1)
                    if n >= 2:
                        down(n - 2)
                    if n == C1 + 4:
                        turn_result(0)
                down(2 * C1 - 2)
                down(2 * C1 - 1)
                turn_result(1)
                finish_turn(pe, "pe")


N_CONSTS, N_LATE = 12, 15
K_BANK = [3, 3, 2, 2]
MX_SLOT, MX_PER, S_SLOT = -1, 3, 6
NORM_SLOT, TURN_SLOT, Q_SLOT, QT_SLOT, OFF_SLOT, TABLE_SLOTS, DX_SLOT = 6, 8, 10, 11, 13, (14, 16), 19
DEVIATIONS = (1, 4, 11)
SLOT = lambda b, i: 3 - 3 * b if i else 1 + b
MAX_UNITS = []
for _g in range(NG):
    MAX_UNITS += [("max", _g, 0), ("max", _g, 1)]
    if _g >= 1:
        MAX_UNITS.append(("turn", _g - 1, 0))
    MAX_UNITS += [("max", _g, 2), ("max", _g, 3)]
MAX_UNITS.append(("turn", NG - 1, 0))
_OUTS = [((B, S, D), "float32")]


def _layout(x, ctx_1024, mask_BxS2_if0, **w):
    import numpy as np
    f = np.float32

    def padded(m, slots, tail=()):
        fill = np.zeros(m.shape[:-1] + (32 - slots * HD,), f)
        fill[..., :len(tail)] = tail
        return np.concatenate([m] * slots + [fill], -1).reshape(m.shape[:-2] + (H * 32,))

    a = {}
    p = np.arange(P)
    a["ident"] = np.eye(P, dtype=f)
    a["ident3"] = np.tile(np.eye(32, dtype=f), (3, 1))
    slot = (p % 32) // HD
    pc = np.zeros((P, 8), f)
    pc[:, 0] = p
    pc[:, 1] = P + p % 32
    pc[:, 2] = p % NK - (NK + 1) // 2
    pc[:, 3] = -(slot == 1).astype(f)
    pc[:, 4] = -(slot == 2).astype(f)
    a["pcol"] = pc
    a["locrow"] = np.tile(np.arange(S, dtype=f), (HK, 1))
    a["erow"] = np.tile(np.arange(32, dtype=f), (P, 1))
    a["lower"] = np.tile(np.tril(np.ones((E1, E1), f), -1).reshape(1, -1), (P, 1))
    a["onerow"] = np.ones((1, P), f)
    v = np.zeros((1, CW), f)
    v[:, 1:1 + M] = 1
    a["vrow"] = v
    a["vtail"] = np.stack([np.tile(v[:, P + n:P + n + 32], (1, GH)) for n in range(2)], 1)
    a["wkv"] = np.concatenate([w["L0_xattn_Wk"].T, w["L0_xattn_Wv"].T], 1)
    a["wq0"] = w["L0_xattn_Wq"].T
    a["woff"] = w["L0_xattn_Woff"].T
    a["wo"] = w["L0_xattn_Wo"].T
    a["bkv"] = np.concatenate([w["L0_xattn_bk"], w["L0_xattn_bv"]])[None]
    a["bq0"] = w["L0_xattn_bq"][None]
    a["bo"] = w["L0_xattn_bo"][None]
    bc = np.zeros((P, 2), f)
    bc[:, 0] = w["L0_xattn_bq"]
    bc[:HK, 1] = w["L0_xattn_boff"]
    a["bcol"] = bc
    t = lambda m: m.transpose(1, 0, 2)
    a["wq1"] = padded(t(w["L1_xattn_Wq"]), 3)
    a["wk1"] = padded(t(w["L1_xattn_Wk"]), 3)
    a["wv1"] = padded(t(w["L1_xattn_Wv"]), 1)
    bq = padded(w["L1_xattn_bq"], 3).reshape(NG, P).T
    bk = padded(w["L1_xattn_bk"], 3, (1, 1)).reshape(NG, P).T
    a["bqk1"] = np.stack([bq, bk], 1)
    a["bv1"] = padded(w["L1_xattn_bv"], 1, (1,))[None]
    a["gamma"] = np.tile(w["L1_xattn_gamma"][None], (P, 1))
    a["beta"] = np.tile(w["L1_xattn_beta"][None], (P, 1))
    a["gw0"] = w["L0_ffn_gate_w"].T
    a["eb0"] = np.tile(w["L0_ffn_e_bias"][None], (P, 1))
    a["gw1"] = w["L1_ffn_gate_W"].T
    a["wg0"] = w["L0_ffn_w1"].transpose(1, 0, 2).reshape(D, -1)
    a["wu0"] = w["L0_ffn_w3"].transpose(1, 0, 2).reshape(D, -1)
    a["wd0"] = w["L0_ffn_w2"].reshape(C0, P, D).transpose(1, 0, 2)
    a["wg1"] = w["L1_ffn_W_gate"].reshape(-1, D).T
    a["wu1"] = w["L1_ffn_W_up"].reshape(-1, D).T
    a["wd1"] = w["L1_ffn_W_down"].transpose(0, 2, 1).reshape(C1, P, D).transpose(1, 0, 2)
    cp = np.zeros((B, D, CW), f)
    cp[:, :, 1:1 + M] = ctx_1024.transpose(0, 2, 1)
    a["ctxp"] = cp
    a["mask"] = np.repeat(mask_BxS2_if0[:, None, :], HK, 1)
    a["x"] = x
    return {k: np.ascontiguousarray(m) for k, m in a.items()}


def kernel(**inputs):
    import numpy as _np
    import concourse.bacc as _bacc
    from concourse.bass_utils import run_bass_kernel_spmd as _run

    nc = _bacc.Bacc("TRN2", target_bir_lowering=False, num_devices=1)
    arrays = _layout(**{k: _np.asarray(v) for k, v in inputs.items()})
    aps = {k: nc.dram_tensor("in_" + k, m.shape, mybir.dt.from_np(m.dtype), kind="ExternalInput").ap()
           for k, m in arrays.items()}
    out = nc.dram_tensor("out_0", _OUTS[0][0], F32, kind="ExternalOutput").ap()
    seq_kernel(nc, aps, out)
    r = _run(nc, [{"in_" + k: m for k, m in arrays.items()}], core_ids=[0])
    return r.results[0]["out_0"]
```

```python
import math
from collections import namedtuple
from contextlib import ExitStack

import concourse.bass as bass
from concourse import mybir

F32 = mybir.dt.float32
F32R = mybir.dt.float32r
BF16 = mybir.dt.bfloat16
I32 = mybir.dt.int32
U32 = mybir.dt.uint32
ALU = mybir.AluOpType
ACT = mybir.ActivationFunctionType
AX_X = mybir.AxisListType.X

P = 128
B, S, D = 4, 512, 128
M = 154
H, HD = 16, 8
NK = 5
QT = S // P
GH = 4
NG = H // GH
HK = H * NK
CW = 162
E0, I0, K0 = 32, 96, 4
E1, F1D = 8, 512
C0 = E0 * I0 // P
C1 = E1 * F1D // P
SINK = 20
EPS = 1e-5
EXP_FLOOR = -87.33654
NT = B * QT


class Steps:

    def __init__(self, eng, sem):
        self.eng, self.sem, self.n = eng, sem, 0

    def tick(self, ins):
        self.n += 1
        return ins.then_inc(self.sem, 1)

    def settle(self):
        if self.n:
            self.eng.wait_ge(self.sem, self.n)

    def link(self, ins):
        self.tick(ins)
        self.settle()


def seq_kernel(nc, a, out):
    ctx = ExitStack()
    with ctx:
        def sb(name, shape, dt=F32, where=ctx):
            return where.enter_context(nc.sbuf_tensor(name, shape, dt))

        def sem(name):
            return ctx.enter_context(nc.semaphore(name))

        PS = ctx.enter_context(nc.psum_tensor("PS", [P, 8, 512], F32))

        ident = sb("ident", [P, P])
        identb = sb("identb", [P, P], BF16)
        ident3 = sb("ident3", [3 * 32, 32])
        ident3b = sb("ident3b", [3 * 32, 32], BF16)
        pcol = sb("pcol", [P, 8])
        locrow = sb("locrow", [HK, S])
        erow = sb("erow", [P, 32])
        lower = sb("lower", [P, E1 * E1])
        onerow = sb("onerow", [1, P])
        vrow = sb("vrow", [1, CW])
        vtail = sb("vtail", [1, 2, P])
        wkv = sb("wkv", [D, 2 * D])
        wq0 = sb("wq0", [D, D])
        woff = sb("woff", [D, HK])
        wo = sb("wo", [D, D])
        bkv = sb("bkv", [1, 2 * D])
        bq0 = sb("bq0", [1, D])
        bo = sb("bo", [P, D])
        bcol = sb("bcol", [P, 2])
        wq1 = sb("wq1", [D, NG * P])
        wk1 = sb("wk1", [D, NG * P])
        wv1 = sb("wv1", [D, NG * P])
        bqk1 = sb("bqk1", [P, 2, NG])
        bv1 = sb("bv1", [1, NG * P])
        gamma = sb("gamma", [P, D])
        beta = sb("beta", [P, D])
        gw0 = sb("gw0", [D, E0])
        eb0 = sb("eb0", [P, E0])
        gw1 = sb("gw1", [D, E1])

        XR = sb("XR", [P, NT, D])
        with ExitStack() as raw_ctx:
            XT3 = sb("XT3", [D, B * S], F32, raw_ctx)
        xlall = sb("xlall", [D, B * S], F32R)
        CST = sb("CST", [P, NT, E1])

        XI = sb("XI", [P, QT, D])
        XX = sb("XX", [P, 2 * QT, D])
        xn = sb("xn", [P, 2 * QT, D])
        xnT = sb("xnT", [D, S])
        pnT = sb("pnT", [D, S])
        xhi = sb("xhi", [D, S], F32R)
        xlo = sb("xlo", [D, S], F32R)
        cbT = sb("cbT", [3 * 32, S], BF16)
        with ExitStack() as vv_ctx:
            vv1 = sb("vv1", [P, NK, 2, QT * GH, HD], F32, vv_ctx)
        sg = sb("sg", [P, 2, S])
        hh = sb("hh", [P, 2, S])
        yT = sb("yT", [D, S])
        st = sb("st", [P, 2 * QT, 6])
        mv = sb("mv", [P, 2 * QT, 2])
        var = sb("var", [P, 2 * QT])
        std = sb("std", [P, 2 * QT])
        rstd = sb("rstd", [P, 2 * QT])

        loop_ctx = ExitStack()
        lsb = lambda name, shape, dt=F32: sb(name, shape, dt, loop_ctx)
        wg0h = lsb("wg0h", [D, C0 * P], F32R)
        wu0h = lsb("wu0h", [D, C0 * P], F32R)
        with ExitStack() as raw_ctx:
            wg0r = sb("wg0r", [D, C0 * P], F32, raw_ctx)
            wu0r = sb("wu0r", [D, C0 * P], F32, raw_ctx)
        wg0l = lsb("wg0l", [D, C0 * P], F32R)
        wu0l = lsb("wu0l", [D, C0 * P], F32R)
        wd0 = lsb("wd0", [P, C0, D])
        cpad = lsb("cpad", [D, CW])
        cprev = lsb("cprev", [D, CW])
        ctailp = lsb("ctailp", [D, P])
        ctail = lsb("ctail", [D, 2, P])
        mski = lsb("mski", [HK, M], I32)
        mskf = lsb("mskf", [HK, M])
        len3 = lsb("len3", [HK, 4])
        T1 = lsb("T1", [P, 3, 2, H * 32], BF16)
        T2 = lsb("T2", [P, 3, NG, P], BF16)
        Kbd = lsb("Kbd", [P, NG, GH, 160], F32R)
        Kb2 = lsb("Kb2", [P, NG, P], F32R)
        V2d = lsb("V2d", [P, NG, P])
        NMp = lsb("NMp", [P, 2, QT, P])
        V1 = lsb("V1", [P, NG * P])

        att = lsb("att", [P, QT, D])

        a_ctx = ExitStack()
        asb = lambda name, shape, dt=F32: sb(name, shape, dt, a_ctx)
        qT = asb("qT", [D, S])
        v0 = asb("v0", [HK, S])
        v1 = asb("v1", [HK, S])
        vi = asb("vi", [HK, S], I32)
        dxf = asb("dxf", [HK, S])
        ibf = asb("ibf", [HK, S], BF16)
        cbc = asb("cbc", [P, GH, S], BF16)
        oh1 = asb("oh1", [P, 2, GH, S], BF16)
        oh2 = asb("oh2", [P, 2, S], BF16)
        gs = asb("gs", [P, 2, S])
        qhg = asb("qhg", [P, NG, QT, GH * HD])
        dxg = asb("dxg", [P, NG, NK, QT * GH])
        tabf, tabr = xnT, qT
        pk = asb("pk", [P, NK, 2, QT * GH, HD])
        vv0 = asb("vv0", [P, NK, 2, QT * GH, HD])
        pkr = asb("pkr", [P, NK, 2, QT * GH])
        sc = asb("sc", [P, NK, QT * GH])
        ee = asb("ee", [P, NK, QT * GH])
        coef = asb("coef", [P, 2, NK, 2, QT * GH])
        sm = asb("sm", [P, 3, QT * GH])
        ctok = asb("ctok", [P, QT, D])
        ctxT = yT
        vv = (vv0, vv1)
        a_ctx.close()

        c_ctx = ExitStack()
        csb = lambda name, shape, dt=F32: sb(name, shape, dt, c_ctx)
        ktmp = csb("ktmp", [P, NG, M])
        khi = csb("khi", [P, NG, M], F32R)
        qhi = csb("qhi", [P, 2, S], F32R)
        qtmp = csb("qtmp", [P, NG, S])
        qf = csb("qf", [P, NG, S], F32R)
        Ex2 = csb("Ex2", [P, S])
        ots = csb("ots", [P, S])
        rsc = csb("rsc", [P, QT, E0])
        rbi = csb("rbi", [P, QT, E0])
        rmx = csb("rmx", [P, QT, 8])
        rix = csb("rix", [P, QT, 8], U32)
        rif = csb("rif", [P, QT, 8])
        roh = csb("roh", [P, QT, K0, E0])
        rms = csb("rms", [P, QT, E0])
        rcm = csb("rcm", [P, QT, E0])
        rsum = csb("rsum", [P, QT, 2])
        cb3 = csb("cb3", [P, QT, 3, 32], BF16)
        nmx = csb("nmx", [P, QT, GH])
        nmh = csb("nmh", [P, QT, GH], F32R)
        Ex = csb("Ex", [P, GH, S])
        rden = csb("rden", [P, QT, GH])
        c_ctx.close()
        loop_ctx.close()

        f_ctx = ExitStack()
        fsb = lambda name, shape, dt=F32: sb(name, shape, dt, f_ctx)
        wg1h = fsb("wg1h", [D, WSLOTS, F1D], F32R)
        wu1h = fsb("wu1h", [D, WSLOTS, F1D], F32R)
        with ExitStack() as raw_ctx:
            wg1r = sb("wg1r", [D, WSLOTS, F1D], F32, raw_ctx)
            wu1r = sb("wu1r", [D, WSLOTS, F1D], F32, raw_ctx)
        wg1l = fsb("wg1l", [D, WSLOTS, F1D], F32R)
        wu1l = fsb("wu1l", [D, WSLOTS, F1D], F32R)
        wd1 = fsb("wd1", [P, WSLOTS, F1D // P, D])
        xhall = fsb("xhall", [D, B * S], F32R)
        tS = fsb("tS", [P, 3, S])
        gS = fsb("gS", [P, 3, S])
        hq = fsb("hq", [P, 4, S])
        yS = fsb("yS", [D, N_STORED + 4, S])
        sR = fsb("sR", [P, NT, E1])
        sE = fsb("sE", [P, NT, E1])
        sG = fsb("sG", [P, NT, E1])
        sQ = fsb("sQ", [P, NT, E1])
        sT = fsb("sT", [P, NT, E1])
        srow = fsb("srow", [P, 4, NT])
        scol = fsb("scol", [P, 6, E1])
        smx = fsb("smx", [E1, 1])
        onesm = fsb("onesm", [P, P])
        rk1 = fsb("rk1", [P, NT, E1, E1])
        rk2 = fsb("rk2", [P, NT, E1, E1])
        rank = fsb("rank", [P, NT, E1])
        f_ctx.close()

        consts_in = sem("consts_in")
        late_consts_in = sem("late_consts_in")
        experts0_in = sem("experts0_in")
        setup_pool = sem("setup_pool")
        consts_made = sem("consts_made")
        experts0_split = sem("experts0_split")
        experts0_low = sem("experts0_low")
        names = """next_in prev_in residual_made prev_used tails tailp tab_ps tab_f tab_split tab_ready ln_var ln_std xn_ready xnT_ps xnT_ready
            q_ps qT_ready qhg_ready off_ps off_read off_ready dxT_ps dxg_ready
            bc_a bc_b bc_c ev_a ev_b oh_a oh_b oh_c g_ps g_ev pt_ps pt_used sc_in sc_exp coef_ready vw_ready ctok_pool ctok_ready
            ctxT_ps ctxT_ready y_ps xhi_ready xlo_ready lg_ps score_in cb3_ready cbT_ps cbT_ready
            gu_ps g_in sg_ready h_used h_ready d_ps g_read t_ready p_ready up_ps y_stored y_added acc_ps yT_ready yt_ps x_sum
            q1_ps q1_ev k1_ps k1_ev v1_ps v1_ready kbd_ready qf_ready mx_ps mx_used nm_ready qn_ready cost_out x3_ready
            s_a s_b s_c e_a e_b e_c ot_ps ot_ev ott_ps att_step att_normed gamma_step cost_read kept bias_added out_in
            act_step dve_step pool_step comb_step split_step arrived""".split()
        s = {n: sem(n) for n in names}
        turn_sems = range(s[names[0]].num, s[names[-1]].num + 1)
        assert [s[n].num for n in names] == list(turn_sems)
        go = {e: sem("go_" + e) for e in ("pe", "act", "dve", "pool")}
        expert_in = [sem("expert%d_in" % e) for e in range(E1)]
        experts1_split = sem("experts1_split")
        x_split = sem("x_split")
        sk_dve = sem("sk_dve")
        sk_row_in = sem("sk_row_in")
        sk_row_exp = sem("sk_row_exp")
        sk_row_sum = sem("sk_row_sum")
        sk_row_ln = sem("sk_row_ln")
        sk_part_max = sem("sk_part_max")
        sk_turned = sem("sk_turned")
        sk_col_max = sem("sk_col_max")
        sk_col_spread = sem("sk_col_spread")
        sk_col_in = sem("sk_col_in")
        sk_col_exp = sem("sk_col_exp")
        sk_part_sum = sem("sk_part_sum")
        sk_col_sum = sem("sk_col_sum")
        sk_ones = sem("sk_ones")
        sk_log_in = sem("sk_log_in")
        sk_log_exp = sem("sk_log_exp")

        block = ctx.enter_context(nc.Block())
        INV_SQRT = 1.0 / math.sqrt(HD)

        def finish_turn(eng, name):
            eng.drain().then_inc(s["arrived"], 1)
            eng.wait_ge(go[name], 1)
            eng.sem_clear(go[name])

        @block.sync
        def _(sp):
            def load_batch(b):
                sp.dma_start(XI[:], a["x"][bass.ds(b, 1)].rearrange("a (t p) d -> p (a t) d", p=P)).then_inc(s["next_in"], 16)
                sp.dma_start(cpad[:], a["ctxp"][bass.ds(b, 1)].rearrange("a p m -> (a p) m")).then_inc(s["next_in"], 16)
                sp.dma_start(mski[:], a["mask"][bass.ds(b, 1)].rearrange("a p m -> (a p) m")).then_inc(s["next_in"], 16)

            def load_previous(b):
                sp.dma_start(cprev[:], a["ctxp"][bass.ds(b, 1)].rearrange("a p m -> (a p) m")).then_inc(s["prev_in"], 16)

            load_batch(0)
            consts = [(ident[:], a["ident"]), (wq0[:], a["wq0"]), (bq0[:], a["bq0"]), (bcol[:], a["bcol"]),
                      (onerow[:], a["onerow"]), (woff[:], a["woff"]), (pcol[:], a["pcol"]), (locrow[:], a["locrow"]),
                      (wkv[:], a["wkv"]), (bkv[:], a["bkv"]), (vrow[:], a["vrow"]), (vtail[:], a["vtail"])]
            assert len(consts) == N_CONSTS
            for dst, src in consts:
                sp.dma_start(dst, src).then_inc(consts_in, 16)
            late = [(ident3[:], a["ident3"]), (erow[:], a["erow"]), (lower[:], a["lower"]), (wo[:], a["wo"]),
                    (bo[:], a["bo"]), (wq1[:], a["wq1"]), (wk1[:], a["wk1"]), (wv1[:], a["wv1"]),
                    (bqk1[:], a["bqk1"]), (bv1[:], a["bv1"]), (gamma[:], a["gamma"]), (beta[:], a["beta"]),
                    (gw0[:], a["gw0"]), (eb0[:], a["eb0"]), (gw1[:], a["gw1"])]
            assert len(late) == N_LATE
            for dst, src in late:
                sp.dma_start(dst, src).then_inc(late_consts_in, 16)
            sp.dma_start(wg0r[:], a["wg0"]).then_inc(experts0_in, 16)
            sp.dma_start(wu0r[:], a["wu0"]).then_inc(experts0_in, 16)
            sp.dma_start(wd0[:], a["wd0"]).then_inc(experts0_in, 16)

            def next_turn():
                sp.wait_ge(s["arrived"], 4)
                sp.sem_clear(turn_sems)
                for e in go:
                    sp.sem_inc(go[e], 1)

            next_turn()
            for b in (0,):
                sp.wait_ge(s["residual_made"], 1)
                load_batch(b + 1)
                load_previous(b)
                sp.wait_ge(s["prev_in"], 16)
                next_turn()
            with sp.Fori(1, B - 1) as b:
                sp.wait_ge(s["residual_made"], 1)
                load_batch(b + 1)
                sp.wait_ge(s["prev_used"], 1)
                load_previous(b)
                sp.wait_ge(s["prev_in"], 16)
                next_turn()
            sp.wait_ge(s["prev_used"], 1)
            load_previous(B - 1)
            sp.wait_ge(s["prev_in"], 16)
            next_turn()

            def load_expert(e):
                w = e % WSLOTS
                cols = slice(e * F1D, (e + 1) * F1D)
                sp.dma_start(wg1r[:, w, :], a["wg1"][:, cols]).then_inc(expert_in[e], 16)
                sp.dma_start(wu1r[:, w, :], a["wu1"][:, cols]).then_inc(expert_in[e], 16)
                sp.dma_start(wd1[:, w], a["wd1"][:, e * (F1D // P):(e + 1) * (F1D // P)]).then_inc(expert_in[e], 16)

            for e in range(WSLOTS):
                load_expert(e)
            next_turn()
            for e in range(WSLOTS, E1):
                sp.wait_ge(s["d_ps"], CHUNKS * B * (e - WSLOTS + 1))
                load_expert(e)
            for i, slot in enumerate(SLOTS):
                sp.wait_ge(s["x_sum"], i + 1)
                sp.dma_start(out[i:i + 1].rearrange("a (t p) d -> p (a t) d", p=P), XR[:, slot * QT:(slot + 1) * QT])\
                  .then_inc(s["out_in"], 16)
            sp.wait_ge(s["out_in"], 16 * B)

        @block.gpsimd
        def _(pool):
            zeros = [T2, V2d, NMp, att]
            for z in zeros:
                pool.memset(z[:], 0.0).then_inc(setup_pool, 1)
            pool.memset(Kbd[:].bitcast(F32), 0.0).then_inc(setup_pool, 1)
            pool.memset(Kb2[:].bitcast(F32), 0.0).then_inc(setup_pool, 1)
            pool.memset(XR[:, 0:QT, :], 0.0).then_inc(setup_pool, 1)
            pool.wait_ge(consts_in, 16 * N_CONSTS)
            pool.tensor_copy(identb[:], ident[:]).then_inc(consts_made, 1)
            pool.wait_ge(setup_pool, 7)

            def prepare():
                c = Steps(pool, s["pool_step"])
                pool.wait_ge(s["next_in"], 48)
                for n in range(2):
                    src = cpad[:, P + n:P + n + 32].unsqueeze(1).to_broadcast([D, GH, 32])
                    pool.tensor_copy(ctail[:, n, :].rearrange("p (j r) -> p j r", j=GH), src).then_inc(s["tails"], 1)
                for i, ch in enumerate((1, 0)):
                    pool.wait_ge(s["tab_f"], 2 * i + 2)
                    c.link(pool.tensor_copy(T1[:, 0, ch], tabf[:]))
                    pool.tensor_tensor(tabr[:], tabf[:], T1[:, 0, ch], ALU.subtract).then_inc(s["tab_split"], 1)
                    pool.wait_ge(s["tab_split"], i + 1)
                    c.link(pool.tensor_copy(T1[:, 1, ch], tabr[:]))
                    pool.tensor_tensor(T1[:, 2, ch], tabr[:], T1[:, 1, ch], ALU.subtract).then_inc(s["tab_ready"], 1)
                    pool.wait_ge(s["tab_ready"], i + 1)

            def tail_of_previous():
                pool.tensor_copy(ctailp[:].rearrange("p (j r) -> p j r", j=GH),
                                 cprev[:, P + 1:P + 33].unsqueeze(1).to_broadcast([D, GH, 32])).then_inc(s["tailp"], 1)

            def combine():
                c = Steps(pool, s["comb_step"])
                for g in range(NG - 1):
                    pool.wait_ge(s["coef_ready"], g + 1)
                    w = coef[:, g % 2].rearrange("p k s q -> p (k s q)").unsqueeze(2).to_broadcast([P, NK * 2 * QT * GH, HD])
                    v = vv[g % 2][:].rearrange("p k s q c -> p (k s q) c")
                    pool.tensor_tensor(v, v, w, ALU.mult).then_inc(s["vw_ready"], 1)
                    pool.wait_ge(s["vw_ready"], g + 1)
                    part = vv[g % 2][:].rearrange("p k s q c -> p (k s) (q c)")
                    for n in (5, 2, 1):
                        c.link(pool.tensor_tensor(part[:, 0:n], part[:, 0:n], part[:, n:2 * n], ALU.add))
                        if n == 5:
                            c.link(pool.tensor_tensor(part[:, 0:1], part[:, 0:1], part[:, 4:5], ALU.add))
                    pool.tensor_copy(ctok[:, :, g * GH * HD:(g + 1) * GH * HD],
                                     part[:, 0].rearrange("p (t c) -> p t c", t=QT)).then_inc(s["ctok_pool"], 1)
                    pool.wait_ge(s["ctok_pool"], g + 1)

            def split_queries():
                c = Steps(pool, s["split_step"])
                for g in range(NG):
                    pool.wait_ge(s["q1_ev"], g + 1)
                    c.link(pool.tensor_scalar(qhi[:, g % 2, :], qhi[:, g % 2, :].bitcast(F32), pcol[:, 3:4], None, ALU.mult))
                    pool.tensor_tensor(qf[:, g, :], qtmp[:, g, :], qhi[:, g % 2, :].bitcast(F32), ALU.add)\
                        .then_inc(s["qf_ready"], 1)

            def add_bias():
                pool.tensor_tensor(XI[:], XI[:], bo[:].unsqueeze(1).to_broadcast([P, QT, D]), ALU.add)\
                    .then_inc(s["bias_added"], 1)

            def keep(slot):
                pool.tensor_tensor(XR[:, bass.ds(slot * QT, QT), :], XX[:, QT:],
                                   beta[:].unsqueeze(1).to_broadcast([P, QT, D]), ALU.add).then_inc(s["kept"], 1)

            def add_attention(slot, n):
                pool.wait_ge(s["att_normed"], n)
                pool.tensor_tensor(att[:], att[:], gamma[:].unsqueeze(1).to_broadcast([P, QT, D]), ALU.mult)\
                    .then_inc(s["gamma_step"], 1)
                pool.wait_ge(s["gamma_step"], n)
                rows = bass.ds(slot * QT, QT)
                pool.tensor_tensor(XR[:, rows, :], XR[:, rows, :], att[:], ALU.add).then_inc(s["x3_ready"], 1)

            def split_step(e, step):
                w, done = e % WSLOTS, 4 * e + step
                high, low, raw = ((wg1h, wg1l, wg1r), (wu1h, wu1l, wu1r))[step // 2]
                if step == 0:
                    pool.wait_ge(expert_in[e], 48)
                if step % 2 == 0:
                    pool.tensor_copy(high[:, w, :], raw[:, w, :]).then_inc(experts1_split, 1)
                else:
                    pool.wait_ge(experts1_split, done)
                    pool.tensor_tensor(low[:, w, :], raw[:, w, :], high[:, w, :].bitcast(F32), ALU.subtract)\
                        .then_inc(experts1_split, 1)

            def split_expert(e):
                for step in range(4):
                    split_step(e, step)

            def split_input(i):
                rows = slice(SLOTS[i] * S, (SLOTS[i] + 1) * S)
                pool.tensor_copy(xhall[:, rows], XT3[:, rows]).then_inc(x_split, 1)
                pool.wait_ge(x_split, 2 * i + 1)
                pool.tensor_tensor(xlall[:, rows], XT3[:, rows], xhall[:, rows].bitcast(F32), ALU.subtract).then_inc(x_split, 1)

            prepare()
            finish_turn(pool, "pool")
            pool.wait_ge(late_consts_in, 16 * N_LATE)
            pool.tensor_copy(ident3b[:], ident3[:]).then_inc(consts_made, 1)
            add_bias()
            for n, (high, low, raw) in enumerate(((wg0h, wg0l, wg0r), (wu0h, wu0l, wu0r))):
                pool.wait_ge(experts0_split, n + 1)
                pool.tensor_tensor(low[:], raw[:], high[:].bitcast(F32), ALU.subtract).then_inc(experts0_low, 1)
            combine()
            prepare()
            finish_turn(pool, "pool")

            def turn_of_loop(b, more):
                tail_of_previous()
                keep(b)
                add_bias()
                add_attention(b - 1, 1)
                combine()
                split_queries()
                if more:
                    prepare()
                finish_turn(pool, "pool")

            with pool.Fori(1, B - 1) as b:
                turn_of_loop(b, True)
            turn_of_loop(B - 1, False)
            tail_of_previous()
            keep(0)
            add_attention(B - 1, 1)
            split_expert(0)
            split_input(0)
            split_input(1)
            for e in range(1, WSLOTS):
                split_expert(e)
            pool.wait_ge(s["kept"], 1)
            add_attention(0, 2)
            finish_turn(pool, "pool")
            split_input(2)
            split_input(3)
            for n in range(N_TANH):
                pool.wait_ge(s["t_ready"], n + 1)
                pool.tensor_tensor(gS[:, n % 3, :], gS[:, n % 3, :], tS[:, n % 3, :], ALU.mult).then_inc(s["p_ready"], 1)
                for e in range(WSLOTS, E1):
                    step, odd = divmod(n - CHUNKS * B * (e - WSLOTS + 1) - 8, 2)
                    if not odd and 0 <= step < 4:
                        split_step(e, step)

        def act_ffn(act, chunks, between):
            for j in range(chunks):
                act.wait_ge(s["g_in"], j + 1)
                if j >= 2:
                    act.wait_ge(s["h_ready"], j - 1)
                act.activation(sg[:, j % 2, :], PS[:, 0, :], ACT.Silu).then_inc(s["sg_ready"], 1)
                between(j)
            act.wait_ge(s["acc_ps"], 1)
            act.copy(yT[:], PS[:, 3, :]).then_inc(s["yT_ready"], 1)

        @block.scalar
        def _(act):
            def deviation(n, tiles=slice(0, 2 * QT)):
                act.wait_ge(s["ln_var"], n)
                act.activation(std[:, tiles], var[:, tiles], ACT.Sqrt).then_inc(s["ln_std"], 1)

            def turned(n, dst, bank):
                act.wait_ge(s["xnT_ps"], n)
                act.copy(dst[:], PS[:, bank, :]).then_inc(s["xnT_ready"], 1)

            def sampling(prev, slot):
                for n in range(NG * NK + 1):
                    if prev and n in DEVIATIONS:
                        i = DEVIATIONS.index(n)
                        deviation(i + 1, slice(QT, 2 * QT) if i == 0 else slice(0, QT))
                    if n < NG * NK:
                        act.wait_ge(s["bc_a"], n + 1)
                        if n >= 1:
                            act.wait_ge(s["oh_a"], n)
                        act.copy(cbc[:, 0:2, :], PS[:, 0:2, :]).then_inc(s["ev_a"], 1)
                        act.wait_ge(s["bc_b"], n + 1)
                        if n >= 1:
                            act.wait_ge(s["oh_b"], n)
                        act.copy(cbc[:, 2:4, :], PS[:, 2:4, :]).then_inc(s["ev_b"], 1)
                    if n >= 1:
                        act.wait_ge(s["g_ps"], n)
                        if n >= 3:
                            act.wait_ge(s["pt_ps"], n - 2)
                        act.copy(gs[:, (n - 1) % 2, :], PS[:, 5 + (n - 1) % 2, :]).then_inc(s["g_ev"], 1)
                    if n > NK and n % NK == 2:
                        g = n // NK - 1
                        act.wait_ge(s["sc_in"], g + 1)
                        act.activation(ee[:], sc[:], ACT.Exp, scale=0.5 * INV_SQRT).then_inc(s["sc_exp"], 1)
                if prev:
                    keys()
                    turned(1, pnT, 4)
                    finished(slot, 2)
                    values(5)
                act.wait_ge(s["sc_in"], NG)
                act.activation(ee[:], sc[:], ACT.Exp, scale=0.5 * INV_SQRT).then_inc(s["sc_exp"], 1)
                if prev:
                    queries(range(2))
                    act.wait_ge(s["cost_read"], 1)
                act.wait_ge(s["ctxT_ps"], 1)
                act.mul(ctxT[:], PS[:, 0, :], 0.5).then_inc(s["ctxT_ready"], 1)
                if prev:
                    queries(range(2, NG))

            def finished(slot, n):
                act.wait_ge(s["xnT_ps"], n)
                act.copy(XT3[:, bass.ds(slot * S, S)], PS[:, 0, :])
                act.copy(yT[:], PS[:, 0, :]).then_inc(s["xnT_ready"], 1)

            def keys():
                for g in range(NG):
                    act.wait_ge(s["k1_ps"], 2 * (g // 2) + 2)
                    src = PS[:, K_BANK[g], (g % 2) * 256:(g % 2) * 256 + M]
                    act.activation(ktmp[:, g, :], src, ACT.Identity, bias=bqk1[:, 1, g:g + 1])
                    act.activation(khi[:, g, :], src, ACT.Identity, bias=bqk1[:, 1, g:g + 1]).then_inc(s["k1_ev"], 1)

            def values(bank):
                act.wait_ge(s["v1_ps"], 1)
                act.copy(V1[:], PS[:, bank, :])
                for j in range(GH):
                    r = slice(32 * j, 32 * j + 32)
                    last = act.copy(V2d[r, :, r], PS[r, bank + 1, :].rearrange("p (g j c) -> p g j c", g=NG, j=GH)[:, :, j, :])
                last.then_inc(s["v1_ready"], 1)

            def queries(groups):
                for g in groups:
                    act.wait_ge(s["q1_ps"], g + 1)
                    if g >= 2:
                        act.wait_ge(s["qf_ready"], g - 1)
                    act.activation(qtmp[:, g, :], PS[:, 4 + g, :], ACT.Identity, bias=bqk1[:, 0, g:g + 1])
                    act.activation(qhi[:, g % 2, :], PS[:, 4 + g, :], ACT.Identity, bias=bqk1[:, 0, g:g + 1])\
                       .then_inc(s["q1_ev"], 1)

            def attend(j, plan=PLAN):
                g, part = (j - plan.s_slot) // 3, (j - plan.s_slot) % 3
                if j >= plan.s_slot and g < NG and part == 0:
                    if g >= 1:
                        act.wait_ge(s["ot_ps"], g)
                    act.wait_ge(s["s_b"], g + 1)
                    act.activation(Ex[:, 2:4, :], PS[:, plan.s_bank:plan.s_bank + 2, :], ACT.Exp, scale=INV_SQRT).then_inc(s["e_b"], 1)
                    act.wait_ge(s["s_c"], g + 1)
                    act.activation(Ex2[:], PS[:, 5, :], ACT.Exp, scale=INV_SQRT).then_inc(s["e_c"], 1)
                if j >= plan.s_slot and g < NG and part == 1:
                    act.wait_ge(s["s_a"], g + 1)
                    act.activation(Ex[:, 0:2, :], PS[:, plan.s_bank:plan.s_bank + 2, :], ACT.Exp, scale=INV_SQRT).then_inc(s["e_a"], 1)

            def prepare(j, ln, turns):
                if j == NORM_SLOT:
                    deviation(ln + 1, slice(0, QT))
                if j == TURN_SLOT:
                    turned(turns + 1, xnT, 4)
                if j == Q_SLOT:
                    act.wait_ge(s["q_ps"], 1)
                    act.activation(qT[:], PS[:, 4, :], ACT.Identity, bias=bcol[:, 0:1]).then_inc(s["qT_ready"], 1)

            def batch(prev, more=True, slot=None):
                norms, turns = (4, 3) if prev else (1, 1)

                def between(j):
                    if j == 0:
                        act.wait_ge(s["cbT_ps"], 1)
                        act.copy(cbT[:], PS[0:96, 3, :].bitcast(BF16)[:, 0:S]).then_inc(s["cbT_ready"], 1)
                    if prev:
                        attend(j)
                    if more:
                        prepare(j, norms, turns)

                sampling(prev, slot)
                deviation(norms, slice(0, QT))
                act.preload_act_table_set("sigmoid_and_others")
                turned(turns, xnT, 0)
                act.copy(xhi[:], PS[:, 0, :]).then_inc(s["xhi_ready"], 1)
                act.wait_ge(s["lg_ps"], 1)
                act.activation(rsc[:], PS[:, 1, 0:QT * E0].rearrange("p (t e) -> p t e", t=QT), ACT.Sigmoid)\
                   .then_inc(s["score_in"], 1)
                act_ffn(act, C0, between)
                finish_turn(act, "act")

            act.wait_ge(consts_in, 16 * N_CONSTS)
            for j in range(C0):
                prepare(j, 0, 0)
            act.wait_ge(experts0_in, 48)
            act.copy(wg0h[:], wg0r[:]).then_inc(experts0_split, 1)
            act.copy(wu0h[:], wu0r[:]).then_inc(experts0_split, 1)
            finish_turn(act, "act")
            act.wait_ge(late_consts_in, 16 * N_LATE)
            batch(False)
            with act.Fori(1, B - 1) as b:
                batch(True, slot=b - 1)
            batch(True, False, B - 2)
            deviation(1, slice(QT, 2 * QT))
            deviation(2, slice(0, QT))
            keys()
            turned(1, pnT, 4)
            queries(range(NG))
            values(4)
            deviation(3, slice(0, QT))
            for j in range(-1, TAIL_PLAN.s_slot + 3 * NG + 1):
                attend(j, TAIL_PLAN)
            finished(B - 1, 2)
            deviation(4, slice(0, QT))
            deviation(5, slice(0, QT))
            finished(0, 3)
            finish_turn(act, "act")

            c = Steps(act, s["act_step"])
            act.preload_act_table_set("exp_and_others")
            act.wait_ge(sk_ones, 1)

            def gate(n):
                g, t = gS[:, n % 3, :], tS[:, n % 3, :]
                act.wait_ge(s["g_in"], n + 1)
                if n >= 3:
                    act.wait_ge(s["h_ready"], n - 2)
                if n < N_TANH:
                    if n >= 3:
                        act.wait_ge(s["p_ready"], n - 2)
                    c.tick(act.activation(t, PS[:, 1 + n % 2, :], ACT.Tanh, scale=0.5))
                    act.copy(g, PS[:, 1 + n % 2, :]).then_inc(s["g_read"], 1)
                    c.settle()
                    act.wait_ge(s["g_read"], n + 1)
                    act.activation(t, t, ACT.Identity, bias=onesm[:, 0:1]).then_inc(s["t_ready"], 1)
                else:
                    act.activation(g, PS[:, 1 + n % 2, :], ACT.Silu).then_inc(s["sg_ready"], 1)

            def store_result(u):
                act.wait_ge(s["d_ps"], CHUNKS * (u + 1))
                if u >= N_STORED + 4:
                    act.wait_ge(s["yt_ps"], u - N_STORED - 3)
                act.mul(yS[:, STORE[u], :], PS[:, 6 + u % 2, :], 0.5 if u < N_TANH // CHUNKS else 1.0).then_inc(s["y_stored"], 1)

            for n in range(N_CHUNKS):
                gate(n)
                it, part = n // CHUNKS, n % CHUNKS
                if 1 <= it <= SINK and part == 0:
                    for i in range(2):
                        act.wait_ge(sk_log_in, 2 * it - 1 + i)
                        act.activation(scol[:, 4, :], scol[:, 2, :], ACT.Exp, scale=-1.0).then_inc(sk_log_exp, 1)
                if n == CHUNKS * SINK:
                    act.wait_ge(sk_row_sum, 1)
                    act.activation(srow[:, 2, :], srow[:, 1, :], ACT.Ln).then_inc(sk_row_ln, 1)
                if it < SINK and part == 2:
                    act.wait_ge(sk_row_in, it + 1)
                    act.activation(sE[:], sR[:], ACT.Exp).then_inc(sk_row_exp, 1)
                if it < SINK and part == 3:
                    act.wait_ge(sk_col_in, it + 1)
                    act.activation(sG[:], sQ[:], ACT.Exp).then_inc(sk_col_exp, 1)
                if n == N_TANH - 1:
                    act.wait_ge(sk_row_in, SINK + 1)
                    act.activation(sE[:], sR[:], ACT.Exp).then_inc(sk_row_exp, 1)
                if n >= CHUNKS and part == LAG - 1:
                    store_result(it - 1)
            store_result(N_UNITS - 1)

        def dve_ffn(dve, chunks, between):
            for j in range(chunks):
                dve.wait_ge(s["sg_ready"], j + 1)
                dve.wait_ge(s["gu_ps"], j + 1)
                dve.tensor_tensor(sg[:, j % 2, :], sg[:, j % 2, :], PS[:, 1, :], ALU.mult).then_inc(s["h_used"], 1)
                dve.wait_ge(s["h_used"], j + 1)
                if j >= 2:
                    dve.wait_ge(s["d_ps"], j - 1)
                dve.tensor_tensor(hh[:, j % 2, :], sg[:, j % 2, :], PS[:, 2, :], ALU.mult).then_inc(s["h_ready"], 1)
                between(j)

        @block.vector
        def _(dve):
            dve.wait_ge(consts_in, 16 * N_CONSTS)
            dve.wait_ge(setup_pool, 7)

            def norm_stats(c, src, tiles):
                for t in tiles:
                    last = dve.bn_stats(st[:, t, :], src[:, t, :])
                c.link(last)
                for t in tiles:
                    last = dve.bn_aggr(mv[:, t, :], st[:, t, :])
                c.link(last)
                r = slice(tiles[0], tiles[-1] + 1)
                dve.tensor_scalar(var[:, r], mv[:, r, 1], EPS, None, ALU.add).then_inc(s["ln_var"], 1)

            def norm_apply(c, src, dst, tiles, n):
                r = slice(tiles[0], tiles[-1] + 1)
                dve.wait_ge(s["ln_std"], n)
                c.link(dve.reciprocal(rstd[:, r], std[:, r]))
                for t in tiles:
                    last = dve.tensor_scalar(dst[:, t, :], src[:, t, :], mv[:, t, 0:1], rstd[:, t:t + 1],
                                             ALU.subtract, ALU.mult)
                return last

            def prepare(c, j, ln):
                length, minus_length, rlength = len3[:, 1:2], len3[:, 2:3], len3[:, 3:4]
                if j == NORM_SLOT:
                    dve.wait_ge(s["next_in"], 48)
                    norm_stats(c, XI, range(QT))
                if j == NORM_SLOT + 1:
                    norm_apply(c, XI, xn, range(QT), ln + 1).then_inc(s["xn_ready"], 1)
                if j == TURN_SLOT:
                    c.link(dve.tensor_copy(mskf[:], mski[:]))
                    c.link(dve.reduce_sum(len3[:, 0:1], mskf[:], AX_X))
                    c.tick(dve.tensor_scalar(len3[:, 1:2], len3[:, 0:1], -1.0, float(M - 1), ALU.mult, ALU.add))
                    c.link(dve.tensor_scalar(len3[:, 2:3], len3[:, 0:1], float(M - 1), None, ALU.subtract))
                    c.link(dve.reciprocal(len3[:, 3:4], len3[:, 1:2]))
                if j == QT_SLOT:
                    dve.wait_ge(s["q_ps"], 2)
                    dve.tensor_copy(qhg[:].rearrange("p g t e -> p t g e"),
                                    PS[:, 4, :].rearrange("p (t g e) -> p t g e", t=QT, g=NG)).then_inc(s["qhg_ready"], 1)
                if j == OFF_SLOT:
                    dve.wait_ge(s["off_ps"], 1)
                    dve.tensor_scalar(v0[:], PS[0:HK, 4, :], bcol[0:HK, 1:2], pcol[0:HK, 2:3], ALU.add, ALU.add)\
                       .then_inc(s["off_read"], 1)
                    dve.wait_ge(s["off_read"], 1)
                    c.link(dve.tensor_tensor(v0[:], v0[:], locrow[:], ALU.add))
                if j == OFF_SLOT + 1:
                    c.link(dve.tensor_scalar(vi[:], v0[:], rlength, None, ALU.mult))
                    c.link(dve.scalar_tensor_tensor(out=v0[:], in0=vi[:], scalar=minus_length, in1=v0[:], op0=ALU.mult, op1=ALU.add))
                if j == OFF_SLOT + 2:
                    c.link(dve.tensor_scalar(v1[:], v0[:], rlength, 0.0, ALU.mult, ALU.is_lt))
                    c.link(dve.scalar_tensor_tensor(out=v0[:], in0=v1[:], scalar=length, in1=v0[:], op0=ALU.mult, op1=ALU.add))
                if j == OFF_SLOT + 3:
                    c.link(dve.tensor_scalar(v0[:], v0[:], float(M) / (M - 1), -0.5, ALU.mult, ALU.add))
                    c.link(dve.tensor_copy(vi[:], v0[:]))
                if j == OFF_SLOT + 4:
                    c.link(dve.tensor_tensor(dxf[:], vi[:], v0[:], ALU.is_gt))
                    c.link(dve.tensor_tensor(v1[:], vi[:], dxf[:], ALU.subtract))
                if j == OFF_SLOT + 5:
                    c.tick(dve.tensor_scalar(ibf[:], v1[:], 1.0, None, ALU.add))
                    dve.tensor_tensor(dxf[:], v0[:], v1[:], ALU.subtract).then_inc(s["off_ready"], 1)
                for i in range(2):
                    if j == TABLE_SLOTS[i]:
                        dve.wait_ge(s["tab_ps"], i + 1)
                        if i:
                            dve.wait_ge(s["tab_split"], 1)
                        t4 = tabf[:].rearrange("p (h v s c) -> p v h s c", h=H, v=2, s=2)
                        ps = PS[:, 4, :].rearrange("p (n v h c) -> p n v h c", n=2, v=2, h=H)
                        dve.tensor_copy(t4[:, :, :, 0, :], ps[:, 0]).then_inc(s["tab_f"], 1)
                        dve.wait_ge(s["tab_f"], 2 * i + 1)
                        dve.tensor_tensor(t4[:, :, :, 1, :], ps[:, 1], t4[:, :, :, 0, :], ALU.subtract).then_inc(s["tab_f"], 1)
                if j == DX_SLOT:
                    dve.wait_ge(s["tab_ready"], 1)
                    for h in range(GH):
                        r = slice(32 * h, 32 * h + 32)
                        for p in range(3):
                            c.tick(dve.tensor_copy(T2[r, p, :, r], T1[r, p, 1, :].rearrange("p (g h c) -> p g h c", g=NG, h=GH)[:, :, h, :]))
                    dve.wait_ge(s["dxT_ps"], 1)
                    for g in range(NG):
                        src = PS[:, 4, 0:QT * HK].rearrange("p (t h k) -> p k t h", t=QT, k=NK)[:, :, :, g * GH:(g + 1) * GH]
                        last = dve.tensor_copy(dxg[:, g].rearrange("p k (t h) -> p k t h", t=QT), src)
                    last.then_inc(s["dxg_ready"], 1)

            def attention_normed(c, n):
                norm_apply(c, att, att, range(QT), n).then_inc(s["att_normed"], 1)

            def residual_stats(c, slot, n):
                dve.wait_ge(s["x3_ready"], n)
                norm_stats(c, XR[:, bass.ds(slot * QT, QT), :], range(QT))

            def residual_normed(c, slot, n):
                norm_apply(c, XR[:, bass.ds(slot * QT, QT), :], xn, range(QT), n).then_inc(s["xn_ready"], 1)

            def costs(c, slot, n):
                dve.wait_ge(s["cost_out"], n)
                dve.tensor_scalar(CST[:, bass.ds(slot * QT, QT), :], PS[:, 1, 0:QT * E1].rearrange("p (t e) -> p t e", t=QT),
                                  -20.0, None, ALU.mult).then_inc(s["cost_read"], 1)

            def sampling(c, prev, slot):
                if prev:
                    norm_stats(c, XX, range(QT, 2 * QT))
                def products(points):
                    return dve.reduce_sum(pkr[:, points].rearrange("p k s q -> p (k s q)"),
                                          pk[:, points].rearrange("p k s q c -> p (k s q) c"), AX_X)

                def weigh(g):
                    c.link(products(slice(NK - 1, NK) if g == NG - 1 else slice(0, NK)))
                    c.link(dve.tensor_tensor(sc[:], pkr[:, :, 1, :], dxg[:, g], ALU.mult))
                    c.link(dve.tensor_tensor(sc[:], sc[:], pkr[:, :, 0, :], ALU.add))
                    c.link(dve.reduce_max(sm[:, 0, :], sc[:].rearrange("p k q -> p q k"), AX_X))
                    dve.tensor_tensor(sc[:], sc[:], sm[:, 0, :].unsqueeze(1).to_broadcast([P, NK, QT * GH]),
                                      ALU.subtract).then_inc(s["sc_in"], 1)

                def weights(g):
                    dve.wait_ge(s["sc_exp"], g + 1)
                    w = coef[:, g % 2]
                    c.link(dve.reduce_sum(sm[:, 1, :], ee[:].rearrange("p k q -> p q k"), AX_X))
                    c.link(dve.reciprocal(sm[:, 2, :], sm[:, 1, :]))
                    if g >= 2:
                        dve.wait_ge(s["vw_ready"], g - 1)
                    c.link(dve.tensor_tensor(w[:, :, 0, :], ee[:],
                                             sm[:, 2, :].unsqueeze(1).to_broadcast([P, NK, QT * GH]), ALU.mult))
                    dve.tensor_tensor(w[:, :, 1, :], w[:, :, 0, :], dxg[:, g], ALU.mult).then_inc(s["coef_ready"], 1)

                def combine_last():
                    g = NG - 1
                    dve.wait_ge(s["coef_ready"], NG)
                    w = coef[:, g % 2].rearrange("p k s q -> p (k s q)").unsqueeze(2).to_broadcast([P, NK * 2 * QT * GH, HD])
                    v = vv[g % 2][:].rearrange("p k s q c -> p (k s q) c")
                    c.link(dve.tensor_tensor(v, v, w, ALU.mult))
                    dve.reduce_sum(ctok[:, :, g * GH * HD:(g + 1) * GH * HD],
                                   vv[g % 2][:].rearrange("p k s (t j) c -> p t (j c) (k s)", t=QT), AX_X)\
                       .then_inc(s["ctok_ready"], 1)

                for n in range(NG * NK + 2):
                    if n < NG * NK:
                        dve.wait_ge(s["ev_a"], n + 1)
                        if n >= 2:
                            dve.wait_ge(s["g_ps"], n - 1)
                        dve.tensor_scalar(oh1[:, n % 2, 0:2, :], cbc[:, 0:2, :], pcol[:, 0:1], None, ALU.is_equal)\
                           .then_inc(s["oh_a"], 1)
                        dve.wait_ge(s["bc_c"], n + 1)
                        dve.tensor_scalar(oh2[:, n % 2, :], PS[:, 4, :], pcol[:, 1:2], None, ALU.is_equal)\
                           .then_inc(s["oh_c"], 1)
                        dve.wait_ge(s["ev_b"], n + 1)
                        dve.tensor_scalar(oh1[:, n % 2, 2:4, :], cbc[:, 2:4, :], pcol[:, 0:1], None, ALU.is_equal)\
                           .then_inc(s["oh_b"], 1)
                    if n == 1 and prev:
                        norm_apply(c, XX, xn, range(QT, 2 * QT), 1).then_inc(s["xn_ready"], 1)
                    if n == 2 and prev:
                        norm_stats(c, att, range(QT))
                    if n == 5 and prev:
                        attention_normed(c, 2)
                    if n == 9 and prev:
                        residual_stats(c, slot, 1)
                    if n == 12 and prev:
                        residual_normed(c, slot, 3)
                    if n >= 2:
                        m = n - 2
                        g, k = m // NK, m % NK
                        if k == 0 and g >= 1:
                            weights(g - 1)
                            if g >= 2:
                                dve.wait_ge(s["ctok_pool"], g - 1)
                        dve.wait_ge(s["pt_ps"], m + 1)
                        pt = PS[:, 7, :].rearrange("p (q v s c) -> p v s q c", q=QT * GH, v=2, s=2)
                        q = qhg[:, g].rearrange("p t (j c) -> p (t j) c", j=GH)
                        dve.tensor_tensor(pk[:, k], pt[:, 0], q.unsqueeze(1).to_broadcast([P, 2, QT * GH, HD]), ALU.mult)
                        dve.tensor_copy(vv[g % 2][:, k], pt[:, 1]).then_inc(s["pt_used"], 1)
                        if k == NK - 1:
                            dve.wait_ge(s["pt_used"], m + 1)
                            weigh(g)
                        if g == NG - 1 and k == NK - 2:
                            dve.wait_ge(s["pt_used"], m + 1)
                            c.link(products(slice(0, NK - 1)))
                weights(NG - 1)
                combine_last()
                if prev:
                    costs(c, slot, 1)
                    split_keys(c)
                dve.wait_ge(s["y_ps"], 1)
                dve.wait_ge(s["bias_added"], 1)
                c.tick(dve.tensor_tensor(XX[:, 0:QT], XI[:], PS[:, 1, :].rearrange("p (t d) -> p t d", t=QT), ALU.add))
                c.settle()
                dve.sem_inc(s["residual_made"], 1)

            def route(c):
                dve.wait_ge(s["score_in"], 1)
                c.link(dve.tensor_tensor(rbi[:], rsc[:], eb0[:].unsqueeze(1).to_broadcast([P, QT, E0]), ALU.add))
                for t in range(QT):
                    last = dve.max(rmx[:, t, :], rbi[:, t, :])
                c.link(last)
                for t in range(QT):
                    last = dve.max_index(rix[:, t, :], rmx[:, t, :], rbi[:, t, :])
                c.link(last)
                c.link(dve.tensor_copy(rif[:], rix[:]))
                for t in range(QT):
                    last = dve.tensor_tensor(roh[:, t], erow[:].unsqueeze(1).to_broadcast([P, K0, E0]),
                                             rif[:, t, 0:K0].unsqueeze(2).to_broadcast([P, K0, E0]), ALU.is_equal)
                c.link(last)
                c.link(dve.reduce_sum(rms[:], roh[:].rearrange("p t k e -> p t e k"), AX_X))
                c.link(dve.tensor_tensor(rms[:], rms[:], rsc[:], ALU.mult))
                c.link(dve.reduce_sum(rsum[:, :, 0], rms[:], AX_X))
                c.link(dve.reciprocal(rsum[:, :, 1], rsum[:, :, 0]))
                c.link(dve.tensor_tensor(rcm[:], rms[:], rsum[:, :, 1:2].to_broadcast([P, QT, E0]), ALU.mult))
                c.link(dve.tensor_copy(cb3[:, :, 0, :], rcm[:]))
                c.link(dve.tensor_tensor(rbi[:], rcm[:], cb3[:, :, 0, :], ALU.subtract))
                c.link(dve.tensor_copy(cb3[:, :, 1, :], rbi[:]))
                dve.tensor_tensor(cb3[:, :, 2, :], rbi[:], cb3[:, :, 1, :], ALU.subtract).then_inc(s["cb3_ready"], 1)

            def split_keys(c):
                dve.wait_ge(s["k1_ev"], NG)
                for j in range(GH):
                    r = slice(32 * j, 32 * j + 32)
                    dve.scalar_tensor_tensor(out=Kbd[r, :, j, 0:M], in0=khi[r].bitcast(F32), scalar=pcol[r, 4:5],
                                             in1=ktmp[r], op0=ALU.mult, op1=ALU.add)
                    last = dve.scalar_tensor_tensor(out=Kb2[r, :, 32 * j:32 * j + M - P], in0=khi[r, :, P:M].bitcast(F32),
                                                    scalar=pcol[r, 4:5], in1=ktmp[r, :, P:M], op0=ALU.mult, op1=ALU.add)
                last.then_inc(s["kbd_ready"], 1)

            def attend(c, j, plan=PLAN):
                for n, (kind, g, t) in enumerate(MAX_UNITS):
                    if n // plan.max_per_slot - 1 != j:
                        continue
                    bank = plan.max_banks[n % 2]
                    dve.wait_ge(s["mx_ps"], n + 1)
                    if kind == "turn":
                        dve.tensor_tensor(qf[:, g, :], qf[:, g, :].bitcast(F32), PS[:, bank, :], ALU.add).then_inc(s["mx_used"], 1)
                        continue
                    src = PS[:, bank:bank + 2, :].rearrange("p a (j m) -> p (a j) m", j=2)[:, :, 0:M]
                    dve.reduce_max(nmx[:, t, :], src, AX_X).then_inc(s["mx_used"], 1)
                    if t == QT - 1:
                        dve.wait_ge(s["mx_used"], n + 1)
                        nm = NMp[:, g % 2].rearrange("p t (j c) -> p t j c", j=GH)
                        c.link(dve.tensor_scalar(nmh[:], nmx[:], -1.0, None, ALU.mult))
                        dve.tensor_copy(nm[:, :, :, 24], nmh[:].bitcast(F32))
                        dve.scalar_tensor_tensor(out=nm[:, :, :, 25], in0=nmx[:], scalar=-1.0, in1=nmh[:].bitcast(F32),
                                                 op0=ALU.mult, op1=ALU.subtract).then_inc(s["nm_ready"], 1)
                        dve.wait_ge(s["nm_ready"], g + 1)
                g, part = (j - plan.s_slot) // 3, (j - plan.s_slot) % 3
                if j > plan.s_slot and part == 0 and g <= NG:
                    m = g - 1
                    dve.wait_ge(s["ott_ps"], m + 1)
                    pt = PS[:, 4, :].rearrange("p (t j c) -> p t j c", t=QT, j=GH)
                    c.link(dve.reciprocal(rden[:], pt[:, :, :, HD]))
                    av = att[:, :, m * GH * HD:(m + 1) * GH * HD].rearrange("p t (j c) -> p t j c", j=GH)
                    for t in range(QT):
                        last = dve.tensor_tensor(av[:, t], pt[:, t, :, 0:HD],
                                                 rden[:, t, :].unsqueeze(2).to_broadcast([P, GH, HD]), ALU.mult)
                    last.then_inc(s["att_step"], 1)
                if j >= plan.s_slot and part == 2 and g < NG:
                    dve.wait_ge(s["ot_ps"], g + 1)
                    if g >= 1:
                        dve.wait_ge(s["ott_ps"], g)
                    dve.tensor_copy(ots[:], PS[:, 5, :]).then_inc(s["ot_ev"], 1)

            def batch(b, prev, more=True):
                c = Steps(dve, s["dve_step"])

                norms = 4 if prev else 1

                def between(j):
                    if prev:
                        attend(c, j)
                    if more:
                        prepare(c, j, norms)

                sampling(c, prev, b - 1)
                norm_stats(c, XX, range(QT))
                norm_apply(c, XX, xn, range(QT), norms).then_inc(s["xn_ready"], 1)
                dve.wait_ge(s["xhi_ready"], 1)
                dve.tensor_tensor(xlo[:], PS[:, 0, :], xhi[:].bitcast(F32), ALU.subtract).then_inc(s["xlo_ready"], 1)
                route(c)
                if prev:
                    attend(c, -1)
                dve_ffn(dve, C0, between)
                dve.wait_ge(s["yt_ps"], 1)
                if prev:
                    dve.wait_ge(s["kept"], 1)
                c.link(dve.tensor_tensor(XX[:, QT:], XX[:, 0:QT], PS[:, 0, :].rearrange("p (t d) -> p t d", t=QT), ALU.add))
                finish_turn(dve, "dve")

            c = Steps(dve, s["dve_step"])
            for j in range(C0):
                prepare(c, j, 0)
            finish_turn(dve, "dve")
            dve.wait_ge(late_consts_in, 16 * N_LATE)
            batch(0, False)
            with dve.Fori(1, B - 1) as b:
                batch(b, True)
            batch(B - 1, True, False)
            c = Steps(dve, s["dve_step"])
            norm_stats(c, XX, range(QT, 2 * QT))
            norm_apply(c, XX, xn, range(QT, 2 * QT), 1).then_inc(s["xn_ready"], 1)
            norm_stats(c, att, range(QT))
            attention_normed(c, 2)
            split_keys(c)
            for g in range(NG):
                dve.wait_ge(s["q1_ev"], g + 1)
                dve.scalar_tensor_tensor(out=qf[:, g, :], in0=qhi[:, g % 2, :].bitcast(F32), scalar=pcol[:, 3:4],
                                         in1=qtmp[:, g, :], op0=ALU.mult, op1=ALU.add).then_inc(s["qf_ready"], 1)
            residual_stats(c, B - 1, 1)
            residual_normed(c, B - 1, 3)
            for j in range(-1, TAIL_PLAN.s_slot + 3 * NG + 1):
                attend(c, j, TAIL_PLAN)
            c.settle()
            dve.wait_ge(s["att_step"], NG)
            norm_stats(c, att, range(QT))
            attention_normed(c, 4)
            costs(c, B - 1, 1)
            residual_stats(c, 0, 2)
            residual_normed(c, 0, 5)
            costs(c, 0, 2)
            finish_turn(dve, "dve")

            c = Steps(dve, sk_dve)
            dve.memset(onesm[:], 1.0).then_inc(sk_ones, 1)
            dve.wait_ge(sk_ones, 1)
            c.tick(dve.memset(scol[:, 2:4, :], 0.0))
            c.link(dve.tensor_copy(sT[:], CST[:]))
            m, rowsum, v, logsum = srow[:, 0, :], srow[:, 1, :], scol[:, 3, :], scol[:, 2, :]
            over_experts = lambda x: x.unsqueeze(2).to_broadcast([P, NT, E1])
            over_tokens = lambda x: x.unsqueeze(1).to_broadcast([P, NT, E1])

            def rows_in(it):
                c.link(dve.tensor_tensor(sR[:], sT[:], over_tokens(logsum), ALU.subtract))
                if it >= 1:
                    c.tick(dve.tensor_tensor(v, v, logsum, ALU.add))
                c.link(dve.reduce_max(m, sR[:], AX_X))
                dve.tensor_tensor(sR[:], sR[:], over_experts(m), ALU.subtract).then_inc(sk_row_in, 1)
                dve.wait_ge(sk_row_in, it + 1)
                dve.reduce_max(scol[:, 0, :], sR[:].rearrange("p t e -> p e t"), AX_X).then_inc(sk_part_max, 1)

            def row_sums(it):
                dve.wait_ge(sk_turned, it + 1)
                dve.reduce_max(smx[:], PS[0:E1, 0, 0:P], AX_X).then_inc(sk_col_max, 1)
                dve.wait_ge(sk_row_exp, it + 1)
                c.link(dve.reduce_sum(rowsum, sE[:], AX_X))
                if it == SINK - 1:
                    dve.sem_inc(sk_row_sum, 1)
                c.tick(dve.reciprocal(srow[:, 3, :], rowsum))

            def columns_in(it):
                dve.wait_ge(sk_col_spread, it + 1)
                dve.tensor_tensor(sQ[:], sR[:], over_tokens(PS[:, 0, P:P + E1]), ALU.subtract).then_inc(sk_col_in, 1)
                c.link(dve.tensor_tensor(v, v, PS[:, 0, P:P + E1], ALU.add))
                c.tick(dve.tensor_tensor(sT[:], CST[:], over_tokens(v), ALU.subtract))

            def column_sums(it):
                dve.wait_ge(sk_col_exp, it + 1)
                c.link(dve.tensor_tensor(sG[:], sG[:], over_experts(srow[:, 3, :]), ALU.mult))
                dve.reduce_sum(scol[:, 5, :], sG[:].rearrange("p t e -> p e t"), AX_X).then_inc(sk_part_sum, 1)

            def column_logs(it):
                total, y, e = scol[:, 1, :], scol[:, 2, :], scol[:, 4, :]
                dve.wait_ge(sk_col_sum, it + 1)
                c.link(dve.tensor_copy(total, PS[:, 0, P + E1:P + 2 * E1]))
                dve.tensor_scalar(y, total.bitcast(I32), LN_SLOPE, LN_OFFSET, ALU.mult, ALU.add).then_inc(sk_log_in, 1)
                for i in range(2):
                    dve.wait_ge(sk_log_exp, 2 * it + i + 1)
                    c.link(dve.tensor_tensor(e, e, total, ALU.mult))
                    c.link(dve.scalar_tensor_tensor(out=y, in0=e, scalar=-1.0, in1=y, op0=ALU.add, op1=ALU.add))
                    if i == 0:
                        dve.sem_inc(sk_log_in, 1)

            def transport(n):
                n -= CHUNKS * SINK
                if n == 0:
                    dve.wait_ge(sk_row_ln, 1)
                    c.link(dve.tensor_tensor(sQ[:], sQ[:], over_experts(srow[:, 2, :]), ALU.subtract))
                    c.link(dve.tensor_tensor(sR[:], sQ[:], over_tokens(logsum), ALU.subtract))
                    dve.sem_inc(sk_row_in, 1)
                    c.link(dve.tensor_scalar(rank[:], sR[:], EXP_FLOOR, None, ALU.is_ge))
                if n == 4:
                    dve.wait_ge(sk_row_exp, SINK + 1)
                    c.link(dve.tensor_tensor(sE[:], sE[:], rank[:], ALU.mult))
                if 5 <= n < 5 + NT // 2:
                    for t in range(2 * (n - 5), 2 * (n - 5) + 2):
                        mine = sE[:, t, :].unsqueeze(2).to_broadcast([P, E1, E1])
                        other = sE[:, t, :].unsqueeze(1).to_broadcast([P, E1, E1])
                        dve.tensor_tensor(rk1[:, t], other, mine, ALU.is_gt)
                        last = dve.tensor_tensor(rk2[:, t], other, mine, ALU.is_ge)
                    c.tick(last)
                r1 = rk1[:].rearrange("p t a b -> p t (a b)")
                r2 = rk2[:].rearrange("p t a b -> p t (a b)")
                if n == 5 + NT // 2:
                    c.settle()
                    c.link(dve.tensor_tensor(r2, r2, r1, ALU.subtract))
                if n == 6 + NT // 2:
                    c.link(dve.tensor_tensor(r2, r2, lower[:].unsqueeze(1).to_broadcast([P, NT, E1 * E1]), ALU.mult))
                if n == 7 + NT // 2:
                    c.link(dve.tensor_tensor(r2, r2, r1, ALU.add))
                if n == 8 + NT // 2:
                    c.link(dve.reduce_sum(rank[:], rk2[:], AX_X))
                if n == 9 + NT // 2:
                    c.link(dve.tensor_scalar(sR[:], rank[:], 0.0, None, ALU.is_equal))
                    c.link(dve.tensor_scalar(rank[:], rank[:], 1.0, None, ALU.is_equal))
                    c.link(dve.tensor_tensor(sR[:], sR[:], sE[:, :, 0:1].to_broadcast([P, NT, E1]), ALU.mult))
                    c.link(dve.tensor_tensor(rank[:], rank[:], sE[:, :, 1:2].to_broadcast([P, NT, E1]), ALU.mult))
                    c.link(dve.tensor_tensor(sR[:], sR[:], rank[:], ALU.add))

            def add_result(r):
                e, slot = UNITS[RESULTS[r]]
                dve.wait_ge(s["yt_ps"], r + 1)
                if r:
                    dve.wait_ge(s["y_added"], r)
                for t in range(QT):
                    row = slot * QT + t
                    last = dve.scalar_tensor_tensor(out=XR[:, row, :], in0=PS[:, 0, t * P:(t + 1) * P],
                                                    scalar=sR[:, row, e:e + 1], in1=XR[:, row, :], op0=ALU.mult, op1=ALU.add)
                last.then_inc(s["y_added"], 1)
                if r in SLOT_DONE:
                    dve.wait_ge(s["y_added"], r + 1)
                    dve.sem_inc(s["x_sum"], 1)

            for n in range(N_CHUNKS):
                g = gS[:, n % 3, :]
                it, part = n // CHUNKS, n % CHUNKS
                if it < SINK and part == 3:
                    column_sums(it)
                if n < N_TANH:
                    dve.wait_ge(s["p_ready"], n + 1)
                else:
                    dve.wait_ge(s["sg_ready"], n - N_TANH + 1)
                dve.wait_ge(s["up_ps"], n + 1)
                if n >= 4:
                    dve.wait_ge(s["d_ps"], n - 3)
                dve.tensor_tensor(hq[:, n % 4, :], g, PS[:, 3 + n % 3, :], ALU.mult).then_inc(s["h_ready"], 1)
                if n < CHUNKS * SINK:
                    (rows_in, row_sums, columns_in, column_logs)[part](it)
                else:
                    transport(n)
                for r, when in enumerate(RESULTS_AT):
                    if when == n:
                        add_result(r)
            for r, when in enumerate(RESULTS_AT):
                if when == N_CHUNKS:
                    add_result(r)

        def pe_ffn(pe, chunks, wgh, wgl, wuh, wul, wd, turn_weights, between):
            def down(j):
                pe.wait_ge(s["h_ready"], j + 1)
                pe.matmul(PS[:, 3, :], wd[:, j, :], hh[:, j % 2, :], start=(j == 0), stop=(j == chunks - 1),
                          skip_group_check=True).then_inc(s["d_ps"], 1)

            for j in range(chunks):
                cs = slice(j * P, (j + 1) * P)
                if j >= 1:
                    pe.wait_ge(s["sg_ready"], j)
                for n, (w, x) in enumerate(((wgh, xhi), (wgh, xlo), (wgl, xhi))):
                    last = pe.matmul(PS[:, 0, :], w[:, cs], x[:], start=(n == 0), stop=(n == 2))
                last.then_inc(s["g_in"], 1)
                if j >= 1:
                    pe.wait_ge(s["h_used"], j)
                for n, (w, x) in enumerate(((wuh, xhi), (wuh, xlo), (wul, xhi))):
                    last = pe.matmul(PS[:, 1, :], w[:, cs], x[:], start=(n == 0), stop=(n == 2))
                if j == 0:
                    turn_weights()
                if j >= 1:
                    pe.wait_ge(s["h_ready"], j)
                for i in range(GH):
                    e = (GH * j + i) // (I0 // 32)
                    last = pe.matmul(PS[32 * i:32 * i + 32, 2, :], ident3b[:, e:e + 1].to_broadcast([96, 32]),
                                     cbT[:], start=True, stop=True)
                last.then_inc(s["gu_ps"], 1)
                if j >= 1:
                    down(j - 1)
                between(j)
            down(chunks - 1)
            pe.wait_ge(s["d_ps"], chunks)
            pe.sem_inc(s["acc_ps"], 1)
            pe.wait_ge(s["yT_ready"], 1)
            for t in range(QT):
                last = pe.transpose(PS[:, 0, t * P:(t + 1) * P], yT[:, t * P:(t + 1) * P], ident[:])
            last.then_inc(s["yt_ps"], 1)

        @block.tensor
        def _(pe):
            pe.wait_ge(consts_in, 16 * N_CONSTS)
            pe.wait_ge(consts_made, 1)

            def turn(norms, t0, bank):
                pe.wait_ge(s["xn_ready"], norms)
                for t in range(QT):
                    last = pe.transpose(PS[:, bank, t * P:(t + 1) * P], xn[:, t0 + t, :], ident[:])
                last.then_inc(s["xnT_ps"], 1)

            def prepare_waits(j, turns):
                if j == TURN_SLOT + 1:
                    pe.wait_ge(s["xnT_ready"], turns + 1)
                if j == QT_SLOT + 1:
                    pe.wait_ge(s["qhg_ready"], 1)
                for i in range(2):
                    if j == TABLE_SLOTS[i] + 1:
                        pe.wait_ge(s["tab_f"], 2 * i + 2)
                if j == DX_SLOT + 1:
                    pe.wait_ge(s["dxg_ready"], 1)

            def prepare(j, norms, turns, prev):
                if j == TURN_SLOT:
                    if prev:
                        pe.wait_ge(s["mx_used"], len(MAX_UNITS))
                    turn(norms + 1, 0, 4)
                if j == Q_SLOT:
                    if prev:
                        pe.wait_ge(s["att_step"], 1)
                    pe.matmul(PS[:, 4, :], wq0[:], xnT[:], start=True, stop=True).then_inc(s["q_ps"], 1)
                if j == QT_SLOT:
                    pe.wait_ge(s["qT_ready"], 1)
                    for t in range(QT):
                        o = PS[:, 4, t * P:(t + 1) * P]
                        pe.matmul(o, xnT[:, t * P:(t + 1) * P], wq0[:], start=True, stop=False)
                        last = pe.matmul(o, onerow[:], bq0[:], start=False, stop=True)
                    last.then_inc(s["q_ps"], 1)
                if j == OFF_SLOT:
                    if prev:
                        pe.wait_ge(s["att_step"], 2)
                    pe.matmul(PS[0:HK, 4, :], woff[:], qT[:], start=True, stop=True).then_inc(s["off_ps"], 1)
                for i, ch in enumerate((1, 0)):
                    if j == TABLE_SLOTS[i]:
                        if i == 0:
                            pe.wait_ge(s["off_read"], 1)
                            pe.wait_ge(s["tails"], 2)
                        elif prev:
                            pe.wait_ge(s["att_step"], 3)
                        else:
                            pe.wait_ge(s["tab_f"], 2)
                        for n in range(2):
                            rows = cpad[:, n:n + P] if ch == 0 else ctail[:, n, :]
                            there = vrow[:, n:n + P] if ch == 0 else vtail[:, n, :]
                            o = PS[:, 4, n * 2 * D:(n + 1) * 2 * D]
                            pe.matmul(o, rows, wkv[:], start=True, stop=False)
                            last = pe.matmul(o, there, bkv[:], start=False, stop=True)
                        last.then_inc(s["tab_ps"], 1)
                if j == DX_SLOT:
                    if prev:
                        pe.wait_ge(s["att_step"], 4)
                    pe.wait_ge(s["off_ready"], 1)
                    for t in range(QT):
                        last = pe.transpose(PS[:, 4, t * HK:(t + 1) * HK], dxf[:, t * P:(t + 1) * P], ident[0:HK, 0:HK])
                    last.then_inc(s["dxT_ps"], 1)

            def sampling(prev):
                for n in range(NG * NK + 2):
                    if n == NG * NK + 1 and prev:
                        pe.wait_ge(s["ev_b"], NG * NK)
                        keys()
                        pe.wait_ge(s["oh_c"], NG * NK)
                        turn(1, QT, 4)
                        turn(2, 0, 0)
                    if n < NG * NK:
                        g, k = n // NK, n % NK
                        row = lambda j: (GH * g + j) * NK + k
                        if n >= 1:
                            pe.wait_ge(s["ev_a"], n)
                        for j in range(2):
                            last = pe.matmul(PS[:, j, :], identb[0:HK, row(j):row(j) + 1].to_broadcast([HK, P]), ibf[:],
                                             start=True, stop=True)
                        last.then_inc(s["bc_a"], 1)
                        if n >= 1:
                            pe.wait_ge(s["ev_b"], n)
                        for j in range(2, 4):
                            last = pe.matmul(PS[:, j, :], identb[0:HK, row(j):row(j) + 1].to_broadcast([HK, P]), ibf[:],
                                             start=True, stop=True)
                        last.then_inc(s["bc_b"], 1)
                        if n >= 1:
                            pe.wait_ge(s["oh_c"], n)
                        for j in range(4):
                            last = pe.matmul(PS[32 * j:32 * j + 32, 4, :],
                                             identb[0:HK, row(j):row(j) + 1].to_broadcast([HK, 32]), ibf[:],
                                             start=True, stop=True)
                        last.then_inc(s["bc_c"], 1)
                    if 1 <= n <= NG * NK:
                        m = n - 1
                        g = m // NK
                        o = PS[:, 5 + m % 2, :]
                        if m >= 2:
                            pe.wait_ge(s["g_ev"], m - 1)
                        pe.wait_ge(s["oh_c"], m + 1)
                        for p in range(3):
                            pe.matmul(o, T2[:, p, g, :], oh2[:, m % 2, :], start=(p == 0), stop=False, skip_group_check=True)
                        pe.wait_ge(s["oh_a"], m + 1)
                        pe.wait_ge(s["oh_b"], m + 1)
                        for p in range(3):
                            for j in range(GH):
                                h = GH * g + j
                                last = pe.matmul(o[32 * j:32 * j + 32, :], T1[:, p, 0, 32 * h:32 * h + 32], oh1[:, m % 2, j, :],
                                                 start=False, stop=(p == 2), skip_group_check=True)
                        last.then_inc(s["g_ps"], 1)
                    if n >= 2:
                        m = n - 2
                        pe.wait_ge(s["g_ev"], m + 1)
                        if m >= 1:
                            pe.wait_ge(s["pt_used"], m)
                        for t in range(QT):
                            last = pe.transpose(PS[:, 7, t * P:(t + 1) * P], gs[:, m % 2, t * P:(t + 1) * P], ident[:])
                        last.then_inc(s["pt_ps"], 1)

                if prev:
                    values(5)
                    pe.wait_ge(s["pt_used"], NG * NK)
                    queries(True)
                    logits(2)
                    pe.wait_ge(s["cost_read"], 1)
                pe.wait_ge(s["ctok_pool"], NG - 1)
                pe.wait_ge(s["ctok_ready"], 1)
                for t in range(QT):
                    last = pe.transpose(PS[:, 0, t * P:(t + 1) * P], ctok[:, t, :], ident[:])
                last.then_inc(s["ctxT_ps"], 1)
                pe.wait_ge(s["ctxT_ready"], 1)
                for t in range(QT):
                    o = PS[:, 1, t * P:(t + 1) * P]
                    last = pe.matmul(o, ctxT[:, t * P:(t + 1) * P], wo[:], start=True, stop=True)
                last.then_inc(s["y_ps"], 1)

            def logits(turns):
                pe.wait_ge(s["xnT_ready"], turns)
                for t in range(QT):
                    last = pe.matmul(PS[:, 1, t * E1:(t + 1) * E1], yT[:, t * P:(t + 1) * P], gw1[:], start=True, stop=True)
                last.then_inc(s["cost_out"], 1)

            def keys():
                for g in range(NG):
                    pe.matmul(PS[:, K_BANK[g], (g % 2) * 256:(g % 2) * 256 + M], wk1[:, g * P:(g + 1) * P],
                              cprev[:, 1:1 + M], start=True, stop=True).then_inc(s["k1_ps"], 1)

            def values(bank):
                pe.wait_ge(s["tailp"], 1)
                pe.matmul(PS[:, bank, :], cprev[:, 1:1 + P], wv1[:], start=True, stop=False)
                pe.matmul(PS[:, bank, :], vrow[:, 1:1 + P], bv1[:], start=False, stop=True)
                pe.matmul(PS[:, bank + 1, :], ctailp[:], wv1[:], start=True, stop=False)
                pe.matmul(PS[:, bank + 1, :], vtail[:, 1, :], bv1[:], start=False, stop=True).then_inc(s["v1_ps"], 1)

            def queries(values_first):
                pe.wait_ge(s["xnT_ready"], 1)
                for g in range(NG):
                    if g == 1 and values_first:
                        pe.wait_ge(s["v1_ready"], 1)
                    pe.matmul(PS[:, 4 + g, :], wq1[:, g * P:(g + 1) * P], pnT[:], start=True, stop=True).then_inc(s["q1_ps"], 1)

            def attend(j, plan=PLAN):
                for n, (kind, g, t) in enumerate(MAX_UNITS):
                    if n // plan.max_per_slot - 1 != j:
                        continue
                    bank = plan.max_banks[n % 2]
                    if n == 0:
                        pe.wait_ge(s["kbd_ready"], 1)
                        pe.wait_ge(s["q1_ev"], NG)
                    if n >= 2:
                        pe.wait_ge(s["mx_used"], n - 1)
                    if kind == "turn":
                        pe.wait_ge(s["nm_ready"], g + 1)
                        for t in range(QT):
                            last = pe.transpose(PS[:, bank, t * P:(t + 1) * P], NMp[:, g % 2, t, :], ident[:])
                    else:
                        pe.wait_ge(s["qf_ready"], g + 1)
                        for i in range(2):
                            o = PS[:, bank + i, :].rearrange("p (j m) -> p j m", j=2)[:, :, 0:M]
                            last = pe.matmul(o, qf[:, g, t * P:(t + 1) * P], Kbd[:, g, 2 * i:2 * i + 2, 0:M],
                                             start=True, stop=True)
                    last.then_inc(s["mx_ps"], 1)
                g, part = (j - plan.s_slot) // 3, (j - plan.s_slot) % 3
                if j > plan.s_slot and part == 0 and g <= NG:
                    m = g - 1
                    pe.wait_ge(s["ot_ev"], m + 1)
                    for t in range(QT):
                        last = pe.transpose(PS[:, 4, t * P:(t + 1) * P], ots[:, t * P:(t + 1) * P], ident[:])
                    last.then_inc(s["ott_ps"], 1)
                if j >= plan.s_slot and g < NG and part == 0:
                    if plan is TAIL_PLAN:
                        pe.wait_ge(s["mx_used"], MAX_UNITS.index(("turn", g, 0)) + 1)
                    elif g == 0:
                        pe.wait_ge(s["mx_used"], len(MAX_UNITS))
                    for h in range(2, 4):
                        last = pe.matmul(PS[:, plan.s_bank + h - 2, :], Kbd[:, g, h, 0:P], qf[:, g, :], start=True, stop=True)
                    last.then_inc(s["s_b"], 1)
                    pe.matmul(PS[:, 5, :], Kb2[:, g, :], qf[:, g, :], start=True, stop=True).then_inc(s["s_c"], 1)
                if j >= plan.s_slot and g < NG and part == 1:
                    pe.wait_ge(s["e_b"], g + 1)
                    for h in range(2):
                        last = pe.matmul(PS[:, plan.s_bank + h, :], Kbd[:, g, h, 0:P], qf[:, g, :], start=True, stop=True)
                    last.then_inc(s["s_a"], 1)
                if j >= plan.s_slot and g < NG and part == 2:
                    pe.wait_ge(s["e_a"], g + 1)
                    pe.wait_ge(s["e_c"], g + 1)
                    if g == 0:
                        pe.wait_ge(s["v1_ready"], 1)
                    pe.matmul(PS[:, 5, :], V2d[:, g, :], Ex2[:], start=True, stop=False, skip_group_check=True)
                    for h in range(GH):
                        last = pe.matmul(PS[32 * h:32 * h + 32, 5, :], V1[:, g * P + 32 * h:g * P + 32 * h + 32],
                                         Ex[:, h, :], start=False, stop=True, skip_group_check=True)
                    last.then_inc(s["ot_ps"], 1)

            def batch(prev, more=True):
                norms = 3 if prev else 1

                def between(j):
                    if more:
                        prepare_waits(j, norms)
                    if prev:
                        attend(j)
                    if more:
                        prepare(j, norms, norms, prev)

                def turn_weights():
                    pe.wait_ge(s["cb3_ready"], 1)
                    turned = PS[0:96, 3, :].bitcast(BF16)
                    for t in range(QT):
                        last = pe.transpose(turned[:, t * P:(t + 1) * P], cb3[:, t].rearrange("p a e -> p (a e)"), identb[:])
                    last.then_inc(s["cbT_ps"], 1)
                    pe.wait_ge(s["cbT_ready"], 1)

                sampling(prev)
                turn(norms, 0, 0)
                pe.wait_ge(s["xnT_ready"], norms)
                for t in range(QT):
                    last = pe.matmul(PS[:, 1, t * E0:(t + 1) * E0], xnT[:, t * P:(t + 1) * P], gw0[:], start=True, stop=True)
                last.then_inc(s["lg_ps"], 1)
                if prev:
                    attend(-1)
                    pe.wait_ge(s["k1_ev"], NG)
                pe.wait_ge(s["score_in"], 1)
                pe.wait_ge(s["xlo_ready"], 1)
                if prev:
                    pe.sem_inc(s["prev_used"], 1)
                else:
                    pe.wait_ge(consts_made, 2)
                    pe.wait_ge(experts0_low, 2)
                    pe.wait_ge(experts0_in, 48)
                pe_ffn(pe, C0, wg0h, wg0l, wu0h, wu0l, wd0, turn_weights, between)
                finish_turn(pe, "pe")

            for j in range(C0):
                prepare_waits(j, 0)
                prepare(j, 0, 0, False)
            finish_turn(pe, "pe")
            pe.wait_ge(late_consts_in, 16 * N_LATE)
            batch(False)
            with pe.Fori(1, B - 1) as b:
                batch(True)
            batch(True, False)
            keys()
            turn(1, QT, 4)
            queries(False)
            pe.wait_ge(s["q1_ev"], 2)
            values(4)
            pe.wait_ge(s["v1_ready"], 1)
            for j in range(-1, TAIL_PLAN.s_slot + 3 * NG + 1):
                attend(j, TAIL_PLAN)
            turn(2, 0, 0)
            logits(2)
            pe.wait_ge(s["cost_read"], 1)
            turn(3, 0, 0)
            logits(3)
            finish_turn(pe, "pe")


            def down(n):
                u, i = n // CHUNKS, n % CHUNKS
                pe.wait_ge(s["h_ready"], n + 1)
                if i == 0 and u >= 2:
                    pe.wait_ge(s["y_stored"], u - 1)
                pe.matmul(PS[:, 6 + u % 2, :], wd1[:, UNITS[u][0] % WSLOTS, i, :], hq[:, n % 4, :], start=(i == 0),
                          stop=(i == CHUNKS - 1), skip_group_check=True).then_inc(s["d_ps"], 1)

            def turn_result(r):
                pe.wait_ge(s["y_stored"], RESULTS[r] + 1)
                if r:
                    pe.wait_ge(s["y_added"], r)
                for t in range(QT):
                    last = pe.transpose(PS[:, 0, t * P:(t + 1) * P], yS[:, STORE[RESULTS[r]], t * P:(t + 1) * P], ident[:])
                last.then_inc(s["yt_ps"], 1)

            for n in range(N_CHUNKS):
                u, i = n // CHUNKS, n % CHUNKS
                e, slot = UNITS[u]
                cs, rows = slice(i * P, (i + 1) * P), slice(slot * S, (slot + 1) * S)
                if i == 0:
                    pe.wait_ge(expert_in[e], 48)
                    pe.wait_ge(experts1_split, 4 * e + 4)
                    pe.wait_ge(x_split, 2 * SLOTS.index(slot) + 2)
                if 2 <= n < N_TANH + 2:
                    pe.wait_ge(s["g_read"], n - 1)
                elif n >= 2:
                    pe.wait_ge(s["sg_ready"], n - 1 - N_TANH)
                for m, (w, x) in enumerate(((wg1h, xhall), (wg1h, xlall), (wg1l, xhall))):
                    last = pe.matmul(PS[:, 1 + n % 2, :], w[:, e % WSLOTS, cs], x[:, rows], start=(m == 0), stop=(m == 2))
                last.then_inc(s["g_in"], 1)
                if n >= 3:
                    pe.wait_ge(s["h_ready"], n - 2)
                for m, (w, x) in enumerate(((wu1h, xhall), (wu1h, xlall), (wu1l, xhall))):
                    last = pe.matmul(PS[:, 3 + n % 3, :], w[:, e % WSLOTS, cs], x[:, rows], start=(m == 0), stop=(m == 2))
                last.then_inc(s["up_ps"], 1)
                if i == 0 and 1 <= u <= SINK:
                    pe.wait_ge(sk_part_sum, u)
                    pe.matmul(PS[:, 0, P + E1:P + 2 * E1], onesm[:], scol[:, 5, :], start=True, stop=True)\
                      .then_inc(sk_col_sum, 1)
                if n >= LAG:
                    down(n - LAG)
                if i == 2 and u < SINK:
                    pe.wait_ge(sk_part_max, u + 1)
                    pe.transpose(PS[0:E1, 0, 0:P], scol[:, 0, :], ident[:]).then_inc(sk_turned, 1)
                if i == 3 and u < SINK:
                    pe.wait_ge(sk_col_max, u + 1)
                    pe.matmul(PS[:, 0, P:P + E1], smx[:].to_broadcast([E1, P]), ident[0:E1, 0:E1], start=True, stop=True)\
                      .then_inc(sk_col_spread, 1)
                for r, when in enumerate(RESULTS_AT):
                    if when == n:
                        turn_result(r)
            for n in range(N_CHUNKS - LAG, N_CHUNKS):
                down(n)
            for r, when in enumerate(RESULTS_AT):
                if when == N_CHUNKS:
                    turn_result(r)


N_CONSTS, N_LATE = 12, 15
K_BANK = [3, 3, 2, 2]
Plan = namedtuple("Plan", "max_per_slot max_banks s_slot s_bank")
PLAN = Plan(2, (4, 6), 10, 6)
TAIL_PLAN = Plan(2, (2, 6), 3, 0)
NORM_SLOT, TURN_SLOT, Q_SLOT, QT_SLOT, OFF_SLOT, TABLE_SLOTS, DX_SLOT = 10, 12, 14, 15, 17, (18, 20), 23
DEVIATIONS = (1, 4, 11)
SLOTS = [1, 2, 3, 0]
WSLOTS = 5
CHUNKS = F1D // P
N_UNITS, N_CHUNKS, N_STORED = E1 * B, E1 * B * CHUNKS, WSLOTS * B
N_TANH = CHUNKS * (SINK + 1)
LN_SLOPE, LN_OFFSET = math.log(2.0) / 2**23, -(127 + 0.043) * math.log(2.0)
LAG = 3
RESULTS_FROM = CHUNKS * SINK + 10 + NT // 2
UNITS = [(e, slot) for e in range(WSLOTS) for slot in SLOTS] + [(e, slot) for slot in SLOTS for e in range(WSLOTS, E1)]
RESULTS, RESULTS_AT = [], []
_queue = [u for slot in SLOTS for u, unit in enumerate(UNITS) if unit[1] == slot]
for _n in range(RESULTS_FROM, N_CHUNKS + 1):
    _free = [u for u in _queue if CHUNKS * u + CHUNKS + LAG + 1 <= _n or _n == N_CHUNKS]
    for _u in _free if _n == N_CHUNKS else _free[:1]:
        _queue.remove(_u)
        RESULTS.append(_u)
        RESULTS_AT.append(_n)
STORE = list(range(N_STORED + 4))
STORE += [STORE[RESULTS[u - N_STORED - 4]] for u in range(N_STORED + 4, N_UNITS)]
assert all(RESULTS_AT[u - N_STORED - 4] < CHUNKS * (u + 1) for u in range(N_STORED + 4, N_UNITS))
SLOT_DONE = [max(r for r, u in enumerate(RESULTS) if UNITS[u][1] == slot) for slot in SLOTS]
MAX_UNITS = []
for _g in range(NG):
    MAX_UNITS += [("max", _g, 0), ("max", _g, 1)]
    if _g >= 1:
        MAX_UNITS.append(("turn", _g - 1, 0))
    MAX_UNITS += [("max", _g, 2), ("max", _g, 3)]
MAX_UNITS.append(("turn", NG - 1, 0))
_OUTS = [((B, S, D), "float32")]


def _layout(x, ctx_1024, mask_BxS2_if0, **w):
    import numpy as np
    f = np.float32

    def padded(m, slots, tail=()):
        fill = np.zeros(m.shape[:-1] + (32 - slots * HD,), f)
        fill[..., :len(tail)] = tail
        return np.concatenate([m] * slots + [fill], -1).reshape(m.shape[:-2] + (H * 32,))

    a = {}
    p = np.arange(P)
    a["ident"] = np.eye(P, dtype=f)
    a["ident3"] = np.tile(np.eye(32, dtype=f), (3, 1))
    slot = (p % 32) // HD
    pc = np.zeros((P, 8), f)
    pc[:, 0] = p
    pc[:, 1] = P + p % 32
    pc[:, 2] = p % NK - (NK + 1) // 2
    pc[:, 3] = -(slot == 1).astype(f)
    pc[:, 4] = -(slot == 2).astype(f)
    a["pcol"] = pc
    a["locrow"] = np.tile(np.arange(S, dtype=f), (HK, 1))
    a["erow"] = np.tile(np.arange(32, dtype=f), (P, 1))
    a["lower"] = np.tile(np.tril(np.ones((E1, E1), f), -1).reshape(1, -1), (P, 1))
    a["onerow"] = np.ones((1, P), f)
    v = np.zeros((1, CW), f)
    v[:, 1:1 + M] = 1
    a["vrow"] = v
    a["vtail"] = np.stack([np.tile(v[:, P + n:P + n + 32], (1, GH)) for n in range(2)], 1)
    a["wkv"] = np.concatenate([w["L0_xattn_Wk"].T, w["L0_xattn_Wv"].T], 1)
    a["wq0"] = w["L0_xattn_Wq"].T
    a["woff"] = w["L0_xattn_Woff"].T
    a["wo"] = w["L0_xattn_Wo"].T
    a["bkv"] = np.concatenate([w["L0_xattn_bk"], w["L0_xattn_bv"]])[None]
    a["bq0"] = w["L0_xattn_bq"][None]
    a["bo"] = np.tile(w["L0_xattn_bo"][None], (P, 1))
    bc = np.zeros((P, 2), f)
    bc[:, 0] = w["L0_xattn_bq"]
    bc[:HK, 1] = w["L0_xattn_boff"]
    a["bcol"] = bc
    t = lambda m: m.transpose(1, 0, 2)
    a["wq1"] = padded(t(w["L1_xattn_Wq"]), 3)
    a["wk1"] = padded(t(w["L1_xattn_Wk"]), 3)
    a["wv1"] = padded(t(w["L1_xattn_Wv"]), 1)
    bq = padded(w["L1_xattn_bq"], 3).reshape(NG, P).T
    bk = padded(w["L1_xattn_bk"], 3, (1, 1)).reshape(NG, P).T
    a["bqk1"] = np.stack([bq, bk], 1)
    a["bv1"] = padded(w["L1_xattn_bv"], 1, (1,))[None]
    a["gamma"] = np.tile(w["L1_xattn_gamma"][None], (P, 1))
    a["beta"] = np.tile(w["L1_xattn_beta"][None], (P, 1))
    a["gw0"] = w["L0_ffn_gate_w"].T
    a["eb0"] = np.tile(w["L0_ffn_e_bias"][None], (P, 1))
    a["gw1"] = w["L1_ffn_gate_W"].T
    a["wg0"] = w["L0_ffn_w1"].transpose(1, 0, 2).reshape(D, -1)
    a["wu0"] = w["L0_ffn_w3"].transpose(1, 0, 2).reshape(D, -1)
    a["wd0"] = w["L0_ffn_w2"].reshape(C0, P, D).transpose(1, 0, 2)
    a["wg1"] = w["L1_ffn_W_gate"].reshape(-1, D).T
    a["wu1"] = w["L1_ffn_W_up"].reshape(-1, D).T
    a["wd1"] = w["L1_ffn_W_down"].transpose(0, 2, 1).reshape(C1, P, D).transpose(1, 0, 2)
    cp = np.zeros((B, D, CW), f)
    cp[:, :, 1:1 + M] = ctx_1024.transpose(0, 2, 1)
    a["ctxp"] = cp
    a["mask"] = np.repeat(mask_BxS2_if0[:, None, :], HK, 1)
    a["x"] = x
    return {k: np.ascontiguousarray(m) for k, m in a.items()}


def kernel(**inputs):
    import numpy as _np
    import concourse.bacc as _bacc
    from concourse.bass_utils import run_bass_kernel_spmd as _run

    nc = _bacc.Bacc("TRN2", target_bir_lowering=False, num_devices=1)
    arrays = _layout(**{k: _np.asarray(v) for k, v in inputs.items()})
    aps = {k: nc.dram_tensor("in_" + k, m.shape, mybir.dt.from_np(m.dtype), kind="ExternalInput").ap()
           for k, m in arrays.items()}
    out = nc.dram_tensor("out_0", _OUTS[0][0], F32, kind="ExternalOutput").ap()
    seq_kernel(nc, aps, out)
    r = _run(nc, [{"in_" + k: m for k, m in arrays.items()}], core_ids=[0])
    return r.results[0]["out_0"]
```
